# Optimizing a Trainium2 kernel written in Bass

```python
import numpy as np
import jax
import jax.numpy as jnp

def _softmax(x, axis=-1):
    return jax.nn.softmax(x, axis=axis)

def _gelu(x):
    return jax.nn.gelu(x, approximate=True)

def _silu(x):
    return jax.nn.silu(x)

def _sigmoid(x):
    return jax.nn.sigmoid(x)

def _layernorm(x, axis=-1, eps=1e-05):
    m = jnp.mean(x, axis=axis, keepdims=True)
    v = jnp.var(x, axis=axis, keepdims=True)
    return (x - m) / jnp.sqrt(v + eps)

def _scatter_add(tgt, idx, src, axis=0):
    return tgt.at[idx].add(src)

def _segment_sum(src, seg, n):
    return jax.ops.segment_sum(src, seg, n)
kernel_name = 'mk_recurrent_d4_jaxref_r8_ab2fff'

def setup_inputs(seed: int=0):
    np.random.seed(seed)
    _w = jnp.asarray

    def _L0_attn_setup():
        import jax, jax.numpy as jnp
        import numpy as np
        D_MODEL = 128
        D_STATE = 128
        D_CONV = 4
        EXPAND = 2
        HEADDIM = 64
        NGROUPS = 1
        D_INNER = EXPAND * D_MODEL
        D_SSM = D_INNER
        NHEADS = D_SSM // HEADDIM
        CONV_DIM = D_SSM + 2 * NGROUPS * D_STATE
        D_IN_PROJ = 2 * D_INNER + 2 * NGROUPS * D_STATE + NHEADS
        GROUP_SIZE = D_SSM // NGROUPS
        EPS = 1e-05
        HEAD_TO_GROUP = np.arange(NHEADS) // (NHEADS // NGROUPS)

        def silu(x):
            return x * jax.nn.sigmoid(x)

        def _forward(u, W_in, conv_w, conv_b, W_rxbc, W_rdt, dt_bias, A_log, D_param, norm_w, W_out):
            B, L, _ = u.shape
            zxbcdt = jnp.einsum('bld,ed->ble', u, W_in)
            z, xBC_u, dt_raw = jnp.split(zxbcdt, [D_SSM, D_SSM + CONV_DIM], axis=-1)
            xp = jnp.pad(xBC_u, ((0, 0), (D_CONV - 1, 0), (0, 0)))
            xBC_conv = conv_b + sum((xp[:, k:k + L, :] * conv_w[:, 0, k] for k in range(D_CONV)))
            A = -jnp.exp(A_log.astype(jnp.float32))

            def step(carry, inp):
                state, y_prev = carry
                xBC_t, dt_t, z_t = inp
                xBC = silu(xBC_t + y_prev @ W_rxbc.T)
                dtr = silu(dt_t + y_prev @ W_rdt.T)
                x_t = xBC[:, :D_SSM]
                Bv = xBC[:, D_SSM:D_SSM + NGROUPS * D_STATE]
                Cv = xBC[:, D_SSM + NGROUPS * D_STATE:]
                dt = jax.nn.softplus(dtr + dt_bias).astype(jnp.float32)
                dA = jnp.exp(dt * A)
                x_h = x_t.reshape(B, NHEADS, HEADDIM).astype(jnp.float32)
                B_hn = Bv.reshape(B, NGROUPS, D_STATE).astype(jnp.float32)[:, HEAD_TO_GROUP, :]
                C_hn = Cv.reshape(B, NGROUPS, D_STATE).astype(jnp.float32)[:, HEAD_TO_GROUP, :]
                state = state * dA[:, :, None, None] + dt[:, :, None, None] * x_h[:, :, :, None] * B_hn[:, :, None, :]
                y = (state * C_hn[:, :, None, :]).sum(-1) + D_param[None, :, None] * x_h
                y = y.reshape(B, D_SSM)
                g = y * silu(z_t)
                gg = g.reshape(B, NGROUPS, GROUP_SIZE)
                ms = jnp.mean(gg * gg, axis=-1, keepdims=True)
                yn = (gg * jax.lax.rsqrt(ms + EPS)).reshape(B, D_SSM) * norm_w
                out_t = yn @ W_out.T
                return ((state, yn), out_t)
            state0 = jnp.zeros((B, NHEADS, HEADDIM, D_STATE), jnp.float32)
            y0 = jnp.zeros((B, D_SSM), u.dtype)
            xs = (jnp.swapaxes(xBC_conv, 0, 1), jnp.swapaxes(dt_raw, 0, 1), jnp.swapaxes(z, 0, 1))
            _, out = jax.lax.scan(step, (state0, y0), xs)
            return jnp.swapaxes(out, 0, 1)
        key = jax.random.key(seed)
        ks = jax.random.split(key, 10)
        B, L = (16, 64)
        u = jax.random.normal(ks[0], (B, L, D_MODEL), jnp.float32)
        W_in = jax.random.normal(ks[1], (D_IN_PROJ, D_MODEL), jnp.float32) / np.sqrt(D_MODEL)
        conv_w = jax.random.normal(ks[2], (CONV_DIM, 1, D_CONV), jnp.float32) / np.sqrt(D_CONV)
        conv_b = jax.random.normal(ks[3], (CONV_DIM,), jnp.float32) * 0.01
        W_rxbc = jax.random.normal(ks[4], (CONV_DIM, D_SSM), jnp.float32) * (0.01 / np.sqrt(D_SSM))
        W_rdt = jax.random.normal(ks[5], (NHEADS, D_SSM), jnp.float32) * (0.01 / np.sqrt(D_SSM))
        dt = jnp.exp(jax.random.uniform(ks[6], (NHEADS,)) * (np.log(0.1) - np.log(0.001)) + np.log(0.001))
        dt_bias = dt + jnp.log(-jnp.expm1(-dt))
        A_log = jnp.log(jax.random.uniform(ks[7], (NHEADS,), minval=1.0, maxval=16.0))
        D_param = jnp.ones((NHEADS,), jnp.float32)
        norm_w = jnp.ones((D_SSM,), jnp.float32)
        W_out = jax.random.normal(ks[8], (D_MODEL, D_INNER), jnp.float32) / np.sqrt(D_INNER)
        return dict(u=u, W_in=W_in, conv_w=conv_w, conv_b=conv_b, W_rxbc=W_rxbc, W_rdt=W_rdt, dt_bias=dt_bias, A_log=A_log, D_param=D_param, norm_w=norm_w, W_out=W_out)
    _L0_attn_in = _L0_attn_setup()

    def _L0_ffn_setup():
        import jax, jax.numpy as jnp
        import numpy as np
        E, D, F = (8, 128, 512)
        LN_EPS = 1e-05
        key = jax.random.key(seed)
        k = jax.random.split(key, 8)
        x = jax.random.normal(k[0], (4, 256, D), jnp.float32)
        centroids = jax.random.normal(k[1], (E, D), jnp.float32) * 0.1
        ln_g = jnp.ones((E, D), jnp.float32)
        ln_b = jnp.zeros((E, D), jnp.float32)
        w1 = jax.random.normal(k[2], (E, F, D), jnp.float32) * (1.0 / np.sqrt(D))
        b1 = jnp.zeros((E, F), jnp.float32)
        w2 = jax.random.normal(k[3], (E, D, F), jnp.float32) * (1.0 / np.sqrt(F))
        b2 = jnp.zeros((E, D), jnp.float32)
        return {'input_features': x, 'centroids': centroids, 'ln_g': ln_g, 'ln_b': ln_b, 'w1': w1, 'b1': b1, 'w2': w2, 'b2': b2}
    _L0_ffn_in = _L0_ffn_setup()

    def _L1_attn_setup():
        import jax, jax.numpy as jnp
        import numpy as np
        D_MODEL = 128
        key = jax.random.key(seed)
        k1, k2, k3, k4 = jax.random.split(key, 4)
        B, T, D, E = (8, 256, 128, 128)
        x = jax.random.normal(k1, (B, T, D), dtype=jnp.float32)
        Wq = jax.random.normal(k2, (D, E), dtype=jnp.float32) * (1.0 / np.sqrt(D))
        Wk = jax.random.normal(k3, (D, E), dtype=jnp.float32) * (1.0 / np.sqrt(D))
        Wv = jax.random.normal(k4, (D, E), dtype=jnp.float32) * (1.0 / np.sqrt(D))
        return {'x': x, 'Wq': Wq, 'Wk': Wk, 'Wv': Wv}
    _L1_attn_in = _L1_attn_setup()

    def _L1_ffn_setup():
        import jax, jax.numpy as jnp
        import numpy as np
        B, S, DIM = (4, 512, 128)
        BASE_COUPLING = 0.1
        NUM_CYCLES = 3

        def _gelu(x):
            return jax.nn.gelu(x, approximate=False)

        def _coupling_net(h, w1, b1, w2, b2, w3, b3, w4, b4):
            h = _gelu(h @ w1 + b1)
            h = _gelu(h @ w2 + b2)
            h = _gelu(h @ w3 + b3)
            return jax.nn.sigmoid(h @ w4 + b4)

        def _global_net(h, w1, b1, w2, b2, w3, b3):
            h = _gelu(h @ w1 + b1)
            h = _gelu(h @ w2 + b2)
            return jax.nn.sigmoid(h @ w3 + b3)

        def _twist(x):
            o_r, o_i, p_r, p_i = jnp.split(x, 4, axis=-1)
            return jnp.concatenate([p_r, -p_i, -o_r, o_i], axis=-1)
        key = jax.random.key(seed)
        ks = jax.random.split(key, 9)
        d = DIM

        def w(k, fan_in, fan_out):
            return jax.random.normal(k, (fan_in, fan_out), dtype=jnp.float32) / np.sqrt(fan_in).astype(np.float32)
        inp = {'x': jax.random.normal(ks[0], (B, S, d), dtype=jnp.float32)}
        cn_dims = [(d, d), (d, d // 2), (d // 2, d // 4), (d // 4, 1)]
        for i, (a, b) in enumerate(cn_dims):
            inp[f'cn_w{i + 1}'] = w(ks[1 + i], a, b)
            inp[f'cn_b{i + 1}'] = jnp.zeros((b,), dtype=jnp.float32)
        gc_dims = [(d, d // 2), (d // 2, d // 4), (d // 4, 1)]
        for i, (a, b) in enumerate(gc_dims):
            inp[f'gc_w{i + 1}'] = w(ks[5 + i], a, b)
            inp[f'gc_b{i + 1}'] = jnp.zeros((b,), dtype=jnp.float32)
        inp['adaptive_range'] = jnp.full((1,), 0.2, dtype=jnp.float32)
        return inp
    _L1_ffn_in = _L1_ffn_setup()

    def _L2_attn_setup():
        import jax, jax.numpy as jnp
        import numpy as np
        import math
        N_EMBD = 128
        NUM_HEADS = 16
        HEAD_DIM = N_EMBD // NUM_HEADS

        def alibi_slopes(num_heads):
            x = (2 ** 8) ** (1.0 / num_heads)
            return jnp.array([1.0 / x ** (i + 1) for i in range(num_heads)], dtype=jnp.float32)
        key = jax.random.key(seed)
        k1, k2 = jax.random.split(key)
        x = jax.random.normal(k1, (2, 256, N_EMBD), dtype=jnp.float32)
        W_kqv = jax.random.normal(k2, (3 * N_EMBD, N_EMBD), dtype=jnp.float32) * (1.0 / math.sqrt(N_EMBD))
        return {'x': x, 'W_kqv': W_kqv}
    _L2_attn_in = _L2_attn_setup()

    def _L2_ffn_setup():
        import jax, jax.numpy as jnp
        import numpy as np
        B, L, D = (4, 128, 128)
        E, H, K = (16, 64, 8)
        EPS = 1e-12

        def _l2norm(v, axis=-1):
            n = jnp.sqrt(jnp.sum(v * v, axis=axis, keepdims=True))
            return v / jnp.maximum(n, EPS)
        if __name__ == '__main__':
            out = reference(**setup_inputs())
            print(out.shape)
        key = jax.random.key(seed)
        ks = jax.random.split(key, 8)
        s = lambda fan_in: 1.0 / np.sqrt(fan_in)
        return {'x': jax.random.normal(ks[0], (B, L, D), jnp.float32), 'gate_w': jax.random.normal(ks[1], (E, D), jnp.float32) * s(D), 'w_gate': jax.random.normal(ks[2], (E, D, H), jnp.float32) * s(D), 'w_up': jax.random.normal(ks[3], (E, D, H), jnp.float32) * s(D), 'w_down': jax.random.normal(ks[4], (E, H, D), jnp.float32) * s(H), 'sw_gate': jax.random.normal(ks[5], (D, H), jnp.float32) * s(D), 'sw_up': jax.random.normal(ks[6], (D, H), jnp.float32) * s(D), 'sw_down': jax.random.normal(ks[7], (H, D), jnp.float32) * s(H)}
    _L2_ffn_in = _L2_ffn_setup()

    def _L3_attn_setup():
        import jax, jax.numpy as jnp
        import numpy as np
        E = 128
        H = 16
        D = E // H
        NUM_BUCKETS = 40
        MAX_DISTANCE = 100

        def _relative_positions_bucket(relative_positions):
            num_buckets = NUM_BUCKETS // 2
            relative_buckets = (relative_positions > 0).astype(jnp.int32) * num_buckets
            rel = jnp.abs(relative_positions)
            max_exact = num_buckets // 2
            is_small = rel < max_exact
            rel_f = jnp.maximum(rel, 1).astype(jnp.float32)
            large = jnp.log(rel_f / max_exact) / np.log(MAX_DISTANCE / max_exact) * (num_buckets - max_exact)
            large = (max_exact + large).astype(jnp.int32)
            large = jnp.minimum(large, num_buckets - 1)
            relative_buckets = relative_buckets + jnp.where(is_small, rel, large)
            return relative_buckets
        key = jax.random.key(seed)
        ks = jax.random.split(key, 12)
        B, T = (2, 256)
        s = 0.02
        return {'hidden_states': jax.random.normal(ks[0], (B, T, E), dtype=jnp.float32), 'q_w': jax.random.normal(ks[1], (E, E), dtype=jnp.float32) * s, 'q_b': jnp.zeros((E,), dtype=jnp.float32), 'k_w': jax.random.normal(ks[2], (E, E), dtype=jnp.float32) * s, 'k_b': jnp.zeros((E,), dtype=jnp.float32), 'v_w': jax.random.normal(ks[3], (E, E), dtype=jnp.float32) * s, 'v_b': jnp.zeros((E,), dtype=jnp.float32), 'out_w': jax.random.normal(ks[4], (E, E), dtype=jnp.float32) * s, 'out_b': jnp.zeros((E,), dtype=jnp.float32), 'rel_embed': jax.random.normal(ks[5], (NUM_BUCKETS, H), dtype=jnp.float32) * s, 'gru_const': jnp.ones((1, H, 1, 1), dtype=jnp.float32), 'gru_w': jax.random.normal(ks[6], (8, D), dtype=jnp.float32) * s, 'gru_b': jnp.zeros((8,), dtype=jnp.float32)}
    _L3_attn_in = _L3_attn_setup()

    def _L3_ffn_setup():
        import jax, jax.numpy as jnp
        import numpy as np
        D_MODEL = 128
        EXPANSION = 4
        D_HIDDEN = D_MODEL * EXPANSION
        NUM_STAGES = int(np.log2(D_HIDDEN))

        def butterfly(y, weights, dim):
            lead = y.shape[:-1]
            for stage in range(weights.shape[0]):
                s = 2 ** stage
                nb = dim // (2 * s)
                yr = y.reshape(*lead, nb, 2, s)
                a = yr[..., 0, :]
                b = yr[..., 1, :]
                w = weights[stage].reshape(nb, s, 2, 2)
                na = w[..., 0, 0] * a + w[..., 0, 1] * b
                nb2 = w[..., 1, 0] * a + w[..., 1, 1] * b
                y = jnp.stack([na, nb2], axis=-2).reshape(*lead, dim)
            return y
        key = jax.random.key(seed)
        ks = jax.random.split(key, 6)
        B, S = (4, 256)
        x = jax.random.normal(ks[0], (B, S, D_MODEL), jnp.float32)
        W_exp = jax.random.normal(ks[1], (D_MODEL, D_HIDDEN), jnp.float32) * 0.02
        b_exp = jnp.zeros((D_HIDDEN,), jnp.float32)
        up_weights = jax.random.normal(ks[2], (NUM_STAGES, D_HIDDEN // 2, 2, 2), jnp.float32) * 0.02
        up_bias = jnp.zeros((D_HIDDEN,), jnp.float32)
        down_weights = jax.random.normal(ks[3], (NUM_STAGES, D_HIDDEN // 2, 2, 2), jnp.float32) * 0.02
        W_con = jax.random.normal(ks[4], (D_HIDDEN, D_MODEL), jnp.float32) * 0.02
        b_con = jnp.zeros((D_MODEL,), jnp.float32)
        down_bias = jnp.zeros((D_MODEL,), jnp.float32)
        return dict(x=x, W_exp=W_exp, b_exp=b_exp, up_weights=up_weights, up_bias=up_bias, down_weights=down_weights, W_con=W_con, b_con=b_con, down_bias=down_bias)
    _L3_ffn_in = _L3_ffn_setup()
    _d = {'L0_attn_u': _L0_attn_in['u'], 'L0_attn_W_in': _L0_attn_in['W_in'], 'L0_attn_conv_w': _L0_attn_in['conv_w'], 'L0_attn_conv_b': _L0_attn_in['conv_b'], 'L0_attn_W_rxbc': _L0_attn_in['W_rxbc'], 'L0_attn_W_rdt': _L0_attn_in['W_rdt'], 'L0_attn_dt_bias': _L0_attn_in['dt_bias'], 'L0_attn_A_log': _L0_attn_in['A_log'], 'L0_attn_D_param': _L0_attn_in['D_param'], 'L0_attn_norm_w': _L0_attn_in['norm_w'], 'L0_attn_W_out': _L0_attn_in['W_out'], 'L0_ffn_centroids': _L0_ffn_in['centroids'], 'L0_ffn_ln_g': _L0_ffn_in['ln_g'], 'L0_ffn_ln_b': _L0_ffn_in['ln_b'], 'L0_ffn_w1': _L0_ffn_in['w1'], 'L0_ffn_b1': _L0_ffn_in['b1'], 'L0_ffn_w2': _L0_ffn_in['w2'], 'L0_ffn_b2': _L0_ffn_in['b2'], 'L1_attn_Wq': _L1_attn_in['Wq'], 'L1_attn_Wk': _L1_attn_in['Wk'], 'L1_attn_Wv': _L1_attn_in['Wv'], 'L1_ffn_cn_w1': _L1_ffn_in['cn_w1'], 'L1_ffn_cn_b1': _L1_ffn_in['cn_b1'], 'L1_ffn_cn_w2': _L1_ffn_in['cn_w2'], 'L1_ffn_cn_b2': _L1_ffn_in['cn_b2'], 'L1_ffn_cn_w3': _L1_ffn_in['cn_w3'], 'L1_ffn_cn_b3': _L1_ffn_in['cn_b3'], 'L1_ffn_cn_w4': _L1_ffn_in['cn_w4'], 'L1_ffn_cn_b4': _L1_ffn_in['cn_b4'], 'L1_ffn_gc_w1': _L1_ffn_in['gc_w1'], 'L1_ffn_gc_b1': _L1_ffn_in['gc_b1'], 'L1_ffn_gc_w2': _L1_ffn_in['gc_w2'], 'L1_ffn_gc_b2': _L1_ffn_in['gc_b2'], 'L1_ffn_gc_w3': _L1_ffn_in['gc_w3'], 'L1_ffn_gc_b3': _L1_ffn_in['gc_b3'], 'L1_ffn_adaptive_range': _L1_ffn_in['adaptive_range'], 'L2_attn_W_kqv': _L2_attn_in['W_kqv'], 'L2_ffn_gate_w': _L2_ffn_in['gate_w'], 'L2_ffn_w_gate': _L2_ffn_in['w_gate'], 'L2_ffn_w_up': _L2_ffn_in['w_up'], 'L2_ffn_w_down': _L2_ffn_in['w_down'], 'L2_ffn_sw_gate': _L2_ffn_in['sw_gate'], 'L2_ffn_sw_up': _L2_ffn_in['sw_up'], 'L2_ffn_sw_down': _L2_ffn_in['sw_down'], 'L3_attn_q_w': _L3_attn_in['q_w'], 'L3_attn_q_b': _L3_attn_in['q_b'], 'L3_attn_k_w': _L3_attn_in['k_w'], 'L3_attn_k_b': _L3_attn_in['k_b'], 'L3_attn_v_w': _L3_attn_in['v_w'], 'L3_attn_v_b': _L3_attn_in['v_b'], 'L3_attn_out_w': _L3_attn_in['out_w'], 'L3_attn_out_b': _L3_attn_in['out_b'], 'L3_attn_rel_embed': _L3_attn_in['rel_embed'], 'L3_attn_gru_const': _L3_attn_in['gru_const'], 'L3_attn_gru_w': _L3_attn_in['gru_w'], 'L3_attn_gru_b': _L3_attn_in['gru_b'], 'L3_ffn_W_exp': _L3_ffn_in['W_exp'], 'L3_ffn_b_exp': _L3_ffn_in['b_exp'], 'L3_ffn_up_weights': _L3_ffn_in['up_weights'], 'L3_ffn_up_bias': _L3_ffn_in['up_bias'], 'L3_ffn_down_weights': _L3_ffn_in['down_weights'], 'L3_ffn_W_con': _L3_ffn_in['W_con'], 'L3_ffn_b_con': _L3_ffn_in['b_con'], 'L3_ffn_down_bias': _L3_ffn_in['down_bias']}
    _x0 = _d['L0_attn_u']
    _d['L0_attn_u'] = jax.random.normal(jax.random.fold_in(jax.random.key(seed), 1), (8, 512, 128), dtype=_x0.dtype)
    del _x0
    return _d

def reference(L0_attn_u, L0_attn_W_in, L0_attn_conv_w, L0_attn_conv_b, L0_attn_W_rxbc, L0_attn_W_rdt, L0_attn_dt_bias, L0_attn_A_log, L0_attn_D_param, L0_attn_norm_w, L0_attn_W_out, L0_ffn_centroids, L0_ffn_ln_g, L0_ffn_ln_b, L0_ffn_w1, L0_ffn_b1, L0_ffn_w2, L0_ffn_b2, L1_attn_Wq, L1_attn_Wk, L1_attn_Wv, L1_ffn_cn_w1, L1_ffn_cn_b1, L1_ffn_cn_w2, L1_ffn_cn_b2, L1_ffn_cn_w3, L1_ffn_cn_b3, L1_ffn_cn_w4, L1_ffn_cn_b4, L1_ffn_gc_w1, L1_ffn_gc_b1, L1_ffn_gc_w2, L1_ffn_gc_b2, L1_ffn_gc_w3, L1_ffn_gc_b3, L1_ffn_adaptive_range, L2_attn_W_kqv, L2_ffn_gate_w, L2_ffn_w_gate, L2_ffn_w_up, L2_ffn_w_down, L2_ffn_sw_gate, L2_ffn_sw_up, L2_ffn_sw_down, L3_attn_q_w, L3_attn_q_b, L3_attn_k_w, L3_attn_k_b, L3_attn_v_w, L3_attn_v_b, L3_attn_out_w, L3_attn_out_b, L3_attn_rel_embed, L3_attn_gru_const, L3_attn_gru_w, L3_attn_gru_b, L3_ffn_W_exp, L3_ffn_b_exp, L3_ffn_up_weights, L3_ffn_up_bias, L3_ffn_down_weights, L3_ffn_W_con, L3_ffn_b_con, L3_ffn_down_bias):

    def _L0_attn_ref(u, W_in, conv_w, conv_b, W_rxbc, W_rdt, dt_bias, A_log, D_param, norm_w, W_out):
        import jax, jax.numpy as jnp
        import numpy as np
        D_MODEL = 128
        D_STATE = 128
        D_CONV = 4
        EXPAND = 2
        HEADDIM = 64
        NGROUPS = 1
        D_INNER = EXPAND * D_MODEL
        D_SSM = D_INNER
        NHEADS = D_SSM // HEADDIM
        CONV_DIM = D_SSM + 2 * NGROUPS * D_STATE
        D_IN_PROJ = 2 * D_INNER + 2 * NGROUPS * D_STATE + NHEADS
        GROUP_SIZE = D_SSM // NGROUPS
        EPS = 1e-05
        HEAD_TO_GROUP = np.arange(NHEADS) // (NHEADS // NGROUPS)

        def silu(x):
            return x * jax.nn.sigmoid(x)

        def _forward(u, W_in, conv_w, conv_b, W_rxbc, W_rdt, dt_bias, A_log, D_param, norm_w, W_out):
            B, L, _ = u.shape
            zxbcdt = jnp.einsum('bld,ed->ble', u, W_in)
            z, xBC_u, dt_raw = jnp.split(zxbcdt, [D_SSM, D_SSM + CONV_DIM], axis=-1)
            xp = jnp.pad(xBC_u, ((0, 0), (D_CONV - 1, 0), (0, 0)))
            xBC_conv = conv_b + sum((xp[:, k:k + L, :] * conv_w[:, 0, k] for k in range(D_CONV)))
            A = -jnp.exp(A_log.astype(jnp.float32))

            def step(carry, inp):
                state, y_prev = carry
                xBC_t, dt_t, z_t = inp
                xBC = silu(xBC_t + y_prev @ W_rxbc.T)
                dtr = silu(dt_t + y_prev @ W_rdt.T)
                x_t = xBC[:, :D_SSM]
                Bv = xBC[:, D_SSM:D_SSM + NGROUPS * D_STATE]
                Cv = xBC[:, D_SSM + NGROUPS * D_STATE:]
                dt = jax.nn.softplus(dtr + dt_bias).astype(jnp.float32)
                dA = jnp.exp(dt * A)
                x_h = x_t.reshape(B, NHEADS, HEADDIM).astype(jnp.float32)
                B_hn = Bv.reshape(B, NGROUPS, D_STATE).astype(jnp.float32)[:, HEAD_TO_GROUP, :]
                C_hn = Cv.reshape(B, NGROUPS, D_STATE).astype(jnp.float32)[:, HEAD_TO_GROUP, :]
                state = state * dA[:, :, None, None] + dt[:, :, None, None] * x_h[:, :, :, None] * B_hn[:, :, None, :]
                y = (state * C_hn[:, :, None, :]).sum(-1) + D_param[None, :, None] * x_h
                y = y.reshape(B, D_SSM)
                g = y * silu(z_t)
                gg = g.reshape(B, NGROUPS, GROUP_SIZE)
                ms = jnp.mean(gg * gg, axis=-1, keepdims=True)
                yn = (gg * jax.lax.rsqrt(ms + EPS)).reshape(B, D_SSM) * norm_w
                out_t = yn @ W_out.T
                return ((state, yn), out_t)
            state0 = jnp.zeros((B, NHEADS, HEADDIM, D_STATE), jnp.float32)
            y0 = jnp.zeros((B, D_SSM), u.dtype)
            xs = (jnp.swapaxes(xBC_conv, 0, 1), jnp.swapaxes(dt_raw, 0, 1), jnp.swapaxes(z, 0, 1))
            _, out = jax.lax.scan(step, (state0, y0), xs)
            return jnp.swapaxes(out, 0, 1)
        return _forward(u, W_in, conv_w, conv_b, W_rxbc, W_rdt, dt_bias, A_log, D_param, norm_w, W_out)

    def _L0_ffn_ref(input_features, centroids, ln_g, ln_b, w1, b1, w2, b2):
        import jax, jax.numpy as jnp
        import numpy as np
        E, D, F = (8, 128, 512)
        LN_EPS = 1e-05
        x = input_features.reshape(-1, D)
        aff = jax.lax.stop_gradient(x) @ centroids.T
        assign = jnp.argmax(aff, axis=1)
        onehot = jax.nn.one_hot(assign, E, dtype=x.dtype)
        mu = jnp.mean(x, axis=-1, keepdims=True)
        var = jnp.mean((x - mu) ** 2, axis=-1, keepdims=True)
        xhat = (x - mu) * jax.lax.rsqrt(var + LN_EPS)
        xn = xhat[None, :, :] * ln_g[:, None, :] + ln_b[:, None, :]
        h = jax.nn.relu(jnp.einsum('etd,efd->etf', xn, w1) + b1[:, None, :])
        y = x[None, :, :] + jnp.einsum('etf,edf->etd', h, w2) + b2[:, None, :]
        alpha = jax.nn.sigmoid(x @ centroids.T)
        a = alpha.T[:, :, None]
        gated = a * y + (1.0 - a) * x[None, :, :]
        out = jnp.einsum('te,etd->td', onehot, gated)
        return out.reshape(input_features.shape)

    def _L1_attn_ref(x, Wq, Wk, Wv):
        import jax, jax.numpy as jnp
        import numpy as np
        D_MODEL = 128
        T = x.shape[1]
        Q = x @ Wq
        K = x @ Wk
        V = x @ Wv
        scale = 1.0 / jnp.sqrt(jnp.asarray(D_MODEL, dtype=x.dtype))
        w = jnp.einsum('bte,bse->bts', Q, K) * scale
        causal = jnp.tril(jnp.ones((T, T), dtype=bool))
        w = jnp.where(causal, w, -jnp.inf)
        w = jax.nn.softmax(w, axis=-1)
        return w @ V

    def _L1_ffn_ref(x, cn_w1, cn_b1, cn_w2, cn_b2, cn_w3, cn_b3, cn_w4, cn_b4, gc_w1, gc_b1, gc_w2, gc_b2, gc_w3, gc_b3, adaptive_range):
        import jax, jax.numpy as jnp
        import numpy as np
        B, S, DIM = (4, 512, 128)
        BASE_COUPLING = 0.1
        NUM_CYCLES = 3

        def _gelu(x):
            return jax.nn.gelu(x, approximate=False)

        def _coupling_net(h, w1, b1, w2, b2, w3, b3, w4, b4):
            h = _gelu(h @ w1 + b1)
            h = _gelu(h @ w2 + b2)
            h = _gelu(h @ w3 + b3)
            return jax.nn.sigmoid(h @ w4 + b4)

        def _global_net(h, w1, b1, w2, b2, w3, b3):
            h = _gelu(h @ w1 + b1)
            h = _gelu(h @ w2 + b2)
            return jax.nn.sigmoid(h @ w3 + b3)

        def _twist(x):
            o_r, o_i, p_r, p_i = jnp.split(x, 4, axis=-1)
            return jnp.concatenate([p_r, -p_i, -o_r, o_i], axis=-1)
        global_context = x.mean(axis=1, keepdims=True)
        gf = _global_net(global_context, gc_w1, gc_b1, gc_w2, gc_b2, gc_w3, gc_b3)
        out = x
        for _ in range(NUM_CYCLES):
            tf = _coupling_net(out, cn_w1, cn_b1, cn_w2, cn_b2, cn_w3, cn_b3, cn_w4, cn_b4)
            combined = 0.7 * gf + 0.3 * tf
            coupling = BASE_COUPLING + adaptive_range * (combined - 0.5) * 2.0
            out = out + coupling * _twist(out)
        return out

    def _L2_attn_ref(x, W_kqv):
        import jax, jax.numpy as jnp
        import numpy as np
        import math
        N_EMBD = 128
        NUM_HEADS = 16
        HEAD_DIM = N_EMBD // NUM_HEADS

        def alibi_slopes(num_heads):
            x = (2 ** 8) ** (1.0 / num_heads)
            return jnp.array([1.0 / x ** (i + 1) for i in range(num_heads)], dtype=jnp.float32)
        B, S, E = x.shape
        H, D = (NUM_HEADS, HEAD_DIM)
        kqv = jnp.einsum('bse,fe->bsf', x, W_kqv)
        k, q, v = jnp.split(kqv, 3, axis=-1)
        q = q.reshape(B, S, H, D).transpose(0, 2, 1, 3)
        k = k.reshape(B, S, H, D).transpose(0, 2, 1, 3)
        v = v.reshape(B, S, H, D).transpose(0, 2, 1, 3)
        rel = jnp.arange(S)[None, :] - jnp.arange(S)[:, None]
        bias = alibi_slopes(H)[:, None, None] * rel.astype(jnp.float32)
        scale = math.sqrt(E)
        score = jnp.einsum('bhqd,bhkd->bhqk', q, k) / scale + bias[None]
        causal = jnp.tril(jnp.ones((S, S), dtype=bool))
        score = jnp.where(causal[None, None], score, -jnp.inf)
        attn = jax.nn.softmax(score, axis=-1)
        out = jnp.einsum('bhqk,bhkd->bhqd', attn, v)
        return out.transpose(0, 2, 1, 3).reshape(B, S, E)

    def _L2_ffn_ref(x, gate_w, w_gate, w_up, w_down, sw_gate, sw_up, sw_down):
        import jax, jax.numpy as jnp
        import numpy as np
        B, L, D = (4, 128, 128)
        E, H, K = (16, 64, 8)
        EPS = 1e-12

        def _l2norm(v, axis=-1):
            n = jnp.sqrt(jnp.sum(v * v, axis=axis, keepdims=True))
            return v / jnp.maximum(n, EPS)
        if __name__ == '__main__':
            out = reference(**setup_inputs())
            print(out.shape)
        b, l, d = x.shape
        xf = x.reshape(-1, d)
        logits = _l2norm(xf) @ _l2norm(gate_w).T
        scores = jax.nn.sigmoid(logits)
        topk_scores, topk_idx = jax.lax.top_k(scores, K)
        topk_w = topk_scores / jnp.sum(topk_scores, axis=-1, keepdims=True)
        combine = jnp.sum(jax.nn.one_hot(topk_idx, E, dtype=xf.dtype) * topk_w[..., None], axis=1)
        g = jnp.einsum('nd,edh->neh', xf, w_gate)
        u = jnp.einsum('nd,edh->neh', xf, w_up)
        y = jnp.einsum('neh,ehd->ned', jax.nn.silu(g) * u, w_down)
        routed = jnp.einsum('ned,ne->nd', y, combine)
        shared = jax.nn.silu(xf @ sw_gate) * (xf @ sw_up) @ sw_down
        return (routed + shared).reshape(b, l, d)

    def _L3_attn_ref(hidden_states, q_w, q_b, k_w, k_b, v_w, v_b, out_w, out_b, rel_embed, gru_const, gru_w, gru_b):
        import jax, jax.numpy as jnp
        import numpy as np
        E = 128
        H = 16
        D = E // H
        NUM_BUCKETS = 40
        MAX_DISTANCE = 100

        def _relative_positions_bucket(relative_positions):
            num_buckets = NUM_BUCKETS // 2
            relative_buckets = (relative_positions > 0).astype(jnp.int32) * num_buckets
            rel = jnp.abs(relative_positions)
            max_exact = num_buckets // 2
            is_small = rel < max_exact
            rel_f = jnp.maximum(rel, 1).astype(jnp.float32)
            large = jnp.log(rel_f / max_exact) / np.log(MAX_DISTANCE / max_exact) * (num_buckets - max_exact)
            large = (max_exact + large).astype(jnp.int32)
            large = jnp.minimum(large, num_buckets - 1)
            relative_buckets = relative_buckets + jnp.where(is_small, rel, large)
            return relative_buckets
        B, T, _ = hidden_states.shape
        scaling = D ** (-0.5)
        ctx = jnp.arange(T, dtype=jnp.int32)[:, None]
        mem = jnp.arange(T, dtype=jnp.int32)[None, :]
        buckets = _relative_positions_bucket(mem - ctx)
        position_bias = rel_embed[buckets]
        position_bias = jnp.transpose(position_bias, (2, 0, 1))
        gated = hidden_states.reshape(B, T, H, D).transpose(0, 2, 1, 3)
        proj = jnp.einsum('bhtd,ed->bhte', gated, gru_w) + gru_b
        proj = proj.reshape(B, H, T, 2, 4).sum(-1)
        gate = jax.nn.sigmoid(proj)
        gate_a = gate[..., 0:1]
        gate_b = gate[..., 1:2]
        gate_out = gate_a * (gate_b * gru_const - 1.0) + 2.0
        gated_position_bias = gate_out * position_bias[None]
        q = (hidden_states @ q_w.T + q_b).reshape(B, T, H, D).transpose(0, 2, 1, 3) * scaling
        k = (hidden_states @ k_w.T + k_b).reshape(B, T, H, D).transpose(0, 2, 1, 3)
        v = (hidden_states @ v_w.T + v_b).reshape(B, T, H, D).transpose(0, 2, 1, 3)
        scores = jnp.einsum('bhtd,bhsd->bhts', q, k) + gated_position_bias
        attn = jax.nn.softmax(scores, axis=-1)
        ctx_out = jnp.einsum('bhts,bhsd->bhtd', attn, v)
        ctx_out = ctx_out.transpose(0, 2, 1, 3).reshape(B, T, E)
        return ctx_out @ out_w.T + out_b

    def _L3_ffn_ref(x, W_exp, b_exp, up_weights, up_bias, down_weights, W_con, b_con, down_bias):
        import jax, jax.numpy as jnp
        import numpy as np
        D_MODEL = 128
        EXPANSION = 4
        D_HIDDEN = D_MODEL * EXPANSION
        NUM_STAGES = int(np.log2(D_HIDDEN))

        def butterfly(y, weights, dim):
            lead = y.shape[:-1]
            for stage in range(weights.shape[0]):
                s = 2 ** stage
                nb = dim // (2 * s)
                yr = y.reshape(*lead, nb, 2, s)
                a = yr[..., 0, :]
                b = yr[..., 1, :]
                w = weights[stage].reshape(nb, s, 2, 2)
                na = w[..., 0, 0] * a + w[..., 0, 1] * b
                nb2 = w[..., 1, 0] * a + w[..., 1, 1] * b
                y = jnp.stack([na, nb2], axis=-2).reshape(*lead, dim)
            return y
        h = jnp.einsum('bsd,dh->bsh', x, W_exp) + b_exp
        h = butterfly(h, up_weights, D_HIDDEN)
        h = jax.nn.gelu(h + up_bias, approximate=False)
        h = butterfly(h, down_weights, D_HIDDEN)
        y = jnp.einsum('bsh,hd->bsd', h, W_con) + b_con
        return y + down_bias
    x = L0_attn_u
    xn = _layernorm(x, axis=-1)
    s = _L0_attn_ref(xn, L0_attn_W_in, L0_attn_conv_w, L0_attn_conv_b, L0_attn_W_rxbc, L0_attn_W_rdt, L0_attn_dt_bias, L0_attn_A_log, L0_attn_D_param, L0_attn_norm_w, L0_attn_W_out)
    g = _silu(_L0_ffn_ref(xn, L0_ffn_centroids, L0_ffn_ln_g, L0_ffn_ln_b, L0_ffn_w1, L0_ffn_b1, L0_ffn_w2, L0_ffn_b2))
    x = x + s * g
    xn = _layernorm(x, axis=-1)
    s = _L1_attn_ref(xn, L1_attn_Wq, L1_attn_Wk, L1_attn_Wv)
    g = _silu(_L1_ffn_ref(xn, L1_ffn_cn_w1, L1_ffn_cn_b1, L1_ffn_cn_w2, L1_ffn_cn_b2, L1_ffn_cn_w3, L1_ffn_cn_b3, L1_ffn_cn_w4, L1_ffn_cn_b4, L1_ffn_gc_w1, L1_ffn_gc_b1, L1_ffn_gc_w2, L1_ffn_gc_b2, L1_ffn_gc_w3, L1_ffn_gc_b3, L1_ffn_adaptive_range))
    x = x + s * g
    xn = _layernorm(x, axis=-1)
    s = _L2_attn_ref(xn, L2_attn_W_kqv)
    g = _silu(_L2_ffn_ref(xn, L2_ffn_gate_w, L2_ffn_w_gate, L2_ffn_w_up, L2_ffn_w_down, L2_ffn_sw_gate, L2_ffn_sw_up, L2_ffn_sw_down))
    x = x + s * g
    xn = _layernorm(x, axis=-1)
    s = _L3_attn_ref(xn, L3_attn_q_w, L3_attn_q_b, L3_attn_k_w, L3_attn_k_b, L3_attn_v_w, L3_attn_v_b, L3_attn_out_w, L3_attn_out_b, L3_attn_rel_embed, L3_attn_gru_const, L3_attn_gru_w, L3_attn_gru_b)
    g = _silu(_L3_ffn_ref(xn, L3_ffn_W_exp, L3_ffn_b_exp, L3_ffn_up_weights, L3_ffn_up_bias, L3_ffn_down_weights, L3_ffn_W_con, L3_ffn_b_con, L3_ffn_down_bias))
    x = x + s * g
    return x

_drawn_inputs = setup_inputs


def setup_inputs(seed=0):
    import zlib

    import numpy as np

    out = dict(_drawn_inputs(seed))
    spreads = {'L0_attn_D_param': (1.0, 0.2),
     'L0_attn_norm_w': (1.0, 0.2),
     'L0_ffn_ln_g': (1.0, 0.2),
     'L0_ffn_ln_b': (0.0, 0.1),
     'L0_ffn_b1': (0.0, 0.1),
     'L0_ffn_b2': (0.0, 0.1),
     'L1_ffn_cn_b1': (0.0, 2.0),
     'L1_ffn_cn_b2': (0.0, 2.0),
     'L1_ffn_cn_b3': (0.0, 2.0),
     'L1_ffn_gc_b1': (0.0, 2.0),
     'L1_ffn_gc_b2': (0.0, 0.8),
     'L3_attn_q_b': (0.0, 0.8),
     'L3_attn_k_b': (0.0, 2.0),
     'L3_attn_v_b': (0.0, 0.8),
     'L3_attn_out_b': (0.0, 0.8),
     'L3_attn_gru_const': (1.0, 0.6),
     'L3_attn_gru_b': (0.0, 2.0),
     'L3_ffn_b_exp': (0.0, 0.1),
     'L3_ffn_up_bias': (0.0, 0.1),
     'L3_ffn_b_con': (0.0, 0.8),
     'L3_ffn_down_bias': (0.0, 0.8)}
    factors = {'L0_attn_conv_b': 6.759,
     'L0_attn_W_rxbc': 8.0,
     'L0_attn_W_rdt': 21.946,
     'L1_ffn_cn_w1': 8.0,
     'L1_ffn_cn_w2': 8.0,
     'L1_ffn_cn_w3': 8.0,
     'L1_ffn_cn_w4': 8.0,
     'L1_ffn_gc_w1': 8.0,
     'L1_ffn_gc_w2': 8.0,
     'L1_ffn_gc_w3': 32.804,
     'L2_ffn_gate_w': 2.847,
     'L3_attn_q_w': 8.0,
     'L3_attn_k_w': 8.0,
     'L3_attn_v_w': 8.0,
     'L3_attn_out_w': 8.0,
     'L3_attn_rel_embed': 8.0,
     'L3_attn_gru_w': 64.0}
    for name, (base, spread) in spreads.items():
        noise = np.random.default_rng([zlib.crc32(name.encode()), seed]).standard_normal(out[name].shape)
        drawn = base * np.exp(spread * noise) if base else spread * noise
        out[name] = jnp.asarray(drawn.astype(out[name].dtype))
    for name, factor in factors.items():
        out[name] = (out[name] * factor).astype(out[name].dtype)
    return out
```

```python
from contextlib import ExitStack, contextmanager

import numpy as np
import concourse.bass as bass
from concourse import mybir

F32 = mybir.dt.float32
BF16 = mybir.dt.bfloat16
ACT = mybir.ActivationFunctionType
ALU = mybir.AluOpType
AX = mybir.AxisListType

P = 128
NB = 8
NT = 512
TOK = NB * NT
TB = 64
NBLK = NT // TB
CH = TB * NB
Q = 16
NCH = TB // Q
LN_EPS = 1e-5


@contextmanager
def stage(nc, *names):
    with ExitStack() as ctx:
        own = {n: ctx.enter_context(nc.semaphore(n)) for n in names}
        with nc.Block() as block:
            yield block, own
        for s in own.values():
            nc.gpsimd.sem_clear(s)
        nc.all_engine_barrier()


def layernorm_stage(nc, mem, src, dst, chunks):
    xc, sq, rs, ps = mem["ln_xc"], mem["ln_sq"], mem["ln_rs"], mem["ps"]
    ones = mem["ones_mean"]
    n = len(chunks)
    with stage(nc, "mean_ready", "centred", "squared", "var_ready", "ln_done", "rstd_ready", "normed") as (block, s):
        @block.tensor
        def _(pe):
            def mean(k):
                if k >= 2:
                    pe.wait_ge(s["centred"], k - 1)
                pe.matmul(ps[k % 2][:, 0:CH], ones[:, :], src[:, chunks[k]], start=True, stop=True).then_inc(s["mean_ready"], 1)

            mean(0)
            for k in range(n):
                if k + 1 < n:
                    mean(k + 1)
                pe.wait_ge(s["squared"], k + 1)
                if k >= 2:
                    pe.wait_ge(s["ln_done"], k - 1)
                pe.matmul(ps[2 + k % 2][:, 0:CH], ones[:, :], sq[:, k % 2, :], start=True, stop=True).then_inc(s["var_ready"], 1)

        @block.scalar
        def _(act):
            for k in range(n):
                act.wait_ge(s["centred"], k + 1)
                if k >= 2:
                    act.wait_ge(s["var_ready"], k - 1)
                act.activation(sq[:, k % 2, :], xc[:, k % 2, :], ACT.Square).then_inc(s["squared"], 1)
                act.wait_ge(s["var_ready"], k + 1)
                if k >= 2:
                    act.wait_ge(s["normed"], k - 1)
                act.activation(rs[:, k % 2, :], ps[2 + k % 2][:, 0:CH], ACT.Ln, bias=mem["eps"][:, 0:1]).then_inc(s["ln_done"], 1)
                act.wait_ge(s["ln_done"], k + 1)
                act.activation(rs[:, k % 2, :], rs[:, k % 2, :], ACT.Exp, scale=-0.5).then_inc(s["rstd_ready"], 1)

        @block.vector
        def _(dve):
            for k in range(n + 1):
                if k < n:
                    dve.wait_ge(s["mean_ready"], k + 1)
                    if k >= 2:
                        dve.wait_ge(s["squared"], k - 1)
                        dve.wait_ge(s["normed"], k - 1)
                    dve.tensor_tensor(xc[:, k % 2, :], src[:, chunks[k]], ps[k % 2][:, 0:CH], ALU.subtract).then_inc(s["centred"], 1)
                if k >= 1:
                    j = k - 1
                    dve.wait_ge(s["rstd_ready"], j + 1)
                    dve.wait_ge(s["centred"], j + 1)
                    dve.tensor_tensor(dst[:, chunks[j]], xc[:, j % 2, :], rs[:, j % 2, :], ALU.mult).then_inc(s["normed"], 1)


def layer0(nc, mem, A, x1):
    NE = 8
    FT = 4
    with ExitStack() as ctx:
        def sb(name, shape, dt=F32):
            return ctx.enter_context(nc.sbuf_tensor(name, shape, dt))

        ps = mem["ps"]
        w_in = sb("w_in", [P, 8, P])
        w_r = sb("w_r", [P, 2, 6 * P])
        w_rs = sb("w_rs", [P, 2, 3, 6 * P], BF16)
        w_res = sb("w_res", [P, 2, 6 * P])
        w_out = sb("w_out", [P, 2, P])
        conv_w = sb("conv_w", [P, 4, 4])
        conv_b = sb("conv_b", [P, 4])
        vec = sb("vec", [P, 8])
        a_neg = sb("a_neg", [P, 2, NB])
        dtb = sb("dtb", [P, 2, NB])
        d_b = sb("d_b", [P, 2, NB])
        zero16 = sb("zero16", [P, 2 * NB])
        cent = sb("cent", [P, NE])
        ln_g = sb("ln_g", [P, NE])
        ln_b = sb("ln_b", [P, NE])
        b1 = sb("b1", [P, NE, FT])
        b2 = sb("b2", [P, NE])
        w1 = sb("w1", [P, NE, FT * P])
        w2 = sb("w2", [P, NE, FT, P])
        rank = sb("rank", [P, 4, NE])
        sel_e = sb("sel_e", [NE, NE, P])
        bmask = sb("bmask", [P, NB])
        hsel = sb("hsel", [P, 2])

        x0 = sb("x0", [P, CH])
        xn = sb("xn", [P, CH])
        xh = sb("xh", [P, CH])
        zs = sb("zs", [P, 2, CH])
        raw = sb("raw", [P, 4, 3 * NB + CH])
        pin = sb("pin", [P, 6, CH])
        gff = sb("gff", [P, CH])
        yb = sb("yb", [P, 2, CH])

        aff = sb("aff", [P, 4, NE])
        affx = sb("affx", [P, 4])
        ea = sb("ea", [P, 4, NE])
        key = sb("key", [P, 4, NE])
        coef = sb("coef", [P, 4, NE])
        coefT = sb("coefT", [NE, CH])
        cb = sb("cb", [P, 2, CH])
        hb = sb("hb", [P, 2, FT, CH])
        tmp = sb("tmp", [P, 2, CH])
        sg = sb("sg", [P, CH])

        S = sb("S", [P, NB, 2, P])
        Ss = sb("Ss", [P, 3, NB, 2, P], BF16)
        Sr = sb("Sr", [P, NB, 2, P])
        V = sb("V", [P, 6, Q, NB])
        Wh = sb("Wh", [P, 2, Q, NB])
        Pc = sb("Pc", [P, 2, NB])
        G = sb("G", [P, 2, NB])
        Gs = sb("Gs", [P, 2, 3, NB], BF16)
        Gr = sb("Gr", [P, 2, 2, NB])
        Gq = sb("Gq", [P, 2, NB])
        Gq1 = sb("Gq1", [P, NB])
        rs = sb("rs", [P, NB])
        pre = sb("pre", [P, 6, NB])
        pre1 = sb("pre1", [P, 6, NB])
        e48 = sb("e48", [P, 6, NB])
        r48 = sb("r48", [P, 6, NB])
        Cs = sb("Cs", [P, 3, NB], BF16)
        Cr = sb("Cr", [P, 2, NB])
        CB = sb("CB", [P, Q, NB])
        prod = sb("prod", [P, 2, Q + 1, NB])
        Us = sb("Us", [P, 2, NB])
        dtv = sb("dtv", [P, 6, 2, NB])
        q1 = sb("q1", [P, 2, NB])
        y1 = sb("y1", [P, 2, NB])
        bT = sb("bT", [P, P])
        wT = sb("wT", [P, NB, 2 * P])
        Psel = sb("Psel", [P, 4, NB])

        with stage(nc, "loaded", "w_scaled", "split", "cast", "bias_mm", "bias_sum", "prep", "expd") as (block, s):
            loads = [(w_in[:, :, :], A["w_in"]), (w_r[:, :, :], A["w_r"]), (w_out[:, :, :], A["w_out"]),
                     (conv_w[:, :, :], A["conv_w"]), (conv_b[:, :], A["conv_b"]), (vec[:, :], A["vec"]),
                     (cent[:, :], A["cent"]), (ln_g[:, :], A["ln_g"]), (ln_b[:, :], A["ln_b"]),
                     (b1[:, :, :], A["b1"]), (b2[:, :], A["b2"]), (w1[:, :, :], A["w1"]), (w2[:, :, :, :], A["w2"]),
                     (rank[:, :, :], A["rank"]), (sel_e[:, :, :], A["sel_e"]), (bmask[:, :], A["bmask"]),
                     (hsel[:, :], A["hsel"])]
            n_loads = 16 * len(loads)

            @block.sync
            def _(sp):
                for dst, src in loads:
                    sp.dma_start(dst, src).then_inc(s["loaded"], 16)

            @block.gpsimd
            def _(pool):
                pool.memset(raw[:, :, 0:3 * NB], 0.0)
                pool.memset(S[:, :, :, :], 0.0)
                pool.memset(Ss[:, :, :, :, :], 0.0)
                pool.memset(Gs[:, :, :, :], 0.0)
                pool.memset(zero16[:, :], 0.0)
                pool.memset(rs[:, :], 0.0).then_inc(s["prep"], 1)

            @block.scalar
            def _(act):
                act.wait_ge(s["loaded"], n_loads)
                act.activation(vec[:, 2:4], vec[:, 2:4], ACT.Exp).then_inc(s["expd"], 1)

            @block.vector
            def _(dve):
                dve.wait_ge(s["loaded"], n_loads)
                dve.wait_ge(s["prep"], 1)
                dve.wait_ge(s["expd"], 1)
                for h in range(2):
                    z8 = zero16[:, 0:NB]
                    dve.tensor_scalar(dtb[:, h, :], z8, vec[:, h:h + 1], None, ALU.add)
                    dve.tensor_scalar(a_neg[:, h, :], z8, vec[:, 2 + h:3 + h], -1.0, ALU.add, ALU.mult)
                    dve.tensor_scalar(d_b[:, h, :], z8, vec[:, 4 + h:5 + h], None, ALU.add)
                    dve.tensor_scalar(w_r[:, h, :], w_r[:, h, :], vec[:, 6 + h:7 + h], None, ALU.mult)
                    dve.tensor_scalar(w_out[:, h, :], w_out[:, h, :], vec[:, 6 + h:7 + h], None, ALU.mult).then_inc(s["w_scaled"], 1)
                dve.wait_ge(s["w_scaled"], 2)
                dve.tensor_copy(w_rs[:, :, 0, :], w_r[:, :, :]).then_inc(s["split"], 1)
                dve.wait_ge(s["split"], 1)
                dve.tensor_tensor(w_res[:, :, :], w_r[:, :, :], w_rs[:, :, 0, :], ALU.subtract).then_inc(s["split"], 1)
                dve.wait_ge(s["split"], 2)
                dve.tensor_copy(w_rs[:, :, 1, :], w_res[:, :, :]).then_inc(s["split"], 1)
                dve.wait_ge(s["split"], 3)
                dve.tensor_tensor(w_rs[:, :, 2, :], w_res[:, :, :], w_rs[:, :, 1, :], ALU.subtract).then_inc(s["split"], 1)
                dve.wait_ge(s["bias_mm"], 1)
                dve.tensor_tensor(b1[:, :, :], b1[:, :, :], ps[0][:, 0:NE * FT].rearrange("p (e f) -> p e f", e=NE), ALU.add)
                for e in range(NE):
                    dve.tensor_scalar(w1[:, e, :], w1[:, e, :], ln_g[:, e:e + 1], None, ALU.mult)

            @block.tensor
            def _(pe):
                pe.wait_ge(s["loaded"], n_loads)
                for e in range(NE):
                    for f in range(FT):
                        last = pe.matmul(ps[0][:, e * FT + f:e * FT + f + 1], w1[:, e, f * P:(f + 1) * P], ln_b[:, e:e + 1],
                                         start=True, stop=True)
                last.then_inc(s["bias_mm"], 1)

        with nc.Fori(0, NBLK) as blk:
            with stage(nc, "x_loaded") as (block, s):
                @block.sync
                def _(sp):
                    sp.dma_start(x0[:, :], A["x0"][:, bass.ts(blk, CH)]).then_inc(s["x_loaded"], 16)
                    sp.wait_ge(s["x_loaded"], 16)
            layernorm_stage(nc, mem, x0, xn, [slice(0, CH)])
            layernorm_stage(nc, mem, xn, xh, [slice(0, CH)])

            with stage(nc, "projected", "moved", "ez", "z1", "z2", "z_out", "conv") as (block, s):
                @block.tensor
                def _(pe):
                    for m in range(8):
                        pe.matmul(ps[m][:, 0:CH], w_in[:, m, :], xn[:, :], start=True, stop=True).then_inc(s["projected"], 1)

                @block.scalar
                def _(act):
                    for m in range(2):
                        act.wait_ge(s["projected"], m + 1)
                        act.activation(zs[:, m, :], ps[m][:, 0:CH], ACT.Exp, scale=-1.0).then_inc(s["ez"], 1)
                    for m in range(2, 6):
                        act.wait_ge(s["projected"], m + 1)
                        act.activation(raw[:, m - 2, 3 * NB:], ps[m][:, 0:CH], ACT.Copy).then_inc(s["moved"], 1)
                    for m in range(6, 8):
                        act.wait_ge(s["projected"], m + 1)
                        act.activation(pin[:, m - 2, :], ps[m][:, 0:CH], ACT.Copy)

                @block.vector
                def _(dve):
                    for m in range(2):
                        dve.wait_ge(s["ez"], m + 1)
                        dve.tensor_scalar(zs[:, m, :], zs[:, m, :], 1.0, None, ALU.add).then_inc(s["z1"], 1)
                    for m in range(2):
                        dve.wait_ge(s["z1"], m + 1)
                        dve.reciprocal(zs[:, m, :], zs[:, m, :]).then_inc(s["z2"], 1)
                    for m in range(2):
                        dve.wait_ge(s["z2"], m + 1)
                        dve.tensor_tensor(zs[:, m, :], ps[m][:, 0:CH], zs[:, m, :], ALU.mult)
                    n = 0
                    for m in range(4):
                        dve.wait_ge(s["moved"], m + 1)
                        dve.tensor_scalar(pin[:, m, :], raw[:, m, 0:CH], conv_w[:, m, 0:1], conv_b[:, m:m + 1],
                                          ALU.mult, ALU.add).then_inc(s["conv"], 1)
                        n += 1
                        for k in range(1, 4):
                            dve.wait_ge(s["conv"], n)
                            dve.scalar_tensor_tensor(pin[:, m, :], raw[:, m, k * NB:k * NB + CH], conv_w[:, m, k:k + 1],
                                                     pin[:, m, :], ALU.mult, ALU.add).then_inc(s["conv"], 1)
                            n += 1
                    dve.wait_ge(s["conv"], n)
                    dve.tensor_copy(raw[:, :, 0:3 * NB], raw[:, :, CH:CH + 3 * NB])

            with stage(nc, "aff_mm", "ea_done", "a1", "a2", "mx", "eq", "k2", "oh", "coef_done", "ct_mm", "ct_done",
                       "c_mm", "cb_done", "up_mm", "h_done", "down_mm", "t_done", "acc_done") as (block, s):
                @block.tensor
                def _(pe):
                    for t in range(4):
                        last = pe.matmul(ps[0][:, t * NE:(t + 1) * NE], xn[:, t * P:(t + 1) * P], cent[:, :], start=True, stop=True)
                    last.then_inc(s["aff_mm"], 1)
                    up = 0

                    def ups(e):
                        nonlocal up
                        for f in range(FT):
                            if up >= 3:
                                pe.wait_ge(s["h_done"], up - 2)
                            pe.matmul(ps[3 + up % 3][:, 0:CH], w1[:, e, f * P:(f + 1) * P], xh[:, :], start=True, stop=True).then_inc(s["up_mm"], 1)
                            up += 1

                    ups(0)
                    pe.wait_ge(s["coef_done"], 1)
                    for t in range(4):
                        last = pe.transpose(ps[7][0:NE, t * P:(t + 1) * P], coef[:, t, :], mem["ident"][:, :])
                    last.then_inc(s["ct_mm"], 1)
                    pe.wait_ge(s["ct_done"], 1)
                    for e in range(NE):
                        if e >= 2:
                            pe.wait_ge(s["cb_done"], e - 1)
                        pe.matmul(ps[1 + e % 2][:, 0:CH], sel_e[:, e, :], coefT[:, :], start=True, stop=True).then_inc(s["c_mm"], 1)
                        if e + 1 < NE:
                            ups(e + 1)
                        if e >= 2:
                            pe.wait_ge(s["t_done"], e - 1)
                        for f in range(FT):
                            pe.wait_ge(s["h_done"], e * FT + f + 1)
                            last = pe.matmul(ps[6 + e % 2][:, 0:CH], w2[:, e, f, :], hb[:, e % 2, f, :], start=(f == 0), stop=(f == FT - 1))
                        last.then_inc(s["down_mm"], 1)

                @block.scalar
                def _(act):
                    act.wait_ge(s["a1"], 1)
                    act.activation(ea[:, :, :], aff[:, :, :], ACT.Exp, scale=-1.0).then_inc(s["ea_done"], 1)

                    def relus(e):
                        for f in range(FT):
                            n = e * FT + f
                            act.wait_ge(s["up_mm"], n + 1)
                            if e >= 2:
                                act.wait_ge(s["down_mm"], e - 1)
                            act.activation(hb[:, e % 2, f, :], ps[3 + n % 3][:, 0:CH], ACT.Relu, bias=b1[:, e, f:f + 1]).then_inc(s["h_done"], 1)

                    relus(0)
                    for e in range(NE):
                        act.wait_ge(s["c_mm"], e + 1)
                        if e >= 2:
                            act.wait_ge(s["t_done"], e - 1)
                        act.activation(cb[:, e % 2, :], ps[1 + e % 2][:, 0:CH], ACT.Copy).then_inc(s["cb_done"], 1)
                        if e + 1 < NE:
                            relus(e + 1)

                @block.vector
                def _(dve):
                    dve.wait_ge(s["aff_mm"], 1)
                    dve.tensor_copy(aff[:, :, :], ps[0][:, 0:4 * NE].rearrange("p (t e) -> p t e", t=4)).then_inc(s["a1"], 1)
                    dve.wait_ge(s["ea_done"], 1)
                    dve.tensor_scalar(ea[:, :, :], ea[:, :, :], 1.0, None, ALU.add).then_inc(s["a2"], 1)
                    dve.wait_ge(s["a1"], 1)
                    dve.tensor_reduce(affx[:, :], aff[:, :, :], AX.X, ALU.max).then_inc(s["mx"], 1)
                    dve.wait_ge(s["mx"], 1)
                    dve.tensor_tensor(key[:, :, :], aff[:, :, :], affx[:, :, None].to_broadcast([P, 4, NE]), ALU.is_equal).then_inc(s["eq"], 1)
                    dve.wait_ge(s["a2"], 1)
                    dve.reciprocal(ea[:, :, :], ea[:, :, :]).then_inc(s["a2"], 1)
                    dve.wait_ge(s["eq"], 1)
                    dve.tensor_tensor(key[:, :, :], key[:, :, :], rank[:, :, :], ALU.mult).then_inc(s["k2"], 1)
                    dve.wait_ge(s["k2"], 1)
                    dve.tensor_reduce(affx[:, :], key[:, :, :], AX.X, ALU.max).then_inc(s["k2"], 1)
                    dve.wait_ge(s["k2"], 2)
                    dve.tensor_tensor(key[:, :, :], key[:, :, :], affx[:, :, None].to_broadcast([P, 4, NE]), ALU.is_equal).then_inc(s["oh"], 1)
                    dve.wait_ge(s["oh"], 1)
                    dve.wait_ge(s["a2"], 2)
                    dve.tensor_tensor(coef[:, :, :], key[:, :, :], ea[:, :, :], ALU.mult).then_inc(s["coef_done"], 1)
                    dve.wait_ge(s["ct_mm"], 1)
                    dve.tensor_copy(coefT[:, :], ps[7][0:NE, 0:CH]).then_inc(s["ct_done"], 1)
                    for e in range(NE):
                        dve.wait_ge(s["down_mm"], e + 1)
                        dve.wait_ge(s["cb_done"], e + 1)
                        if e >= 2:
                            dve.wait_ge(s["acc_done"], e - 1)
                        dve.scalar_tensor_tensor(tmp[:, e % 2, :], ps[6 + e % 2][:, 0:CH], b2[:, e:e + 1], cb[:, e % 2, :],
                                                 ALU.add, ALU.mult).then_inc(s["t_done"], 1)

                @block.gpsimd
                def _(pool):
                    for e in range(NE):
                        pool.wait_ge(s["t_done"], e + 1)
                        if e:
                            pool.wait_ge(s["acc_done"], e)
                        pool.tensor_tensor(gff[:, :], xn[:, :] if e == 0 else gff[:, :], tmp[:, e % 2, :], ALU.add).then_inc(s["acc_done"], 1)

            silu_stage(nc, gff, sg, gff)

            with nc.Fori(0, NCH) as chunk:
                scan_chunk(nc, mem, dict(w_rs=w_rs, S=S, Ss=Ss, Sr=Sr, V=V, Wh=Wh, Pc=Pc, G=G, Gs=Gs, Gr=Gr, Gq=Gq, Gq1=Gq1,
                                         rs=rs, pre=pre, pre1=pre1, e48=e48, r48=r48, Cs=Cs, Cr=Cr, CB=CB, prod=prod, Us=Us,
                                         dtv=dtv, q1=q1, y1=y1, bT=bT, wT=wT, Psel=Psel, pin=pin, zs=zs, yb=yb, a_neg=a_neg,
                                         dtb=dtb, d_b=d_b, bmask=bmask, hsel=hsel, zero16=zero16), chunk)

            with stage(nc, "out_mm", "gated") as (block, s):
                @block.tensor
                def _(pe):
                    for h in range(2):
                        last = pe.matmul(ps[0][:, 0:CH], w_out[:, h, :], yb[:, h, :], start=(h == 0), stop=(h == 1))
                    last.then_inc(s["out_mm"], 1)

                @block.vector
                def _(dve):
                    dve.wait_ge(s["out_mm"], 1)
                    dve.tensor_tensor(gff[:, :], ps[0][:, 0:CH], gff[:, :], ALU.mult).then_inc(s["gated"], 1)
                    dve.wait_ge(s["gated"], 1)
                    v = lambda a: a[:, :].rearrange("p (t b) -> p b t", b=NB)
                    dve.tensor_tensor(x1[:, :].rearrange("p (b t) -> p b t", b=NB)[:, :, bass.ts(blk, TB)], v(gff), v(x0), ALU.add)


def silu_stage(nc, src, work, dst):
    with stage(nc, "e_done", "d_done", "r_done") as (block, s):
        @block.scalar
        def _(act):
            act.activation(work[:, :], src[:, :], ACT.Exp, scale=-1.0).then_inc(s["e_done"], 1)

        @block.vector
        def _(dve):
            dve.wait_ge(s["e_done"], 1)
            dve.tensor_scalar(work[:, :], work[:, :], 1.0, None, ALU.add).then_inc(s["d_done"], 1)
            dve.wait_ge(s["d_done"], 1)
            dve.reciprocal(work[:, :], work[:, :]).then_inc(s["r_done"], 1)
            dve.wait_ge(s["r_done"], 1)
            dve.tensor_tensor(dst[:, :], src[:, :], work[:, :], ALU.mult)


def scan_chunk(nc, mem, m, chunk):
    ps, ones = mem["ps"], mem["ones"]
    Ss, Gs, V, Wh, Pc, G = m["Ss"], m["Gs"], m["V"], m["Wh"], m["Pc"], m["G"]
    dtv, prod, pre, pre1 = m["dtv"], m["prod"], m["pre"], m["pre1"]
    W2 = [P, 2, NB]

    def both(a):
        return a[:, None, :].to_broadcast(W2)

    with stage(nc, "g_sq", "g_sum", "g_split", "w_mm", "ms_mm", "lnms", "rs_done", "pre_a", "pre_b", "pre_done", "e_done", "d_done",
               "r_done", "v_done", "c_split", "u_mm", "cb_prod", "dots_mm", "dt_a", "dt_b", "dt_c", "dt_d", "dt_e", 
               "dt_done", "dta", "da_done", "dx", "hist", "q_a", "q_done", "prod_done", "y_sum", "y_a", "y_done", "g_done",
               "yn_done", "us_done") as (block, s):
        step = chunk * Q

        @block.tensor
        def _(pe):
            for t in range(Q):
                if t >= 1:
                    pe.wait_ge(s["g_sum"], t)
                    pe.wait_ge(s["lnms"], t)
                    pe.matmul(ps[1][:, 0:NB], ones[:, :], m["Gq1"][:, :], start=True, stop=True).then_inc(s["ms_mm"], 1)
                    pe.wait_ge(s["g_split"], 3 * t)
                if t >= 1:
                    pe.wait_ge(s["pre_a"], t)
                for j in range(6):
                    for part in range(3):
                        for h in range(2):
                            last = pe.matmul(ps[0][:, j * 24:(j + 1) * 24], m["w_rs"][:, h, part, j * P:(j + 1) * P],
                                             Gs[:, h, :, :].rearrange("p c b -> p (c b)"),
                                             start=(part == 0 and h == 0), stop=(part == 2 and h == 1))
                last.then_inc(s["w_mm"], 1)
                pe.wait_ge(s["cb_prod"], t + 1)
                if t >= 1:
                    pe.wait_ge(s["prod_done"], t)
                    pe.wait_ge(s["q_a"], t)
                pe.matmul(ps[3][:, 0:(t + 1) * NB], ones[:, :], m["CB"][:, 0:t + 1, :].rearrange("p s b -> p (s b)"),
                          start=True, stop=True).then_inc(s["dots_mm"], 1)
                pe.wait_ge(s["c_split"], 3 * t + 3)
                if t >= 1:
                    pe.wait_ge(s["us_done"], t)
                for b in range(NB):
                    for h in range(2):
                        for part in range(3):
                            last = pe.matmul(ps[2][:, (h * NB + b) * 3:(h * NB + b) * 3 + 3], Ss[:, part, b, h, :],
                                             m["Cs"][:, :, b], start=(part == 0), stop=(part == 2))
                last.then_inc(s["u_mm"], 1)
            pe.wait_ge(s["g_sum"], Q)
            pe.wait_ge(s["lnms"], Q)
            pe.matmul(ps[1][:, 0:NB], ones[:, :], m["Gq1"][:, :], start=True, stop=True).then_inc(s["ms_mm"], 1)

        @block.scalar
        def _(act):
            def rstd(n):
                act.wait_ge(s["ms_mm"], n)
                if n >= 2:
                    act.wait_ge(s["yn_done"], n - 1)
                act.activation(m["rs"][:, :], ps[1][:, 0:NB], ACT.Ln, bias=mem["eps"][:, 0:1], scale=1.0 / (2 * P)).then_inc(s["lnms"], 1)
                act.wait_ge(s["lnms"], n + 1)
                act.activation(m["rs"][:, :], m["rs"][:, :], ACT.Exp, scale=-0.5).then_inc(s["rs_done"], 1)

            act.sem_inc(s["lnms"], 1)
            for t in range(Q):
                if t >= 1:
                    act.wait_ge(s["pre_b"], t)
                    rstd(t)
                act.wait_ge(s["pre_done"], t + 1)
                act.activation(m["e48"][:, :, :], pre[:, :, :], ACT.Exp, scale=-1.0).then_inc(s["e_done"], 1)
                act.wait_ge(s["dt_a"], t + 1)
                act.activation(dtv[:, 1, :, :], dtv[:, 0, :, :], ACT.Abs).then_inc(s["dt_b"], 1)
                act.wait_ge(s["dt_b"], t + 1)
                act.activation(dtv[:, 1, :, :], dtv[:, 1, :, :], ACT.Exp, scale=-1.0).then_inc(s["dt_c"], 1)
                act.wait_ge(s["dt_c"], t + 1)
                act.activation(dtv[:, 1, :, :], dtv[:, 1, :, :], ACT.Ln, bias=1.0).then_inc(s["dt_d"], 1)
                act.wait_ge(s["dta"], t + 1)
                act.activation(dtv[:, 4, :, :], dtv[:, 3, :, :], ACT.Exp).then_inc(s["da_done"], 1)
            act.wait_ge(s["pre_b"], Q)
            rstd(Q)

        @block.gpsimd
        def _(pool):
            for t in range(Q):
                pool.wait_ge(s["v_done"], t + 1)
                if t >= 1:
                    pool.wait_ge(s["y_a"], 3 * t - 1)
                pool.tensor_tensor(dtv[:, 0, :, :], V[:, 4:6, t, :], m["dtb"][:, :, :], ALU.add).then_inc(s["dt_a"], 1)
                pool.wait_ge(s["dt_a"], t + 1)
                pool.tensor_scalar(dtv[:, 5, :, :], dtv[:, 0, :, :], 0.0, None, ALU.max).then_inc(s["dt_e"], 1)
                pool.wait_ge(s["dt_d"], t + 1)
                pool.wait_ge(s["dt_e"], t + 1)
                pool.tensor_tensor(dtv[:, 2, :, :], dtv[:, 5, :, :], dtv[:, 1, :, :], ALU.add).then_inc(s["dt_done"], 1)
                pool.wait_ge(s["dt_done"], t + 1)
                pool.tensor_tensor(dtv[:, 3, :, :], dtv[:, 2, :, :], m["a_neg"][:, :, :], ALU.mult).then_inc(s["dta"], 1)
                pool.tensor_tensor(Wh[:, :, t, :], dtv[:, 2, :, :], V[:, 0:2, t, :], ALU.mult).then_inc(s["dx"], 1)
                pool.wait_ge(s["da_done"], t + 1)
                pool.wait_ge(s["prod_done"], t + 1)
                if t == 0:
                    pool.tensor_copy(Pc[:, :, :], dtv[:, 4, :, :]).then_inc(s["hist"], 1)
                else:
                    pool.tensor_tensor(Wh[:, :, 0:t, :], Wh[:, :, 0:t, :], dtv[:, 4, :, :][:, :, None, :].to_broadcast([P, 2, t, NB]), ALU.mult)
                    pool.tensor_tensor(Pc[:, :, :], Pc[:, :, :], dtv[:, 4, :, :], ALU.mult).then_inc(s["hist"], 1)
                pool.wait_ge(s["g_done"], t + 1)
                pool.tensor_tensor(m["Gq"][:, :, :], G[:, :, :], G[:, :, :], ALU.mult).then_inc(s["g_sq"], 1)
                pool.wait_ge(s["g_sq"], t + 1)
                if t >= 1:
                    pool.wait_ge(s["ms_mm"], t)
                pool.tensor_tensor(m["Gq1"][:, :], m["Gq"][:, 0, :], m["Gq"][:, 1, :], ALU.add).then_inc(s["g_sum"], 1)

        @block.vector
        def _(dve):
            yb = m["yb"]

            def col(t):
                return bass.ds((step + t) * NB, NB)

            for t in range(Q):
                dve.wait_ge(s["w_mm"], t + 1)
                dve.tensor_reduce(pre1[:, :, :], ps[0][:, 0:144].rearrange("p (m c b) -> p m b c", m=6, c=3), AX.X, ALU.add).then_inc(s["pre_a"], 1)
                dve.wait_ge(s["pre_a"], t + 1)
                if t >= 1:
                    dve.wait_ge(s["rs_done"], t)
                dve.tensor_tensor(pre1[:, :, :], pre1[:, :, :], m["rs"][:, None, :].to_broadcast([P, 6, NB]), ALU.mult).then_inc(s["pre_b"], 1)
                if t >= 1:
                    dve.tensor_tensor(yb[:, :, col(t - 1)], G[:, :, :], both(m["rs"]), ALU.mult).then_inc(s["yn_done"], 1)
                dve.wait_ge(s["pre_b"], t + 1)
                dve.tensor_tensor(pre[:, :, :], pre1[:, :, :], m["pin"][:, :, col(t)], ALU.add).then_inc(s["pre_done"], 1)
                dve.wait_ge(s["e_done"], t + 1)
                dve.tensor_scalar(m["r48"][:, :, :], m["e48"][:, :, :], 1.0, None, ALU.add).then_inc(s["d_done"], 1)
                dve.wait_ge(s["d_done"], t + 1)
                dve.reciprocal(m["r48"][:, :, :], m["r48"][:, :, :]).then_inc(s["r_done"], 1)
                dve.wait_ge(s["r_done"], t + 1)
                dve.tensor_tensor(V[:, :, t, :], pre[:, :, :], m["r48"][:, :, :], ALU.mult).then_inc(s["v_done"], 1)
                dve.wait_ge(s["v_done"], t + 1)
                dve.tensor_tensor(m["CB"][:, 0:t + 1, :], V[:, 2, 0:t + 1, :], V[:, 3, t, :][:, None, :].to_broadcast([P, t + 1, NB]),
                                  ALU.mult).then_inc(s["cb_prod"], 1)
                C, Cs, Cr = V[:, 3, t, :], m["Cs"], m["Cr"]
                if t >= 1:
                    dve.wait_ge(s["u_mm"], t)
                dve.tensor_copy(Cs[:, 0, :], C).then_inc(s["c_split"], 1)
                dve.wait_ge(s["c_split"], 3 * t + 1)
                dve.tensor_tensor(Cr[:, 0, :], C, Cs[:, 0, :], ALU.subtract).then_inc(s["y_a"], 1)
                dve.wait_ge(s["y_a"], 3 * t + 1)
                dve.tensor_copy(Cs[:, 1, :], Cr[:, 0, :]).then_inc(s["c_split"], 1)
                dve.wait_ge(s["c_split"], 3 * t + 2)
                dve.tensor_tensor(Cs[:, 2, :], Cr[:, 0, :], Cs[:, 1, :], ALU.subtract).then_inc(s["c_split"], 1)
                dve.wait_ge(s["dots_mm"], t + 1)
                if t >= 1:
                    dve.wait_ge(s["hist"], t)
                    dve.wait_ge(s["dx"], t)
                    dve.tensor_tensor(prod[:, :, 0:t, :], Wh[:, :, 0:t, :],
                                      ps[3][:, 0:t * NB].rearrange("p (s b) -> p s b", b=NB)[:, None, :, :].to_broadcast([P, 2, t, NB]),
                                      ALU.mult)
                dve.wait_ge(s["u_mm"], t + 1)
                dve.tensor_reduce(m["Us"][:, :, :], ps[2][:, 0:48].rearrange("p (h b c) -> p h b c", h=2, b=NB), AX.X, ALU.add).then_inc(s["us_done"], 1)
                dve.wait_ge(s["us_done"], t + 1)
                if t >= 1:
                    dve.tensor_tensor(prod[:, :, t, :], m["Us"][:, :, :], Pc[:, :, :], ALU.mult).then_inc(s["prod_done"], 1)
                else:
                    dve.tensor_copy(prod[:, :, t, :], m["Us"][:, :, :]).then_inc(s["prod_done"], 1)
                dve.wait_ge(s["prod_done"], t + 1)
                dve.tensor_reduce(m["y1"][:, :, :], prod[:, :, 0:t + 1, :].rearrange("p h s b -> p h b s"), AX.X, ALU.add).then_inc(s["y_sum"], 1)
                dve.wait_ge(s["dt_done"], t + 1)
                dve.tensor_tensor(m["q1"][:, :, :], dtv[:, 2, :, :], both(ps[3][:, t * NB:(t + 1) * NB]), ALU.mult).then_inc(s["q_a"], 1)
                dve.wait_ge(s["q_a"], t + 1)
                dve.tensor_tensor(m["q1"][:, :, :], m["q1"][:, :, :], m["d_b"][:, :, :], ALU.add).then_inc(s["q_done"], 1)
                dve.wait_ge(s["q_done"], 2 * t + 1)
                dve.tensor_tensor(m["q1"][:, :, :], m["q1"][:, :, :], V[:, 0:2, t, :], ALU.mult).then_inc(s["q_done"], 1)
                dve.wait_ge(s["da_done"], t + 1)
                dve.wait_ge(s["y_sum"], t + 1)
                dve.tensor_tensor(m["y1"][:, :, :], m["y1"][:, :, :], dtv[:, 4, :, :], ALU.mult).then_inc(s["y_a"], 1)
                dve.wait_ge(s["y_a"], 3 * t + 2)
                dve.wait_ge(s["q_done"], 2 * t + 2)
                dve.tensor_tensor(m["y1"][:, :, :], m["y1"][:, :, :], m["q1"][:, :, :], ALU.add).then_inc(s["y_a"], 1)
                dve.wait_ge(s["y_a"], 3 * t + 3)
                if t >= 1:
                    dve.wait_ge(s["g_sum"], t)
                    dve.wait_ge(s["yn_done"], t)
                dve.tensor_tensor(G[:, :, :], m["y1"][:, :, :], m["zs"][:, :, col(t)], ALU.mult).then_inc(s["g_done"], 1)
                dve.wait_ge(s["g_done"], t + 1)
                dve.tensor_copy(Gs[:, :, 0, :], G[:, :, :]).then_inc(s["g_split"], 1)
                dve.wait_ge(s["g_split"], 3 * t + 1)
                dve.tensor_tensor(m["Gr"][:, 0, :, :], G[:, :, :], Gs[:, :, 0, :], ALU.subtract).then_inc(s["y_done"], 1)
                dve.wait_ge(s["y_done"], t + 1)
                dve.tensor_copy(Gs[:, :, 1, :], m["Gr"][:, 0, :, :]).then_inc(s["g_split"], 1)
                dve.wait_ge(s["g_split"], 3 * t + 2)
                dve.tensor_tensor(Gs[:, :, 2, :], m["Gr"][:, 0, :, :], Gs[:, :, 1, :], ALU.subtract).then_inc(s["g_split"], 1)
            dve.wait_ge(s["rs_done"], Q)
            dve.tensor_tensor(yb[:, :, col(Q - 1)], G[:, :, :], both(m["rs"]), ALU.mult).then_inc(s["yn_done"], 1)

    S, Sr, bT, wT, Psel = m["S"], m["Sr"], m["bT"], m["wT"], m["Psel"]
    with stage(nc, "sel_done", "t_mm", "bT_done", "wT_done", "p_mm", "s_mul", "o_mm", "s_add", "sp1", "sp2", "sp3") as (block, s):
        @block.tensor
        def _(pe):
            pe.transpose(ps[0][:, 0:P], V[:, 2, :, :].rearrange("p s b -> p (s b)"), mem["ident"][:, :])
            for h in range(2):
                last = pe.transpose(ps[1][:, h * P:(h + 1) * P], Wh[:, h, :, :].rearrange("p s b -> p (s b)"), mem["ident"][:, :])
            last.then_inc(s["t_mm"], 1)
            pe.wait_ge(s["sel_done"], 1)
            pe.matmul(ps[2][:, 0:4 * NB], ones[:, :], Psel[:, :, :].rearrange("p h b -> p (h b)"), start=True, stop=True).then_inc(s["p_mm"], 1)
            pe.wait_ge(s["bT_done"], 1)
            for b2 in range(NB // 2):
                pe.wait_ge(s["wT_done"], 2 * b2 + 2)
                pe.matmul(ps[4 + b2][:, :], bT[:, :], wT[:, 2 * b2:2 * b2 + 2, :].rearrange("p b f -> p (b f)"), start=True, stop=True).then_inc(s["o_mm"], 1)

        @block.scalar
        def _(act):
            act.wait_ge(s["t_mm"], 1)
            act.activation(bT[:, :], ps[0][:, 0:P], ACT.Copy).then_inc(s["bT_done"], 1)
            for b in range(NB):
                act.activation(wT[:, b, :], ps[1][:, 0:2 * P], ACT.Copy, scale=m["bmask"][:, b:b + 1]).then_inc(s["wT_done"], 1)

        @block.vector
        def _(dve):
            for hh in range(2):
                last = dve.tensor_scalar(Psel[:, hh::2, :], Pc[:, :, :], m["hsel"][:, hh:hh + 1], None, ALU.mult)
            last.then_inc(s["sel_done"], 1)
            dve.wait_ge(s["p_mm"], 1)
            sv = S[:, :, :, :].rearrange("p b h (k j) -> p b (h k) j", k=2)
            pv = ps[2][:, 0:4 * NB].rearrange("p (h b) -> p b h", h=4)[:, :, :, None].to_broadcast([P, NB, 4, 64])
            dve.tensor_tensor(sv, sv, pv, ALU.mult).then_inc(s["s_mul"], 1)
            dve.wait_ge(s["s_mul"], 1)
            for b2 in range(NB // 2):
                sl = slice(2 * b2, 2 * b2 + 2)
                dve.wait_ge(s["o_mm"], b2 + 1)
                dve.tensor_tensor(S[:, sl, :, :], S[:, sl, :, :], ps[4 + b2][:, :].rearrange("p (b h f) -> p b h f", b=2, h=2), ALU.add).then_inc(s["s_add"], 1)
                dve.wait_ge(s["s_add"], b2 + 1)
                dve.tensor_copy(Ss[:, 0, sl, :, :], S[:, sl, :, :]).then_inc(s["sp1"], 1)
                dve.wait_ge(s["sp1"], b2 + 1)
                dve.tensor_tensor(Sr[:, sl, :, :], S[:, sl, :, :], Ss[:, 0, sl, :, :], ALU.subtract).then_inc(s["sp2"], 1)
                dve.wait_ge(s["sp2"], b2 + 1)
                dve.tensor_copy(Ss[:, 1, sl, :, :], Sr[:, sl, :, :]).then_inc(s["sp3"], 1)
                dve.wait_ge(s["sp3"], b2 + 1)
                dve.tensor_tensor(Ss[:, 2, sl, :, :], Sr[:, sl, :, :], Ss[:, 1, sl, :, :], ALU.subtract)


def attention_memory(sb, group):
    return dict(sc=sb("sc", [P, 3, NT]), pr=sb("pr", [P, 3, NT]), PT=sb("PT", [P, 2, 4, NT]),
                nmax=sb("nmax", [P, 4 * group]), rsum=sb("rsum", [P, 4 * group]), rinv=sb("rinv", [P, 4 * group]))


def heads_stage(nc, mem, w, group, causal, qm, kT, vm, bias, scale_of, prepare, out_acc, first=None):
    ps = mem["ps"]
    sc, pr, PT, nmax, rsum, rinv = (w[k] for k in ("sc", "pr", "PT", "nmax", "rsum", "rinv"))
    n_tiles = 4 * group

    def width(i):
        return (i + 1) * P if causal else NT

    with stage(nc, "q_ready", "v_ready", "s_mm", "sc_done", "mx_done", "exp_done", "rc_done", "norm_done", "t_mm", "tc_done",
               "pv_done") as (block, s):
        @block.tensor
        def _(pe):
            def scores(n):
                h, i = divmod(n, 4)
                if i == 0:
                    pe.wait_ge(s["q_ready"], h + 1)
                if n >= 3:
                    pe.wait_ge(s["sc_done"], n - 2)
                pe.matmul(ps[n % 3][:, 0:width(i)], qm(h)[:, i * P:(i + 1) * P], kT[:, 0:width(i)],
                          start=True, stop=True).then_inc(s["s_mm"], 1)

            def transposes(n):
                i = n % 4
                pe.wait_ge(s["norm_done"], n + 1)
                if n >= 2:
                    pe.wait_ge(s["tc_done"], n - 1)
                for j in range(width(i) // P):
                    last = pe.transpose(ps[3 + n % 2][:, j * P:(j + 1) * P], pr[:, n % 3, j * P:(j + 1) * P], mem["ident"][:, :])
                last.then_inc(s["t_mm"], 1)

            def values(h):
                if h == 0:
                    pe.wait_ge(s["v_ready"], group)
                pe.wait_ge(s["tc_done"], 4 * h + 4)
                for j in range(4):
                    c = j * P if causal else 0
                    last = pe.matmul(ps[5][:, c:NT], vm(h)[:, j, :], PT[:, h % 2, j, c:NT], start=(h == 0 and j == 0),
                                     stop=(h == group - 1 and j == 3), skip_group_check=True)
                last.then_inc(s["pv_done"], 1)

            scores(0)
            scores(1)
            for n in range(n_tiles):
                if n + 2 < n_tiles:
                    scores(n + 2)
                transposes(n)
                if n % 4 == 1 and n >= 4:
                    values(n // 4 - 1)
            values(group - 1)

        @block.scalar
        def _(act):
            def copy_out(n):
                h, i = divmod(n, 4)
                act.wait_ge(s["t_mm"], n + 1)
                if h >= 2 and i == 0:
                    act.wait_ge(s["pv_done"], h - 1)
                k = width(i)
                act.activation(PT[:, h % 2, 0:k // P, i * P:(i + 1) * P], ps[3 + n % 2][:, 0:k].rearrange("p (j t) -> p j t", t=P),
                               ACT.Copy).then_inc(s["tc_done"], 1)

            for n in range(n_tiles + 1):
                if n < n_tiles:
                    k = width(n % 4)
                    act.wait_ge(s["mx_done"], n + 1)
                    if n >= 3:
                        act.wait_ge(s["t_mm"], n - 2)
                    act.activation(pr[:, n % 3, 0:k], sc[:, n % 3, 0:k], ACT.Exp, bias=nmax[:, n:n + 1],
                                   accum_out=rsum[:, n:n + 1]).then_inc(s["exp_done"], 1)
                if n >= 1:
                    copy_out(n - 1)

        @block.gpsimd
        def _(pool):
            prepare[1](pool, s["v_ready"])

        @block.vector
        def _(dve):
            prepare[0](dve, s["q_ready"])

            def normalise(n):
                k = width(n % 4)
                dve.wait_ge(s["exp_done"], n + 1)
                dve.reciprocal(rinv[:, n:n + 1], rsum[:, n:n + 1]).then_inc(s["rc_done"], 1)
                dve.wait_ge(s["rc_done"], n + 1)
                dve.tensor_scalar(pr[:, n % 3, 0:k], pr[:, n % 3, 0:k], rinv[:, n:n + 1], None, ALU.mult).then_inc(s["norm_done"], 1)

            for n in range(n_tiles + 1):
                if n < n_tiles:
                    h, i = divmod(n, 4)
                    k = width(i)
                    dve.wait_ge(s["s_mm"], n + 1)
                    if n >= 3:
                        dve.wait_ge(s["exp_done"], n - 2)
                    dve.scalar_tensor_tensor(sc[:, n % 3, 0:k], bias(h, i), scale_of(h, i), ps[n % 3][:, 0:k], ALU.mult,
                                             ALU.add).then_inc(s["sc_done"], 1)
                    dve.wait_ge(s["sc_done"], n + 1)
                    dve.tensor_reduce(nmax[:, n:n + 1], sc[:, n % 3, 0:k], AX.X, ALU.max, negate=True).then_inc(s["mx_done"], 1)
                if n >= 1:
                    normalise(n - 1)
            dve.wait_ge(s["pv_done"], group)
            if first is None:
                dve.tensor_tensor(out_acc, out_acc, ps[5][:, :], ALU.add)
            else:
                dve.tensor_copy(out_acc, ps[5][:, :])


def residual_stage(nc, mem, x, sat, f, e, gap=None):
    n = TOK // CH
    with stage(nc, "e_done", "d_done", "r_done", "g_done", "m_done", "x_done") as (block, s):
        @block.scalar
        def _(act):
            for k in range(n):
                if k >= 2:
                    act.wait_ge(s["x_done"], k - 1)
                act.activation(e[:, k % 2, :], f[:, k * CH:(k + 1) * CH], ACT.Exp, scale=-1.0).then_inc(s["e_done"], 1)

        @block.gpsimd
        def _(pool):
            for k in range(n):
                c = slice(k * CH, (k + 1) * CH)
                pool.tensor_tensor(sat[:, c], sat[:, c], f[:, c], ALU.mult).then_inc(s["m_done"], 1)

        @block.vector
        def _(dve):
            for k in range(n):
                c = slice(k * CH, (k + 1) * CH)
                dve.wait_ge(s["e_done"], k + 1)
                dve.tensor_scalar(e[:, k % 2, :], e[:, k % 2, :], 1.0, None, ALU.add).then_inc(s["d_done"], 1)
                dve.wait_ge(s["d_done"], k + 1)
                dve.reciprocal(e[:, k % 2, :], e[:, k % 2, :]).then_inc(s["r_done"], 1)
                dve.wait_ge(s["r_done"], k + 1)
                dve.wait_ge(s["m_done"], k + 1)
                dve.tensor_tensor(e[:, k % 2, :], e[:, k % 2, :], sat[:, c], ALU.mult).then_inc(s["g_done"], 1)
                dve.wait_ge(s["g_done"], k + 1)
                dve.tensor_tensor(x[:, c], x[:, c], e[:, k % 2, :], ALU.add).then_inc(s["x_done"], 1)


CHUNKS = [slice(k * CH, (k + 1) * CH) for k in range(TOK // CH)]


def layer1(nc, mem, A, x):
    ps = mem["ps"]
    with ExitStack() as ctx:
        def sb(name, shape, dt=F32):
            return ctx.enter_context(nc.sbuf_tensor("l1_" + name, shape, dt))

        xn, sat = sb("xn", [P, TOK]), sb("sat", [P, TOK])
        wq, wk, wv = sb("wq", [P, P]), sb("wk", [P, P]), sb("wv", [P, P])
        cmask = sb("cmask", [P, NT])
        cn_w1, cn_w2, cn_w3, cn_w4 = sb("cn_w1", [P, P]), sb("cn_w2", [P, 64]), sb("cn_w3", [64, 32]), sb("cn_w4", [32, P])
        gc_w1, gc_w2, gc_w3 = sb("gc_w1", [P, 64]), sb("gc_w2", [64, 32]), sb("gc_w3", [32, P])
        cvec = sb("cvec", [P, 8])
        half = sb("half", [P, 2])
        twist = sb("twist", [P, P])
        with stage(nc, "loaded", "halved") as (block, s):
            loads = [(wq[:, :], A["l1_wq"]), (wk[:, :], A["l1_wk"]), (wv[:, :], A["l1_wv"]), (cmask[:, :], A["cmask"]),
                     (cn_w1[:, :], A["cn_w1"]), (cn_w2[:, :], A["cn_w2"]), (cn_w3[:, :], A["cn_w3"]), (cn_w4[:, :], A["cn_w4"]),
                     (gc_w1[:, :], A["gc_w1"]), (gc_w2[:, :], A["gc_w2"]), (gc_w3[:, :], A["gc_w3"]), (cvec[:, :], A["cvec"]),
                     (twist[:, :], A["twist"])]

            @block.sync
            def _(sp):
                for dst, src in loads:
                    sp.dma_start(dst, src).then_inc(s["loaded"], 16)
                sp.wait_ge(s["loaded"], 16 * len(loads))

            @block.vector
            def _(dve):
                dve.wait_ge(s["loaded"], 16 * len(loads))
                dve.tensor_scalar(half[:, :], cvec[:, 3:7:3], 0.5, None, ALU.mult)
        layernorm_stage(nc, mem, x, xn, CHUNKS)

        with ExitStack() as attn:
            def asb(name, shape, dt=F32):
                return attn.enter_context(nc.sbuf_tensor("l1_" + name, shape, dt))

            xb, qT, kT, vb = asb("xb", [P, NT]), asb("qT", [P, NT]), asb("kT", [P, NT]), asb("vb", [P, 4, P])
            w = attention_memory(asb, 1)
            with nc.Fori(0, NB) as b:
                qkv_stage(nc, mem, xn, b, xb, wq, wk, wv, qT, kT, vb, P ** -0.5)
                heads_stage(nc, mem, w, 1, True, lambda h: qT, kT, lambda h: vb,
                            lambda h, i: cmask[:, NT - (i + 1) * P:NT], lambda h, i: 1.0,
                            (lambda dve, sem: dve.sem_inc(sem, 1), lambda pool, sem: pool.sem_inc(sem, 1)),
                            sat[:, bass.ts(b, NT)], first=True)

        with ExitStack() as ffn:
            def fsb(name, shape, dt=F32):
                return ffn.enter_context(nc.sbuf_tensor("l1_" + name, shape, dt))

            hid = fsb("hid", [P, NB, CH])
            cpl = fsb("cpl", [P, 2, CH])
            gm, g1, g2, gt = fsb("gm", [P, NB]), fsb("g1", [64, NB]), fsb("g2", [32, NB]), fsb("gt", [P, NB])
            arc = fsb("arc", [P, 2])
            base = fsb("base", [P, NB])
            nc.scalar.preload_act_table_set("gelu_and_others")
            with stage(nc, "mean_done", "g_mm", "g_act", "ar_done", "b1_done") as (block, s):
                @block.tensor
                def _(pe):
                    pe.wait_ge(s["mean_done"], 1)
                    pe.matmul(ps[0][0:64, 0:NB], gc_w1[:, :], gm[:, :], start=True, stop=True).then_inc(s["g_mm"], 1)
                    pe.wait_ge(s["g_act"], 1)
                    pe.matmul(ps[1][0:32, 0:NB], gc_w2[:, :], g1[:, :], start=True, stop=True).then_inc(s["g_mm"], 1)
                    pe.wait_ge(s["g_act"], 2)
                    pe.matmul(ps[2][:, 0:NB], gc_w3[:, :], g2[:, :], start=True, stop=True).then_inc(s["g_mm"], 1)

                @block.scalar
                def _(act):
                    act.wait_ge(s["g_mm"], 1)
                    act.activation(g1[:, :], ps[0][0:64, 0:NB], ACT.Gelu, scale=1.0 / NT, bias=cvec[0:64, 4:5]).then_inc(s["g_act"], 1)
                    act.wait_ge(s["g_mm"], 2)
                    act.activation(g2[:, :], ps[1][0:32, 0:NB], ACT.Gelu, bias=cvec[0:32, 5:6]).then_inc(s["g_act"], 1)
                    act.wait_ge(s["g_mm"], 3)
                    act.activation(gt[:, :], ps[2][:, 0:NB], ACT.Tanh, scale=0.5, bias=half[:, 1:2]).then_inc(s["g_act"], 1)

                @block.vector
                def _(dve):
                    dve.tensor_reduce(gm[:, :], xn[:, :].rearrange("p (b t) -> p b t", b=NB), AX.X, ALU.add).then_inc(s["mean_done"], 1)
                    dve.tensor_scalar(arc[:, 0:1], cvec[:, 7:8], 0.3, None, ALU.mult)
                    dve.tensor_scalar(arc[:, 1:2], cvec[:, 7:8], 0.7, None, ALU.mult).then_inc(s["ar_done"], 1)
                    dve.wait_ge(s["g_act"], 3)
                    dve.wait_ge(s["ar_done"], 1)
                    dve.tensor_scalar(base[:, :], gt[:, :], arc[:, 1:2], 0.1, ALU.mult, ALU.add)
            with nc.Fori(0, 3) as cycle:
                with stage(nc, "mm", "acted", "read", "cpl_done", "tw_done") as (block, s):
                    ws = [cn_w1[:, :], cn_w2[:, :], cn_w3[:, :], cn_w4[:, :]]
                    rows = [P, 64, 32, P]

                    @block.tensor
                    def _(pe):
                        for l in range(4):
                            for k in range(NB):
                                if l:
                                    pe.wait_ge(s["acted"], (l - 1) * NB + k + 1)
                                src = xn[:, CHUNKS[k]] if l == 0 else hid[0:rows[l - 1], k, :]
                                pe.matmul(ps[k][0:rows[l], :], ws[l], src, start=True, stop=True).then_inc(s["mm"], 1)
                        for k in range(NB):
                            pe.wait_ge(s["acted"], 3 * NB + k + 1)
                            pe.matmul(ps[k][:, :], twist[:, :], xn[:, CHUNKS[k]], start=True, stop=True).then_inc(s["mm"], 1)

                    @block.scalar
                    def _(act):
                        for l in range(4):
                            for k in range(NB):
                                act.wait_ge(s["mm"], l * NB + k + 1)
                                r = rows[l]
                                if l < 3:
                                    act.activation(hid[0:r, k, :], ps[k][0:r, :], ACT.Gelu, bias=cvec[0:r, l:l + 1]).then_inc(s["acted"], 1)
                                else:
                                    act.activation(hid[:, k, :], ps[k][:, :], ACT.Tanh, scale=0.5, bias=half[:, 0:1]).then_inc(s["acted"], 1)

                    @block.vector
                    def _(dve):
                        for k in range(NB):
                            dve.wait_ge(s["acted"], 3 * NB + k + 1)
                            dve.tensor_scalar(hid[:, k, :], hid[:, k, :], arc[:, 0:1], base[:, k:k + 1], ALU.mult, ALU.add).then_inc(s["cpl_done"], 1)
                            dve.wait_ge(s["cpl_done"], k + 1)
                            dve.wait_ge(s["mm"], 4 * NB + k + 1)
                            if k >= 2:
                                dve.wait_ge(s["read"], k - 1)
                            dve.tensor_tensor(cpl[:, k % 2, :], hid[:, k, :], ps[k][:, :], ALU.mult).then_inc(s["tw_done"], 1)
                            dve.wait_ge(s["tw_done"], k + 1)
                            dve.tensor_tensor(xn[:, CHUNKS[k]], xn[:, CHUNKS[k]], cpl[:, k % 2, :], ALU.add).then_inc(s["read"], 1)
            nc.scalar.preload_act_table_set("natural_log_exp_and_others")
            residual_stage(nc, mem, x, sat, xn, cpl)


def qkv_stage(nc, mem, xn, b, xb, wq, wk, wv, qT, kT, vb, q_scale, q_bias=None, k_bias=None):
    ps = mem["ps"]
    with stage(nc, "x_done", "q_mm", "k_mm", "v_mm") as (block, s):
        @block.tensor
        def _(pe):
            pe.wait_ge(s["x_done"], 1)
            pe.matmul(ps[0][:, :], wq[:, :], xb[:, :], start=True, stop=True).then_inc(s["q_mm"], 1)
            pe.matmul(ps[1][:, :], wk[:, :], xb[:, :], start=True, stop=True).then_inc(s["k_mm"], 1)
            for j in range(4):
                last = pe.matmul(ps[2][:, j * P:(j + 1) * P], xb[:, j * P:(j + 1) * P], wv[:, :], start=True, stop=True)
            last.then_inc(s["v_mm"], 1)

        @block.scalar
        def _(act):
            act.wait_ge(s["q_mm"], 1)
            if q_bias is None:
                act.activation(qT[:, :], ps[0][:, :], ACT.Copy, scale=q_scale)
            else:
                act.activation(qT[:, :], ps[0][:, :], ACT.Identity, bias=q_bias)
            act.wait_ge(s["v_mm"], 1)
            act.activation(vb[:, :, :], ps[2][:, :].rearrange("p (j e) -> p j e", e=P), ACT.Copy)

        @block.vector
        def _(dve):
            dve.tensor_copy(xb[:, :], xn[:, bass.ts(b, NT)]).then_inc(s["x_done"], 1)
            dve.wait_ge(s["k_mm"], 1)
            if k_bias is None:
                dve.tensor_copy(kT[:, :], ps[1][:, :])
            else:
                dve.tensor_scalar(kT[:, :], ps[1][:, :], k_bias, None, ALU.add)


def layout_l1(i, A):
    A["l1_wq"], A["l1_wk"], A["l1_wv"] = i["L1_attn_Wq"], i["L1_attn_Wk"], i["L1_attn_Wv"]
    t, c = np.arange(P)[:, None], np.arange(NT)[None, :]
    A["cmask"] = np.where(c - 3 * P <= t, 0.0, -1e30).astype(np.float32)
    for n in ("cn_w1", "cn_w2", "cn_w3", "gc_w1", "gc_w2"):
        A[n] = i["L1_ffn_" + n]
    A["cn_w4"] = np.broadcast_to(i["L1_ffn_cn_w4"], (32, P))
    A["gc_w3"] = np.broadcast_to(i["L1_ffn_gc_w3"], (32, P))
    cv = np.zeros((P, 8), np.float32)
    for j, n in enumerate(("cn_b1", "cn_b2", "cn_b3", "cn_b4", "gc_b1", "gc_b2", "gc_b3", "adaptive_range")):
        v = i["L1_ffn_" + n]
        if v.shape == (1,):
            cv[:, j] = v[0]
        else:
            cv[0:v.shape[0], j] = v
    A["cvec"] = cv
    tw = np.zeros((P, P), np.float32)
    for r in range(32):
        tw[64 + r, r] = 1.0
        tw[96 + r, 32 + r] = -1.0
        tw[r, 64 + r] = -1.0
        tw[32 + r, 96 + r] = 1.0
    A["twist"] = tw


NH = 16
HD = P // NH
HG = 8


def group_prepare(w, group_index, qT, vb, hq, hv):
    def queries(dve, sem):
        for h in range(HG):
            dve.tensor_scalar(w["qm"][:, h, :], qT[:, :], hq[:, bass.ds(group_index * HG + h, 1)], None, ALU.mult).then_inc(sem, 1)

    def values(pool, sem):
        for h in range(HG):
            pool.tensor_tensor(w["vm"][:, h, :, :], vb[:, :, :],
                               hv[:, bass.ds(group_index * HG + h, 1), :].to_broadcast([P, 4, P]), ALU.mult).then_inc(sem, 1)

    return queries, values


def layer2(nc, mem, A, x):
    ps = mem["ps"]
    NE, TOPK, NPAIR = 16, 8, 8
    with ExitStack() as ctx:
        def sb(name, shape, dt=F32):
            return ctx.enter_context(nc.sbuf_tensor("l2_" + name, shape, dt))

        xn, sat = sb("xn", [P, TOK]), sb("sat", [P, TOK])
        layernorm_stage(nc, mem, x, xn, CHUNKS)

        with ExitStack() as attn:
            def asb(name, shape, dt=F32):
                return attn.enter_context(nc.sbuf_tensor("l2_" + name, shape, dt))

            wq, wk, wv = asb("wq", [P, P]), asb("wk", [P, P]), asb("wv", [P, P])
            rel, slope = asb("rel", [P, NT]), asb("slope", [P, NH])
            hq, hv = asb("hq", [P, NH]), asb("hv", [P, NH, P])
            xb, qT, kT, vb = asb("xb", [P, NT]), asb("qT", [P, NT]), asb("kT", [P, NT]), asb("vb", [P, 4, P])
            acc, slopes = asb("acc", [P, NT]), asb("slopes", [P, HG])
            w = attention_memory(asb, HG)
            w["qm"], w["vm"] = asb("qm", [P, HG, NT]), asb("vm", [P, HG, 4, P])
            with stage(nc, "loaded") as (block, s):
                loads = [(wq[:, :], A["l2_wq"]), (wk[:, :], A["l2_wk"]), (wv[:, :], A["l2_wv"]), (rel[:, :], A["rel"]),
                         (slope[:, :], A["slope"]), (hq[:, :], A["head_q"]), (hv[:, :, :], A["head_v"])]

                @block.sync
                def _(sp):
                    for dst, src in loads:
                        sp.dma_start(dst, src).then_inc(s["loaded"], 16)
                    sp.wait_ge(s["loaded"], 16 * len(loads))

            with nc.Fori(0, NB) as b:
                qkv_stage(nc, mem, xn, b, xb, wq, wk, wv, qT, kT, vb, P ** -0.5)
                zero_stage(nc, acc)
                with nc.Fori(0, NH // HG) as g:
                    copy_stage(nc, slopes[:, :], slope[:, bass.ts(g, HG)])
                    heads_stage(nc, mem, w, HG, True, lambda h: w["qm"][:, h, :], kT, lambda h: w["vm"][:, h, :, :],
                                lambda h, i: rel[:, NT - (i + 1) * P:NT], lambda h, i: slopes[:, h:h + 1],
                                group_prepare(w, g, qT, vb, hq, hv), acc[:, :])
                copy_stage(nc, sat[:, bass.ts(b, NT)], acc[:, :])

        with ExitStack() as ffn:
            def fsb(name, shape, dt=F32):
                return ffn.enter_context(nc.sbuf_tensor("l2_" + name, shape, dt))

            NTILE = TOK // P
            gate_w = fsb("gate_w", [P, NE])
            wg, wu, wd = fsb("wg", [P, NPAIR + 1, P]), fsb("wu", [P, NPAIR + 1, P]), fsb("wd", [P, NPAIR + 1, P])
            sel = fsb("sel", [NE, NPAIR, P])
            sq = fsb("sq", [P, 2, CH])
            gsq, gnorm, gi = fsb("gsq", [P, NE]), fsb("gnorm", [P, NE]), fsb("gi", [P, NE])
            xnorm, xinv = fsb("xnorm", [P, NTILE]), fsb("xinv", [P, NTILE])
            lg, lr = fsb("lg", [P, NTILE, NE]), fsb("lr", [P, NTILE, NE])
            top = fsb("top", [P, NTILE, TOPK])
            th = fsb("th", [P, NTILE, NE])
            csum, cinv = fsb("csum", [P, NTILE]), fsb("cinv", [P, NTILE])
            cT = fsb("cT", [NE, TOK])
            sl, us, cbuf = fsb("sl", [P, 3, CH]), fsb("us", [P, 2, CH]), fsb("cbuf", [P, 2, CH])

            with stage(nc, "loaded", "squared", "g_sq", "ss_mm", "g_mm", "ss_max", "root", "n_max", "inv", "gw_done", "lg_mm",
                       "lg_done", "top_done", "rep", "mask", "tanh_done", "sig", "wts", "sum_done", "comb", "c_mm", "c_done") as (block, s):
                loads = [(gate_w[:, :], A["l2_gate_w"]), (wg[:, :, :], A["l2_wg"]), (wu[:, :, :], A["l2_wu"]),
                         (wd[:, :, :], A["l2_wd"]), (sel[:, :, :], A["sel_pair"])]

                @block.sync
                def _(sp):
                    for dst, src in loads:
                        sp.dma_start(dst, src).then_inc(s["loaded"], 16)

                @block.tensor
                def _(pe):
                    pe.wait_ge(s["g_sq"], 1)
                    pe.matmul(ps[1][:, 0:NE], mem["ones"][:, :], gsq[:, :], start=True, stop=True).then_inc(s["g_mm"], 1)
                    for t in range(NTILE):
                        pe.wait_ge(s["squared"], t // 4 + 1)
                        pe.matmul(ps[0][:, t:t + 1], sq[:, (t // 4) % 2, (t % 4) * P:(t % 4 + 1) * P], mem["ones"][:, 0:1],
                                  start=True, stop=True).then_inc(s["ss_mm"], 1)
                    pe.wait_ge(s["gw_done"], 1)
                    for t in range(NTILE):
                        last = pe.matmul(ps[2][:, t * NE:(t + 1) * NE], xn[:, t * P:(t + 1) * P], gi[:, :], start=True, stop=True)
                    last.then_inc(s["lg_mm"], 1)
                    pe.wait_ge(s["comb"], 1)
                    for k in range(NB):
                        if k >= 2:
                            pe.wait_ge(s["c_done"], k - 1)
                        for t in range(4):
                            last = pe.transpose(ps[3 + k % 2][0:NE, t * P:(t + 1) * P], th[:, 4 * k + t, :], mem["ident"][:, :])
                        last.then_inc(s["c_mm"], 1)

                @block.scalar
                def _(act):
                    for k in range(NB):
                        if k >= 2:
                            act.wait_ge(s["ss_mm"], 4 * (k - 1))
                        act.activation(sq[:, k % 2, :], xn[:, CHUNKS[k]], ACT.Square).then_inc(s["squared"], 1)
                    act.wait_ge(s["ss_max"], 2)
                    act.activation(xnorm[:, :], xnorm[:, :], ACT.Sqrt).then_inc(s["root"], 1)
                    act.activation(gnorm[:, :], gnorm[:, :], ACT.Sqrt).then_inc(s["root"], 1)
                    act.wait_ge(s["lg_done"], 1)
                    act.activation(th[:, :, :], lg[:, :, :], ACT.Tanh, scale=0.5).then_inc(s["tanh_done"], 1)
                    for k in range(NB):
                        act.wait_ge(s["c_mm"], k + 1)
                        act.activation(cT[:, CHUNKS[k]], ps[3 + k % 2][0:NE, :], ACT.Copy).then_inc(s["c_done"], 1)

                @block.vector
                def _(dve):
                    dve.wait_ge(s["loaded"], 16 * len(loads))
                    dve.tensor_tensor(gsq[:, :], gate_w[:, :], gate_w[:, :], ALU.mult).then_inc(s["g_sq"], 1)
                    dve.wait_ge(s["g_mm"], 1)
                    dve.tensor_scalar(gnorm[:, :], ps[1][:, 0:NE], 1e-34, None, ALU.max).then_inc(s["ss_max"], 1)
                    dve.wait_ge(s["ss_mm"], NTILE)
                    dve.tensor_scalar(xnorm[:, :], ps[0][:, 0:NTILE], 1e-34, None, ALU.max).then_inc(s["ss_max"], 1)
                    dve.wait_ge(s["root"], 2)
                    dve.tensor_scalar(xnorm[:, :], xnorm[:, :], 1e-12, None, ALU.max).then_inc(s["n_max"], 1)
                    dve.tensor_scalar(gnorm[:, :], gnorm[:, :], 1e-12, None, ALU.max).then_inc(s["n_max"], 1)
                    dve.wait_ge(s["n_max"], 2)
                    dve.reciprocal(xinv[:, :], xnorm[:, :]).then_inc(s["inv"], 1)
                    dve.reciprocal(gsq[:, :], gnorm[:, :]).then_inc(s["inv"], 1)
                    dve.wait_ge(s["inv"], 2)
                    dve.tensor_tensor(gi[:, :], gate_w[:, :], gsq[:, :], ALU.mult).then_inc(s["gw_done"], 1)
                    dve.wait_ge(s["lg_mm"], 1)
                    dve.tensor_tensor(lg[:, :, :], ps[2][:, :].rearrange("p (t e) -> p t e", e=NE),
                                      xinv[:, :, None].to_broadcast([P, NTILE, NE]), ALU.mult).then_inc(s["lg_done"], 1)
                    dve.wait_ge(s["lg_done"], 1)
                    for t in range(NTILE):
                        dve.max(top[:, t, :], lg[:, t, :]).then_inc(s["top_done"], 1)
                    for t in range(NTILE):
                        dve.wait_ge(s["top_done"], t + 1)
                        dve.match_replace(lr[:, t, :], top[:, t, :], lg[:, t, :], -1e30).then_inc(s["rep"], 1)
                    dve.wait_ge(s["rep"], NTILE)
                    dve.tensor_scalar(lr[:, :, :], lr[:, :, :], -1e29, None, ALU.is_lt).then_inc(s["mask"], 1)
                    dve.wait_ge(s["tanh_done"], 1)
                    dve.tensor_scalar(th[:, :, :], th[:, :, :], 0.5, 0.5, ALU.mult, ALU.add).then_inc(s["sig"], 1)
                    dve.wait_ge(s["sig"], 1)
                    dve.wait_ge(s["mask"], 1)
                    dve.tensor_tensor(th[:, :, :], th[:, :, :], lr[:, :, :], ALU.mult).then_inc(s["wts"], 1)
                    dve.wait_ge(s["wts"], 1)
                    dve.tensor_reduce(csum[:, :], th[:, :, :], AX.X, ALU.add).then_inc(s["sum_done"], 1)
                    dve.wait_ge(s["sum_done"], 1)
                    dve.reciprocal(cinv[:, :], csum[:, :]).then_inc(s["sum_done"], 1)
                    dve.wait_ge(s["sum_done"], 2)
                    dve.tensor_tensor(th[:, :, :], th[:, :, :], cinv[:, :, None].to_broadcast([P, NTILE, NE]), ALU.mult).then_inc(s["comb"], 1)

            nc.scalar.preload_act_table_set("silu_and_others")
            with nc.Fori(0, NB) as k:
                with stage(nc, "g_mm", "u_mm", "c_mm", "silu_done", "c_done", "m1", "m2", "d_mm") as (block, s):
                    @block.tensor
                    def _(pe):
                        def up(e):
                            r = P if e < NPAIR else 64
                            if e >= 2:
                                pe.wait_ge(s["silu_done"], e - 1)
                            pe.matmul(ps[e % 2][0:r, :], wg[:, e, 0:r], xn[:, bass.ts(k, CH)], start=True, stop=True).then_inc(s["g_mm"], 1)
                            if e >= 2:
                                pe.wait_ge(s["m1"], e - 1)
                            pe.matmul(ps[2 + e % 2][0:r, :], wu[:, e, 0:r], xn[:, bass.ts(k, CH)], start=True, stop=True).then_inc(s["u_mm"], 1)
                            if e < NPAIR:
                                if e >= 2:
                                    pe.wait_ge(s["c_done"], e - 1)
                                pe.matmul(ps[4 + e % 2][:, :], sel[:, e, :], cT[:, bass.ts(k, CH)], start=True, stop=True).then_inc(s["c_mm"], 1)

                        up(0)
                        for e in range(NPAIR + 1):
                            if e < NPAIR:
                                up(e + 1)
                            r = P if e < NPAIR else 64
                            pe.wait_ge(s["m2"], e + 1)
                            pe.matmul(ps[6][:, :], wd[0:r, e, :], us[0:r, e % 2, :], start=(e == 0), stop=(e == NPAIR)).then_inc(s["d_mm"], 1)

                    @block.scalar
                    def _(act):
                        for e in range(NPAIR + 1):
                            r = P if e < NPAIR else 64
                            act.wait_ge(s["g_mm"], e + 1)
                            if e >= 3:
                                act.wait_ge(s["m2"], e - 2)
                            act.activation(sl[0:r, e % 3, :], ps[e % 2][0:r, :], ACT.Silu).then_inc(s["silu_done"], 1)
                            if e < NPAIR:
                                act.wait_ge(s["c_mm"], e + 1)
                                if e >= 2:
                                    act.wait_ge(s["m2"], e - 1)
                                act.activation(cbuf[:, e % 2, :], ps[4 + e % 2][:, :], ACT.Copy).then_inc(s["c_done"], 1)

                    @block.vector
                    def _(dve):
                        for e in range(NPAIR + 1):
                            r = P if e < NPAIR else 64
                            dve.wait_ge(s["silu_done"], e + 1)
                            dve.wait_ge(s["u_mm"], e + 1)
                            if e >= 2:
                                dve.wait_ge(s["d_mm"], e - 1)
                            if e < NPAIR:
                                dve.tensor_tensor(sl[0:r, e % 3, :], sl[0:r, e % 3, :], ps[2 + e % 2][0:r, :], ALU.mult).then_inc(s["m1"], 1)
                                dve.wait_ge(s["m1"], e + 1)
                                dve.wait_ge(s["c_done"], e + 1)
                                dve.tensor_tensor(us[:, e % 2, :], sl[:, e % 3, :], cbuf[:, e % 2, :], ALU.mult).then_inc(s["m2"], 1)
                            else:
                                dve.tensor_tensor(us[0:r, e % 2, :], sl[0:r, e % 3, :], ps[2 + e % 2][0:r, :], ALU.mult).then_inc(s["m2"], 1)
                        dve.wait_ge(s["d_mm"], NPAIR + 1)
                        dve.tensor_copy(xn[:, bass.ts(k, CH)], ps[6][:, :])

            nc.scalar.preload_act_table_set("natural_log_exp_and_others")
            residual_stage(nc, mem, x, sat, xn, cbuf)


def zero_stage(nc, a):
    with stage(nc, "zeroed") as (block, s):
        @block.gpsimd
        def _(pool):
            pool.memset(a[:, :], 0.0).then_inc(s["zeroed"], 1)


def copy_stage(nc, dst, src):
    with stage(nc, "copied") as (block, s):
        @block.vector
        def _(dve):
            dve.tensor_copy(dst, src).then_inc(s["copied"], 1)


def layout_l2(i, A):
    wkqv = i["L2_attn_W_kqv"]
    A["l2_wk"], A["l2_wq"], A["l2_wv"] = wkqv[0:P].T, wkqv[P:2 * P].T, wkqv[2 * P:3 * P].T
    t, c = np.arange(P)[:, None], np.arange(NT)[None, :]
    r = (c - 3 * P - t).astype(np.float32)
    A["rel"] = np.where(r <= 0, r, -1e30).astype(np.float32)
    sl = np.array([1.0 / (2.0 ** 8) ** ((n + 1) / NH) for n in range(NH)], np.float32)
    A["slope"] = np.broadcast_to(sl, (P, NH))
    own = (np.arange(P)[:, None] // HD == np.arange(NH)).astype(np.float32)
    A["head_q"] = own
    A["head_v"] = np.broadcast_to(own.T, (P, NH, P))
    A["l2_gate_w"] = i["L2_ffn_gate_w"].T
    for n, full, shared in (("l2_wg", "w_gate", "sw_gate"), ("l2_wu", "w_up", "sw_up")):
        a = np.zeros((P, 9, P), np.float32)
        a[:, 0:8, :] = i["L2_ffn_" + full].transpose(1, 0, 2).reshape(P, 8, P)
        a[:, 8, 0:64] = i["L2_ffn_" + shared]
        A[n] = a
    a = np.zeros((P, 9, P), np.float32)
    a[:, 0:8, :] = i["L2_ffn_w_down"].reshape(8, P, P).transpose(1, 0, 2)
    a[0:64, 8, :] = i["L2_ffn_sw_down"]
    A["l2_wd"] = a
    A["sel_pair"] = (np.arange(16)[:, None, None] == 2 * np.arange(8)[None, :, None] + np.arange(P)[None, None, :] // 64).astype(np.float32)


def butterfly_stages(dve, s, W, buf, work, weights, rows, transposed, bf0, m0):
    src, dst = W, buf
    for n, st in enumerate(range(8, -1, -1) if transposed else range(9)):
        d = 1 << st

        def half(t, r, k):
            return t[:, r, :].rearrange("p (n h s) -> p n h s", h=2, s=d)[:, :, k, :]

        def pair_weight(o, i):
            return weights[:, st, o, i, :].rearrange("p (n s) -> p n s", s=d)

        dve.wait_ge(s["bf"], bf0 + n * rows)
        for r in range(rows):
            for o in range(2):
                a, b = ((0, o), (1, o)) if transposed else ((o, 0), (o, 1))
                dve.tensor_tensor(half(dst, r, o), half(src, r, 0), pair_weight(*a), ALU.mult)
                dve.tensor_tensor(half(work, r, o), half(src, r, 1), pair_weight(*b), ALU.mult).then_inc(s["bf_m"], 1)
        dve.wait_ge(s["bf_m"], m0 + 2 * rows * (n + 1))
        for r in range(rows):
            dve.tensor_tensor(dst[:, r, :], dst[:, r, :], work[:, r, :], ALU.add).then_inc(s["bf"], 1)
        src, dst = dst, src
    return src


def layer3(nc, mem, A, x):
    ps = mem["ps"]
    NBU = 40
    LR = 1024
    with ExitStack() as ctx:
        def sb(name, shape, dt=F32):
            return ctx.enter_context(nc.sbuf_tensor("l3_" + name, shape, dt))

        xn, sat = sb("xn", [P, TOK]), sb("sat", [P, TOK])
        layernorm_stage(nc, mem, x, xn, CHUNKS)
        bias_dram = nc.dram_tensor("l3_bias_rows", (NH, LR), F32, kind="Internal").ap()

        with ExitStack() as attn:
            def asb(name, shape, dt=F32):
                return attn.enter_context(nc.sbuf_tensor("l3_" + name, shape, dt))

            wq, wk, wv, wo = asb("wq", [P, P]), asb("wk", [P, P]), asb("wv", [P, P]), asb("wo", [P, P])
            bvec = asb("bvec", [P, 4])
            gw = asb("gw", [P, 8, NH])
            gb = asb("gb", [P, 8])
            gconst = asb("gconst", [P, NH])
            hq, hv = asb("hq", [P, NH]), asb("hv", [P, NH, P])
            xb, qT, kT, vb = asb("xb", [P, NT]), asb("qT", [P, NT]), asb("kT", [P, NT]), asb("vb", [P, 4, P])
            acc = asb("acc", [P, NT])
            flip = asb("flip", [P, P])
            gp, gs = asb("gp", [P, 4, 8, NH]), asb("gs", [P, 4, 2, NH])
            gate, gates = asb("gate", [P, 4, NH]), asb("gates", [P, 4, HG])
            PBW = 7 * P
            pb = asb("pb", [P, HG, PBW])
            w = attention_memory(asb, HG)
            w["qm"], w["vm"] = asb("qm", [P, HG, NT]), asb("vm", [P, HG, 4, P])
            with ExitStack() as setup:
                rel_embed = setup.enter_context(nc.sbuf_tensor("l3_rel_embed", [NBU, NH], F32))
                onehot = setup.enter_context(nc.sbuf_tensor("l3_onehot", [NBU, LR], F32))
                rows = setup.enter_context(nc.sbuf_tensor("l3_rows", [NH, LR], F32))
                with stage(nc, "loaded", "row_mm", "row_done", "stored") as (block, s):
                    loads = [(rel_embed[:, :], A["rel_embed"]), (onehot[:, :], A["bucket_onehot"]),
                             (wq[:, :], A["l3_wq"]), (wk[:, :], A["l3_wk"]), (wv[:, :], A["l3_wv"]), (wo[:, :], A["l3_wo"]),
                             (bvec[:, :], A["l3_bvec"]), (gw[:, :, :], A["l3_gw"]), (gb[:, :], A["l3_gb"]),
                             (gconst[:, :], A["l3_gconst"]), (hq[:, :], A["head_q3"]), (hv[:, :, :], A["head_v"]), (flip[:, :], A["flip"])]

                    @block.sync
                    def _(sp):
                        for dst, src in loads:
                            sp.dma_start(dst, src).then_inc(s["loaded"], 16)
                        sp.wait_ge(s["row_done"], 2)
                        sp.dma_start(bias_dram, rows[:, :]).then_inc(s["stored"], 16)
                        sp.wait_ge(s["stored"], 16)

                    @block.tensor
                    def _(pe):
                        pe.wait_ge(s["loaded"], 16 * len(loads))
                        for c in range(2):
                            pe.matmul(ps[c][0:NH, :], rel_embed[:, :], onehot[:, c * 512:(c + 1) * 512], start=True, stop=True).then_inc(s["row_mm"], 1)

                    @block.vector
                    def _(dve):
                        for c in range(2):
                            dve.wait_ge(s["row_mm"], c + 1)
                            dve.tensor_copy(rows[:, c * 512:(c + 1) * 512], ps[c][0:NH, :]).then_inc(s["row_done"], 1)

            zero_stage(nc, sat)
            with nc.Fori(0, NH // HG) as g:
                with stage(nc, "loaded", "flip_mm", "flip_done") as (block, s):
                    hankel = [w["PT"][:, :, :, :].rearrange("p a j t -> p (a j t)"), w["vm"][:, :, :, :].rearrange("p h j t -> p (h j t)")]
                    cols = [slice(0, 512), slice(512, PBW)]

                    def rows_of(h):
                        return hankel[h // 4][:, (h % 4) * PBW:(h % 4 + 1) * PBW]

                    @block.sync
                    def _(sp):
                        for h in range(HG):
                            row = bias_dram[bass.ds(g * HG + h, 1), :]
                            sp.dma_start(rows_of(h), bass.AP(row.tensor, row.offset, [[1, P], [1, PBW]])).then_inc(s["loaded"], 16)

                    @block.tensor
                    def _(pe):
                        pe.wait_ge(s["loaded"], 16 * HG)
                        for h in range(HG):
                            for c in range(2):
                                n = 2 * h + c
                                if n >= 2:
                                    pe.wait_ge(s["flip_done"], n - 1)
                                pe.matmul(ps[c][:, 0:cols[c].stop - cols[c].start], flip[:, :], rows_of(h)[:, cols[c]],
                                          start=True, stop=True).then_inc(s["flip_mm"], 1)

                    @block.vector
                    def _(dve):
                        for h in range(HG):
                            for c in range(2):
                                dve.wait_ge(s["flip_mm"], 2 * h + c + 1)
                                dve.tensor_copy(pb[:, h, cols[c]], ps[c][:, 0:cols[c].stop - cols[c].start]).then_inc(s["flip_done"], 1)
                with nc.Fori(0, NB) as b:
                    qkv_stage(nc, mem, xn, b, xb, wq, wk, wv, qT, kT, vb, None, bvec[:, 0:1], bvec[:, 1:2])
                    with stage(nc, "p_mm", "g1", "g2", "g3", "e_done", "g4", "g5", "g6", "g7") as (block, s):
                        @block.tensor
                        def _(pe):
                            for i in range(4):
                                last = pe.matmul(ps[0][:, i * P:(i + 1) * P], xb[:, i * P:(i + 1) * P],
                                                 gw[:, :, :].rearrange("p e h -> p (e h)"), start=True, stop=True)
                            last.then_inc(s["p_mm"], 1)

                        @block.scalar
                        def _(act):
                            act.wait_ge(s["g2"], 1)
                            act.activation(gs[:, :, :, :], gs[:, :, :, :], ACT.Exp, scale=-1.0).then_inc(s["e_done"], 1)

                        @block.vector
                        def _(dve):
                            dve.wait_ge(s["p_mm"], 1)
                            for i in range(4):
                                dve.tensor_tensor(gp[:, i, :, :], ps[0][:, i * P:(i + 1) * P].rearrange("p (e h) -> p e h", e=8),
                                                  gb[:, :, None].to_broadcast([P, 8, NH]), ALU.add).then_inc(s["g1"], 1)
                            dve.wait_ge(s["g1"], 4)
                            dve.tensor_reduce(gs[:, :, :, :], gp[:, :, :, :].rearrange("p i (k e) h -> p (i k) h e", k=2), AX.X, ALU.add).then_inc(s["g2"], 1)
                            dve.wait_ge(s["e_done"], 1)
                            dve.tensor_scalar(gs[:, :, :, :], gs[:, :, :, :], 1.0, None, ALU.add).then_inc(s["g3"], 1)
                            dve.wait_ge(s["g3"], 1)
                            dve.reciprocal(gs[:, :, :, :], gs[:, :, :, :]).then_inc(s["g4"], 1)
                            dve.wait_ge(s["g4"], 1)
                            dve.tensor_tensor(gate[:, :, :], gs[:, :, 1, :], gconst[:, None, :].to_broadcast([P, 4, NH]), ALU.mult).then_inc(s["g5"], 1)
                            dve.wait_ge(s["g5"], 1)
                            dve.scalar_tensor_tensor(gate[:, :, :], gate[:, :, :], -1.0, gs[:, :, 0, :], ALU.add, ALU.mult).then_inc(s["g6"], 1)
                            dve.wait_ge(s["g6"], 1)
                            dve.tensor_scalar(gate[:, :, :], gate[:, :, :], 2.0, None, ALU.add).then_inc(s["g7"], 1)
                            dve.wait_ge(s["g7"], 1)
                            dve.tensor_copy(gates[:, :, :], gate[:, :, bass.ts(g, HG)])
                    heads_stage(nc, mem, w, HG, False, lambda h: w["qm"][:, h, :], kT, lambda h: w["vm"][:, h, :, :],
                                lambda h, i: pb[:, h, (3 - i) * P:(3 - i) * P + NT], lambda h, i: gates[:, i, h:h + 1],
                                group_prepare(w, g, qT, vb, hq, hv), acc[:, :], first=True)
                    store_rows_stage(nc, sat, acc, b, g)
            with stage(nc, "b_done", "o_mm", "o_done") as (block, s):
                @block.tensor
                def _(pe):
                    for k in range(NB):
                        pe.wait_ge(s["b_done"], k + 1)
                        pe.matmul(ps[k][:, :], wo[:, :], sat[:, CHUNKS[k]], start=True, stop=True).then_inc(s["o_mm"], 1)

                @block.scalar
                def _(act):
                    for k in range(NB):
                        act.wait_ge(s["o_mm"], k + 1)
                        act.activation(sat[:, CHUNKS[k]], ps[k][:, :], ACT.Identity, bias=bvec[:, 3:4]).then_inc(s["o_done"], 1)

                @block.vector
                def _(dve):
                    for k in range(NB):
                        dve.tensor_scalar(sat[:, CHUNKS[k]], sat[:, CHUNKS[k]], bvec[:, 2:3], None, ALU.add).then_inc(s["b_done"], 1)

        with ExitStack() as ffn:
            def fsb(name, shape, dt=F32):
                return ffn.enter_context(nc.sbuf_tensor("l3_" + name, shape, dt))

            H = 512
            FT = H // P
            up = fsb("up", [P, 2, H])
            down = fsb("down", [P, 1, H])
            buf, work = fsb("buf", [P, 2, H]), fsb("work", [P, 2, H])
            uw, dw = fsb("uw", [P, 9, 2, 2, 256]), fsb("dw", [P, 9, 2, 2, 256])
            ubias = fsb("ubias", [P, FT])
            obias = fsb("obias", [P, 2])
            hbias = fsb("hbias", [P, FT])
            w_up, w_down = fsb("w_up", [P, H]), fsb("w_down", [P, FT, P])
            hid = fsb("hid", [P, 2, FT, CH])
            e = fsb("e", [P, 2, CH])
            with stage(nc, "loaded", "bf", "bf_m", "t_mm", "hb_done", "ob_done") as (block, s):
                loads = [(up[:, :, :], A["l3_up"]), (down[:, :, :], A["l3_down"]), (ubias[:, :], A["l3_ubias"]), (obias[:, :], A["l3_obias"])]

                @block.sync
                def _(sp):
                    for dst, src in loads:
                        sp.dma_start(dst, src).then_inc(s["loaded"], 16)
                    sp.dma_start(uw[:, :, :, :, :], A["l3_uw"].partition_broadcast(P)).then_inc(s["loaded"], 16)
                    sp.dma_start(dw[:, :, :, :, :], A["l3_dw"].partition_broadcast(P)).then_inc(s["loaded"], 16)

                @block.vector
                def _(dve):
                    dve.wait_ge(s["loaded"], 16 * (len(loads) + 2))
                    dve.sem_inc(s["bf"], 1)
                    end = butterfly_stages(dve, s, up, buf, work, uw, 2, False, 1, 0)
                    n = 1 + 9 * 2
                    dve.wait_ge(s["bf"], n)
                    dve.tensor_copy(w_up[:, :], end[:, 0, :]).then_inc(s["bf"], 1)
                    for f in range(FT):
                        dve.tensor_tensor(work[:, 0, f * P:(f + 1) * P], end[:, 1, f * P:(f + 1) * P], mem["ident"][:, :], ALU.mult).then_inc(s["bf"], 1)
                    dve.wait_ge(s["bf"], n + 5)
                    dve.tensor_reduce(hbias[:, :], work[:, 0, :].rearrange("p (f c) -> p f c", f=FT), AX.X, ALU.add).then_inc(s["hb_done"], 1)
                    dve.wait_ge(s["hb_done"], 1)
                    dve.tensor_tensor(hbias[:, :], hbias[:, :], ubias[:, :], ALU.add)
                    butterfly_stages(dve, s, down, buf, work, dw, 1, True, n + 5, 36)
                    dve.tensor_scalar(obias[:, 0:1], obias[:, 0:1], obias[:, 1:2], None, ALU.add).then_inc(s["ob_done"], 1)
                    dve.wait_ge(s["t_mm"], 1)
                    dve.tensor_copy(w_down[:, :, :], ps[0][:, :].rearrange("p (f d) -> p f d", f=FT))

                @block.tensor
                def _(pe):
                    pe.wait_ge(s["bf"], 1 + 9 * 2 + 5 + 9)
                    for f in range(FT):
                        last = pe.transpose(ps[0][:, f * P:(f + 1) * P], buf[:, 0, f * P:(f + 1) * P], mem["ident"][:, :])
                    last.then_inc(s["t_mm"], 1)

            nc.scalar.preload_act_table_set("gelu_and_others")
            with stage(nc, "up_mm", "gelu_done", "down_mm", "out_done") as (block, s):
                @block.tensor
                def _(pe):
                    def ups(k):
                        for f in range(FT):
                            if k:
                                pe.wait_ge(s["gelu_done"], (k - 1) * FT + f + 1)
                            pe.matmul(ps[f][:, :], w_up[:, f * P:(f + 1) * P], xn[:, CHUNKS[k]], start=True, stop=True).then_inc(s["up_mm"], 1)

                    ups(0)
                    for k in range(NB):
                        if k + 1 < NB:
                            ups(k + 1)
                        if k >= 2:
                            pe.wait_ge(s["out_done"], k - 1)
                        for f in range(FT):
                            pe.wait_ge(s["gelu_done"], k * FT + f + 1)
                            last = pe.matmul(ps[4 + k % 2][:, :], w_down[:, f, :], hid[:, k % 2, f, :], start=(f == 0), stop=(f == FT - 1))
                        last.then_inc(s["down_mm"], 1)

                @block.scalar
                def _(act):
                    for k in range(NB):
                        for f in range(FT):
                            act.wait_ge(s["up_mm"], k * FT + f + 1)
                            if k >= 2:
                                act.wait_ge(s["down_mm"], k - 1)
                            act.activation(hid[:, k % 2, f, :], ps[f][:, :], ACT.Gelu, bias=hbias[:, f:f + 1]).then_inc(s["gelu_done"], 1)

                @block.vector
                def _(dve):
                    for k in range(NB):
                        dve.wait_ge(s["down_mm"], k + 1)
                        if k + 1 < NB:
                            dve.wait_ge(s["up_mm"], (k + 2) * FT)
                        dve.tensor_scalar(xn[:, CHUNKS[k]], ps[4 + k % 2][:, :], obias[:, 0:1], None, ALU.add).then_inc(s["out_done"], 1)
            nc.scalar.preload_act_table_set("natural_log_exp_and_others")
            residual_stage(nc, mem, x, sat, xn, e)


def store_rows_stage(nc, sat, acc, b, g):
    with stage(nc, "added") as (block, s):
        @block.vector
        def _(dve):
            dve.tensor_tensor(sat[:, bass.ts(b, NT)], sat[:, bass.ts(b, NT)], acc[:, :], ALU.add).then_inc(s["added"], 1)


def layout_l3(i, A):
    for n, k in (("l3_wq", "q_w"), ("l3_wk", "k_w"), ("l3_wv", "v_w"), ("l3_wo", "out_w")):
        A[n] = i["L3_attn_" + k].T
    A["l3_bvec"] = np.stack([i["L3_attn_" + k] for k in ("q_b", "k_b", "v_b", "out_b")], axis=1)
    own = (np.arange(P)[:, None] // HD == np.arange(NH)).astype(np.float32)
    A["head_q3"] = (own * np.float32(HD ** -0.5)).astype(np.float32)
    gw = np.zeros((NH, HD, 8, NH), np.float32)
    for h in range(NH):
        gw[h, :, :, h] = i["L3_attn_gru_w"].T
    A["l3_gw"] = gw.reshape(P, 8, NH)
    A["l3_gb"] = np.broadcast_to(i["L3_attn_gru_b"], (P, 8))
    A["l3_gconst"] = np.broadcast_to(i["L3_attn_gru_const"].reshape(NH), (P, NH))
    A["flip"] = np.eye(P, dtype=np.float32)[::-1]
    A["rel_embed"] = i["L3_attn_rel_embed"]
    rel = np.arange(-511, 512)
    n = np.abs(rel)
    large = np.log(np.maximum(n, 1).astype(np.float32) / np.float32(10)) / np.float32(np.log(100 / 10)) * np.float32(10)
    large = np.minimum((10 + large).astype(np.int32), 19)
    bucket = (rel > 0) * 20 + np.where(n < 10, n, large)
    oh = np.zeros((40, 1024), np.float32)
    oh[bucket, np.arange(1023)] = 1.0
    A["bucket_onehot"] = oh
    A["l3_up"] = np.stack([i["L3_ffn_W_exp"], np.broadcast_to(i["L3_ffn_b_exp"], (P, 512))], axis=1)
    A["l3_down"] = i["L3_ffn_W_con"].T.reshape(P, 1, 512)
    A["l3_uw"] = i["L3_ffn_up_weights"].transpose(0, 2, 3, 1)
    A["l3_dw"] = i["L3_ffn_down_weights"].transpose(0, 2, 3, 1)
    A["l3_ubias"] = columns(i["L3_ffn_up_bias"], 4)
    A["l3_obias"] = np.stack([i["L3_ffn_b_con"], i["L3_ffn_down_bias"]], axis=1)


def layout_rest(i, A):
    layout_l1(i, A)
    layout_l2(i, A)
    layout_l3(i, A)


def shared_memory(nc, ctx, A):
    def sb(name, shape, dt=F32):
        return ctx.enter_context(nc.sbuf_tensor(name, shape, dt))

    mem = dict(
        ps=[ctx.enter_context(nc.psum_tensor(f"bank{i}", [P, 512], F32)) for i in range(8)],
        ident=sb("ident", [P, P]), ones=sb("ones", [P, P]), ones_mean=sb("ones_mean", [P, P]), eps=sb("eps", [P, 1]),
        ln_xc=sb("ln_xc", [P, 2, CH]), ln_sq=sb("ln_sq", [P, 2, CH]), ln_rs=sb("ln_rs", [P, 2, CH]))
    with stage(nc, "loaded") as (block, s):
        @block.sync
        def _(sp):
            sp.dma_start(mem["ident"][:, :], A["ident"]).then_inc(s["loaded"], 16)
            sp.wait_ge(s["loaded"], 16)

        @block.gpsimd
        def _(pool):
            pool.memset(mem["ones"][:, :], 1.0)
            pool.memset(mem["ones_mean"][:, :], 1.0 / P)
            pool.memset(mem["eps"][:, :], LN_EPS)
    return mem


def program(nc, A, out, layers=4):
    with ExitStack() as ctx:
        x1 = ctx.enter_context(nc.sbuf_tensor("x1", [P, TOK], F32))
        mem = shared_memory(nc, ctx, A)
        nc.scalar.preload_act_table_set("natural_log_exp_and_others")
        layer0(nc, mem, A, x1)
        if layers >= 2:
            layer1(nc, mem, A, x1)
        if layers >= 3:
            layer2(nc, mem, A, x1)
        if layers >= 4:
            layer3(nc, mem, A, x1)
        with stage(nc, "stored") as (block, s):
            @block.sync
            def _(sp):
                sp.dma_start(out, x1[:, :]).then_inc(s["stored"], 16)
                sp.wait_ge(s["stored"], 16)


def columns(v, n):
    return v.reshape(n, P).T


def layout(i):
    c = np.ascontiguousarray
    A = {}
    A["ident"] = np.eye(P, dtype=np.float32)
    A["x0"] = i["L0_attn_u"].transpose(2, 1, 0).reshape(P, TOK)
    w = np.concatenate([i["L0_attn_W_in"][:768], np.repeat(i["L0_attn_W_in"][768:], 64, axis=0)], axis=0)
    A["w_in"] = w.reshape(8, P, P).transpose(2, 0, 1)
    w = np.concatenate([i["L0_attn_W_rxbc"], np.repeat(i["L0_attn_W_rdt"], 64, axis=0)], axis=0)
    A["w_r"] = w.reshape(6 * P, 2, P).transpose(2, 1, 0)
    A["w_out"] = i["L0_attn_W_out"].reshape(P, 2, P).transpose(2, 1, 0)
    A["conv_w"] = i["L0_attn_conv_w"].reshape(4, P, 4).transpose(1, 0, 2)
    A["conv_b"] = columns(i["L0_attn_conv_b"], 4)
    A["vec"] = np.concatenate([columns(np.repeat(i["L0_attn_" + n], 64), 2) for n in ("dt_bias", "A_log", "D_param")]
                              + [columns(i["L0_attn_norm_w"], 2)], axis=1)
    A["cent"] = i["L0_ffn_centroids"].T
    A["ln_g"] = i["L0_ffn_ln_g"].T
    A["ln_b"] = i["L0_ffn_ln_b"].T
    A["b1"] = i["L0_ffn_b1"].reshape(8, 4, P).transpose(2, 0, 1)
    A["b2"] = i["L0_ffn_b2"].T
    A["w1"] = i["L0_ffn_w1"].transpose(2, 0, 1)
    A["w2"] = i["L0_ffn_w2"].reshape(8, P, 4, P).transpose(3, 0, 2, 1)
    A["rank"] = np.broadcast_to((8.0 - np.arange(8)).astype(np.float32), (P, 4, 8))
    A["sel_e"] = np.broadcast_to(np.eye(8, dtype=np.float32)[:, :, None], (8, 8, P))
    A["bmask"] = (np.arange(P)[:, None] % 8 == np.arange(8)).astype(np.float32)
    A["hsel"] = (np.arange(P)[:, None] == 64 * np.arange(2)).astype(np.float32)
    layout_rest(i, A)
    return {n: c(a) for n, a in A.items()}


def kernel(**inputs):
    import concourse.bacc as bacc
    from concourse.bass_utils import run_bass_kernel_spmd

    arrays = layout({n: np.asarray(a) for n, a in inputs.items()})
    nc = bacc.Bacc("TRN2", target_bir_lowering=False, num_devices=1)
    A = {n: nc.dram_tensor(f"in_{n}", a.shape, mybir.dt.from_np(a.dtype), kind="ExternalInput").ap() for n, a in arrays.items()}
    out = nc.dram_tensor("out_x", (P, TOK), F32, kind="ExternalOutput").ap()
    program(nc, A, out)
    r = run_bass_kernel_spmd(nc, [{f"in_{n}": a for n, a in arrays.items()}], core_ids=[0])
    return r.results[0]["out_x"].reshape(P, NB, NT).transpose(1, 2, 0)
```

```python
from contextlib import ExitStack, contextmanager

import numpy as np
import concourse.bass as bass
from concourse import mybir

F32 = mybir.dt.float32
BF16 = mybir.dt.bfloat16
ACT = mybir.ActivationFunctionType
ALU = mybir.AluOpType
AX = mybir.AxisListType

P = 128
NB = 8
NT = 512
TOK = NB * NT
TB = 64
NBLK = NT // TB
CH = TB * NB
Q = 16
NCH = TB // Q
LN_EPS = 1e-5


@contextmanager
def stage(nc, *names):
    with ExitStack() as ctx:
        own = {n: ctx.enter_context(nc.semaphore(n)) for n in names}
        with nc.Block() as block:
            yield block, own
        numbers = sorted(s.num for s in own.values())
        first = 0
        for i in range(len(numbers)):
            if i + 1 == len(numbers) or numbers[i + 1] != numbers[i] + 1:
                nc.gpsimd.sem_clear(range(numbers[first], numbers[i] + 1))
                first = i + 1
        nc.all_engine_barrier()


def layernorm_stage(nc, mem, src, dst, chunks):
    xc, sq, rs, ps = mem["ln_xc"], mem["ln_sq"], mem["ln_rs"], mem["ps"]
    ones = mem["ones_mean"]
    n = len(chunks)
    with stage(nc, "mean_ready", "centred", "squared", "var_ready", "ln_done", "rstd_ready", "normed") as (block, s):
        @block.tensor
        def _(pe):
            def mean(k):
                if k >= 2:
                    pe.wait_ge(s["centred"], k - 1)
                pe.matmul(ps[k % 2][:, 0:CH], ones[:, :], src[:, chunks[k]], start=True, stop=True).then_inc(s["mean_ready"], 1)

            mean(0)
            for k in range(n):
                if k + 1 < n:
                    mean(k + 1)
                pe.wait_ge(s["squared"], k + 1)
                if k >= 2:
                    pe.wait_ge(s["ln_done"], k - 1)
                pe.matmul(ps[2 + k % 2][:, 0:CH], ones[:, :], sq[:, k % 2, :], start=True, stop=True).then_inc(s["var_ready"], 1)

        @block.scalar
        def _(act):
            for k in range(n):
                act.wait_ge(s["centred"], k + 1)
                if k >= 2:
                    act.wait_ge(s["var_ready"], k - 1)
                act.activation(sq[:, k % 2, :], xc[:, k % 2, :], ACT.Square).then_inc(s["squared"], 1)
                act.wait_ge(s["var_ready"], k + 1)
                if k >= 2:
                    act.wait_ge(s["normed"], k - 1)
                act.activation(rs[:, k % 2, :], ps[2 + k % 2][:, 0:CH], ACT.Ln, bias=mem["eps"][:, 0:1]).then_inc(s["ln_done"], 1)
                act.wait_ge(s["ln_done"], k + 1)
                act.activation(rs[:, k % 2, :], rs[:, k % 2, :], ACT.Exp, scale=-0.5).then_inc(s["rstd_ready"], 1)

        @block.vector
        def _(dve):
            for k in range(n + 1):
                if k < n:
                    dve.wait_ge(s["mean_ready"], k + 1)
                    if k >= 2:
                        dve.wait_ge(s["squared"], k - 1)
                        dve.wait_ge(s["normed"], k - 1)
                    dve.tensor_tensor(xc[:, k % 2, :], src[:, chunks[k]], ps[k % 2][:, 0:CH], ALU.subtract).then_inc(s["centred"], 1)
                if k >= 1:
                    j = k - 1
                    dve.wait_ge(s["rstd_ready"], j + 1)
                    dve.wait_ge(s["centred"], j + 1)
                    dve.tensor_tensor(dst[:, chunks[j]], xc[:, j % 2, :], rs[:, j % 2, :], ALU.mult).then_inc(s["normed"], 1)


def layer0(nc, mem, A, x1):
    NE = 8
    FT = 4
    with ExitStack() as ctx:
        def sb(name, shape, dt=F32):
            return ctx.enter_context(nc.sbuf_tensor(name, shape, dt))

        ps = mem["ps"]
        w_in = sb("w_in", [P, 8, P])
        w_r = sb("w_r", [P, 2, 6 * P])
        w_rs = sb("w_rs", [P, 2, 3, 6 * P], BF16)
        w_out = sb("w_out", [P, 2, P])
        conv_w = sb("conv_w", [P, 4, 4])
        conv_b = sb("conv_b", [P, 4])
        vec = sb("vec", [P, 8])
        a_col = sb("a_col", [P, 2])
        dtb = sb("dtb", [P, 2, NB])
        d_b = sb("d_b", [P, 2, NB])
        a_b = sb("a_b", [P, 2, NB])
        zero16 = sb("zero16", [P, 2 * NB])
        cent = sb("cent", [P, NE])
        ln_g = sb("ln_g", [P, NE])
        ln_b = sb("ln_b", [P, NE])
        b1 = sb("b1", [P, NE, FT])
        b2 = sb("b2", [P, NE])
        w1 = sb("w1", [P, NE, FT * P])
        w2 = sb("w2", [P, NE, FT, P])
        rank = sb("rank", [P, 4, NE])
        sel_e = sb("sel_e", [NE, NE, P])
        bmask = sb("bmask", [P, NB])
        hsel = sb("hsel", [P, 2])

        x0 = sb("x0", [P, CH])
        xn = sb("xn", [P, CH])
        xh = sb("xh", [P, CH])
        zs = sb("zs", [P, 2, CH + Q * NB])
        raw = sb("raw", [P, 4, 3 * NB + CH])
        pin = sb("pin", [P, 6, CH + Q * NB])
        gff = sb("gff", [P, CH])
        yb = sb("yb", [P, 2, CH])

        aff = sb("aff", [P, 4, NE])
        affx = sb("affx", [P, 4])
        ea = sb("ea", [P, 4, NE])
        key = sb("key", [P, 4, NE])
        coef = sb("coef", [P, 4, NE])
        coefT = sb("coefT", [NE, CH])
        cb = sb("cb", [P, 2, CH])
        hb = sb("hb", [P, 2, FT, CH])
        w_res = hb[:, 0, 0:3, :].rearrange("p f c -> p (f c)").rearrange("p (h c) -> p h c", h=2)
        tmp = sb("tmp", [P, 2, CH])
        sg = sb("sg", [P, CH])

        S = sb("S", [P, NB, 2, P])
        Ss = sb("Ss", [P, 3, NB, 2, P], BF16)
        Sr = sb("Sr", [P, NB, 2, P])
        V = sb("V", [P, 6, Q, NB])
        Wh = sb("Wh", [P, 2, Q, NB])
        Pc = sb("Pc", [P, 2, NB])
        G = sb("G", [P, 2, NB])
        Gs = sb("Gs", [P, 2, 3, NB], BF16)
        Gr = sb("Gr", [P, 2, 2, NB])
        Gq = sb("Gq", [P, 2, NB])
        Gq1 = sb("Gq1", [P, NB])
        rs = sb("rs", [P, NB])
        pre = sb("pre", [P, 6, NB])
        e48 = sb("e48", [P, 6, NB])
        r48 = sb("r48", [P, 6, NB])
        Cs = sb("Cs", [P, 3, NB], BF16)
        Cr = sb("Cr", [P, 2, NB])
        CB = sb("CB", [P, Q, NB])
        prod = sb("prod", [P, 2, Q + 1, NB])
        small = {k: sb(k, [P, 2, NB]) for k in ("w", "wa", "wm", "dt", "dA", "dta", "dtz", "dtzx", "R")}
        zz, zzd = sb("zz", [P, 2, 2, NB]), sb("zzd", [P, 2, 2, NB])
        gt = sb("gt", [P, 2, NB, 6])
        pinc = sb("pinc", [P, 6, Q, NB])
        zc = sb("zc", [P, 2, Q, NB])
        zdc = sb("zdc", [P, 2, Q, NB])
        yc = sb("yc", [P, 2, Q, NB])
        bT = sb("bT", [P, P])
        wT = sb("wT", [P, NB, 2, P])
        Psel = sb("Psel", [P, 4, NB])
        pd = sb("pd", [P, NB, 4])

        with stage(nc, "loaded", "w_scaled", "split", "cast", "bias_mm", "bias_sum", "prep", "expd") as (block, s):
            loads = [(w_in[:, :, :], A["w_in"]), (w_r[:, :, :], A["w_r"]), (w_out[:, :, :], A["w_out"]),
                     (conv_w[:, :, :], A["conv_w"]), (conv_b[:, :], A["conv_b"]), (vec[:, :], A["vec"]),
                     (cent[:, :], A["cent"]), (ln_g[:, :], A["ln_g"]), (ln_b[:, :], A["ln_b"]),
                     (b1[:, :, :], A["b1"]), (b2[:, :], A["b2"]), (w1[:, :, :], A["w1"]), (w2[:, :, :, :], A["w2"]),
                     (rank[:, :, :], A["rank"]), (sel_e[:, :, :], A["sel_e"]), (bmask[:, :], A["bmask"]),
                     (hsel[:, :], A["hsel"])]
            n_loads = 16 * len(loads)

            @block.sync
            def _(sp):
                for dst, src in loads:
                    sp.dma_start(dst, src).then_inc(s["loaded"], 16)

            @block.gpsimd
            def _(pool):
                pool.memset(raw[:, :, 0:3 * NB], 0.0)
                pool.memset(zs[:, :, CH:], 0.0)
                pool.memset(pin[:, :, CH:], 0.0)
                pool.memset(S[:, :, :, :], 0.0)
                pool.memset(Ss[:, :, :, :, :], 0.0)
                pool.memset(Gs[:, :, :, :], 0.0)
                pool.memset(zero16[:, :], 0.0)
                pool.memset(rs[:, :], 0.0).then_inc(s["prep"], 1)

            @block.scalar
            def _(act):
                act.wait_ge(s["loaded"], n_loads)
                act.activation(a_col[:, :], vec[:, 2:4], ACT.Exp).then_inc(s["expd"], 1)

            @block.vector
            def _(dve):
                dve.wait_ge(s["loaded"], n_loads)
                dve.wait_ge(s["prep"], 1)
                dve.wait_ge(s["expd"], 1)
                for h in range(2):
                    z8 = zero16[:, 0:NB]
                    dve.tensor_scalar(dtb[:, h, :], z8, vec[:, h:h + 1], None, ALU.add)
                    dve.tensor_scalar(a_b[:, h, :], z8, a_col[:, h:h + 1], -1.0, ALU.add, ALU.mult)
                    dve.tensor_scalar(d_b[:, h, :], z8, vec[:, 4 + h:5 + h], None, ALU.add)
                    dve.tensor_scalar(w_r[:, h, :], w_r[:, h, :], vec[:, 6 + h:7 + h], None, ALU.mult)
                    dve.tensor_scalar(w_out[:, h, :], w_out[:, h, :], vec[:, 6 + h:7 + h], None, ALU.mult).then_inc(s["w_scaled"], 1)
                dve.wait_ge(s["w_scaled"], 2)
                dve.tensor_copy(w_rs[:, :, 0, :], w_r[:, :, :]).then_inc(s["split"], 1)
                dve.wait_ge(s["split"], 1)
                dve.tensor_tensor(w_res, w_r[:, :, :], w_rs[:, :, 0, :], ALU.subtract).then_inc(s["split"], 1)
                dve.wait_ge(s["split"], 2)
                dve.tensor_copy(w_rs[:, :, 1, :], w_res).then_inc(s["split"], 1)
                dve.wait_ge(s["split"], 3)
                dve.tensor_tensor(w_rs[:, :, 2, :], w_res, w_rs[:, :, 1, :], ALU.subtract).then_inc(s["split"], 1)
                dve.wait_ge(s["bias_mm"], 1)
                dve.tensor_tensor(b1[:, :, :], b1[:, :, :], ps[0][:, 0:NE * FT].rearrange("p (e f) -> p e f", e=NE), ALU.add)
                for e in range(NE):
                    dve.tensor_scalar(w1[:, e, :], w1[:, e, :], ln_g[:, e:e + 1], None, ALU.mult)

            @block.tensor
            def _(pe):
                pe.wait_ge(s["loaded"], n_loads)
                for e in range(NE):
                    for f in range(FT):
                        last = pe.matmul(ps[0][:, e * FT + f:e * FT + f + 1], w1[:, e, f * P:(f + 1) * P], ln_b[:, e:e + 1],
                                         start=True, stop=True)
                last.then_inc(s["bias_mm"], 1)

        with nc.Fori(0, NBLK) as blk:
            with stage(nc, "x_loaded") as (block, s):
                @block.sync
                def _(sp):
                    sp.dma_start(x0[:, :], A["x0"][:, bass.ts(blk, CH)]).then_inc(s["x_loaded"], 16)
                    sp.wait_ge(s["x_loaded"], 16)
            layernorm_stage(nc, mem, x0, xn, [slice(0, CH)])
            layernorm_stage(nc, mem, xn, xh, [slice(0, CH)])

            with stage(nc, "projected", "moved", "ez", "z1", "z2", "z_out", "conv") as (block, s):
                @block.tensor
                def _(pe):
                    for m in range(8):
                        pe.matmul(ps[m][:, 0:CH], w_in[:, m, :], xn[:, :], start=True, stop=True).then_inc(s["projected"], 1)

                @block.scalar
                def _(act):
                    for m in range(2):
                        act.wait_ge(s["projected"], m + 1)
                        act.activation(zs[:, m, 0:CH], ps[m][:, 0:CH], ACT.Exp, scale=-1.0).then_inc(s["ez"], 1)
                    for m in range(2, 6):
                        act.wait_ge(s["projected"], m + 1)
                        act.activation(raw[:, m - 2, 3 * NB:], ps[m][:, 0:CH], ACT.Copy).then_inc(s["moved"], 1)
                    for m in range(6, 8):
                        act.wait_ge(s["projected"], m + 1)
                        act.activation(pin[:, m - 2, 0:CH], ps[m][:, 0:CH], ACT.Copy)

                @block.vector
                def _(dve):
                    for m in range(2):
                        dve.wait_ge(s["ez"], m + 1)
                        dve.tensor_scalar(zs[:, m, 0:CH], zs[:, m, 0:CH], 1.0, None, ALU.add).then_inc(s["z1"], 1)
                    for m in range(2):
                        dve.wait_ge(s["z1"], m + 1)
                        dve.reciprocal(zs[:, m, 0:CH], zs[:, m, 0:CH]).then_inc(s["z2"], 1)
                    for m in range(2):
                        dve.wait_ge(s["z2"], m + 1)
                        dve.tensor_tensor(zs[:, m, 0:CH], ps[m][:, 0:CH], zs[:, m, 0:CH], ALU.mult)
                    n = 0
                    for m in range(4):
                        dve.wait_ge(s["moved"], m + 1)
                        dve.tensor_scalar(pin[:, m, 0:CH], raw[:, m, 0:CH], conv_w[:, m, 0:1], conv_b[:, m:m + 1],
                                          ALU.mult, ALU.add).then_inc(s["conv"], 1)
                        n += 1
                        for k in range(1, 4):
                            dve.wait_ge(s["conv"], n)
                            dve.scalar_tensor_tensor(pin[:, m, 0:CH], raw[:, m, k * NB:k * NB + CH], conv_w[:, m, k:k + 1],
                                                     pin[:, m, 0:CH], ALU.mult, ALU.add).then_inc(s["conv"], 1)
                            n += 1
                    dve.wait_ge(s["conv"], n)
                    dve.tensor_copy(raw[:, :, 0:3 * NB], raw[:, :, CH:CH + 3 * NB])

            with stage(nc, "aff_mm", "ea_done", "a1", "a2", "mx", "eq", "k2", "oh", "coef_done", "ct_mm", "ct_done",
                       "c_mm", "cb_done", "up_mm", "h_done", "down_mm", "t_done", "acc_done") as (block, s):
                @block.tensor
                def _(pe):
                    for t in range(4):
                        last = pe.matmul(ps[0][:, t * NE:(t + 1) * NE], xn[:, t * P:(t + 1) * P], cent[:, :], start=True, stop=True)
                    last.then_inc(s["aff_mm"], 1)
                    up = 0

                    def ups(e):
                        nonlocal up
                        for f in range(FT):
                            if up >= 3:
                                pe.wait_ge(s["h_done"], up - 2)
                            pe.matmul(ps[3 + up % 3][:, 0:CH], w1[:, e, f * P:(f + 1) * P], xh[:, :], start=True, stop=True).then_inc(s["up_mm"], 1)
                            up += 1

                    ups(0)
                    pe.wait_ge(s["coef_done"], 1)
                    for t in range(4):
                        last = pe.transpose(ps[7][0:NE, t * P:(t + 1) * P], coef[:, t, :], mem["ident"][:, :])
                    last.then_inc(s["ct_mm"], 1)
                    pe.wait_ge(s["ct_done"], 1)
                    for e in range(NE):
                        if e >= 2:
                            pe.wait_ge(s["cb_done"], e - 1)
                        pe.matmul(ps[1 + e % 2][:, 0:CH], sel_e[:, e, :], coefT[:, :], start=True, stop=True).then_inc(s["c_mm"], 1)
                        if e + 1 < NE:
                            ups(e + 1)
                        if e >= 2:
                            pe.wait_ge(s["t_done"], e - 1)
                        for f in range(FT):
                            pe.wait_ge(s["h_done"], e * FT + f + 1)
                            last = pe.matmul(ps[6 + e % 2][:, 0:CH], w2[:, e, f, :], hb[:, e % 2, f, :], start=(f == 0), stop=(f == FT - 1))
                        last.then_inc(s["down_mm"], 1)

                @block.scalar
                def _(act):
                    act.wait_ge(s["a1"], 1)
                    act.activation(ea[:, :, :], aff[:, :, :], ACT.Exp, scale=-1.0).then_inc(s["ea_done"], 1)

                    def relus(e):
                        for f in range(FT):
                            n = e * FT + f
                            act.wait_ge(s["up_mm"], n + 1)
                            if e >= 2:
                                act.wait_ge(s["down_mm"], e - 1)
                            act.activation(hb[:, e % 2, f, :], ps[3 + n % 3][:, 0:CH], ACT.Relu, bias=b1[:, e, f:f + 1]).then_inc(s["h_done"], 1)

                    relus(0)
                    for e in range(NE):
                        act.wait_ge(s["c_mm"], e + 1)
                        if e >= 2:
                            act.wait_ge(s["t_done"], e - 1)
                        act.activation(cb[:, e % 2, :], ps[1 + e % 2][:, 0:CH], ACT.Copy).then_inc(s["cb_done"], 1)
                        if e + 1 < NE:
                            relus(e + 1)

                @block.vector
                def _(dve):
                    dve.wait_ge(s["aff_mm"], 1)
                    dve.tensor_copy(aff[:, :, :], ps[0][:, 0:4 * NE].rearrange("p (t e) -> p t e", t=4)).then_inc(s["a1"], 1)
                    dve.wait_ge(s["ea_done"], 1)
                    dve.tensor_scalar(ea[:, :, :], ea[:, :, :], 1.0, None, ALU.add).then_inc(s["a2"], 1)
                    dve.wait_ge(s["a1"], 1)
                    dve.tensor_reduce(affx[:, :], aff[:, :, :], AX.X, ALU.max).then_inc(s["mx"], 1)
                    dve.wait_ge(s["mx"], 1)
                    dve.tensor_tensor(key[:, :, :], aff[:, :, :], affx[:, :, None].to_broadcast([P, 4, NE]), ALU.is_equal).then_inc(s["eq"], 1)
                    dve.wait_ge(s["a2"], 1)
                    dve.reciprocal(ea[:, :, :], ea[:, :, :]).then_inc(s["a2"], 1)
                    dve.wait_ge(s["eq"], 1)
                    dve.tensor_tensor(key[:, :, :], key[:, :, :], rank[:, :, :], ALU.mult).then_inc(s["k2"], 1)
                    dve.wait_ge(s["k2"], 1)
                    dve.tensor_reduce(affx[:, :], key[:, :, :], AX.X, ALU.max).then_inc(s["k2"], 1)
                    dve.wait_ge(s["k2"], 2)
                    dve.tensor_tensor(key[:, :, :], key[:, :, :], affx[:, :, None].to_broadcast([P, 4, NE]), ALU.is_equal).then_inc(s["oh"], 1)
                    dve.wait_ge(s["oh"], 1)
                    dve.wait_ge(s["a2"], 2)
                    dve.tensor_tensor(coef[:, :, :], key[:, :, :], ea[:, :, :], ALU.mult).then_inc(s["coef_done"], 1)
                    dve.wait_ge(s["ct_mm"], 1)
                    dve.tensor_copy(coefT[:, :], ps[7][0:NE, 0:CH]).then_inc(s["ct_done"], 1)
                    for e in range(NE):
                        dve.wait_ge(s["down_mm"], e + 1)
                        dve.wait_ge(s["cb_done"], e + 1)
                        if e >= 2:
                            dve.wait_ge(s["acc_done"], e - 1)
                        dve.scalar_tensor_tensor(tmp[:, e % 2, :], ps[6 + e % 2][:, 0:CH], b2[:, e:e + 1], cb[:, e % 2, :],
                                                 ALU.add, ALU.mult).then_inc(s["t_done"], 1)

                @block.gpsimd
                def _(pool):
                    for e in range(NE):
                        pool.wait_ge(s["t_done"], e + 1)
                        if e:
                            pool.wait_ge(s["acc_done"], e)
                        pool.tensor_tensor(gff[:, :], xn[:, :] if e == 0 else gff[:, :], tmp[:, e % 2, :], ALU.add).then_inc(s["acc_done"], 1)

            silu_stage(nc, gff, sg, gff)

            with stage(nc) as (block, s):
                @block.gpsimd
                def _(pool):
                    chunk_z(zs, zc, 0)(pool)

                @block.scalar
                def _(act):
                    chunk_pre(pin, pinc, 0)(act)

                @block.vector
                def _(dve):
                    chunk_zd(zs, d_b, zdc, 0)(dve)

            with nc.Fori(0, NCH) as chunk:
                scan_chunk(nc, mem, dict(w_rs=w_rs, S=S, Ss=Ss, Sr=Sr, V=V, Wh=Wh, Pc=Pc, G=G, Gs=Gs, Gr=Gr, Gq=Gq,
                                         rs=rs, pre=pre, e48=e48, r48=r48, Cs=Cs, Cr=Cr, CB=CB, prod=prod, gt=gt,
                                         bT=bT, wT=wT, Psel=Psel, zs=zs, pin=pin, pd=pd, pinc=pinc, zc=zc, zdc=zdc, yc=yc, a_b=a_b, zz=zz, zzd=zzd, Gq1=Gq1,
                                         dtb=dtb, d_b=d_b, bmask=bmask, hsel=hsel, **small), yb, chunk)

            with stage(nc, "out_mm", "gated") as (block, s):
                @block.tensor
                def _(pe):
                    for h in range(2):
                        last = pe.matmul(ps[0][:, 0:CH], w_out[:, h, :], yb[:, h, :], start=(h == 0), stop=(h == 1))
                    last.then_inc(s["out_mm"], 1)

                @block.vector
                def _(dve):
                    dve.wait_ge(s["out_mm"], 1)
                    dve.tensor_tensor(gff[:, :], ps[0][:, 0:CH], gff[:, :], ALU.mult).then_inc(s["gated"], 1)
                    dve.wait_ge(s["gated"], 1)
                    v = lambda a: a[:, :].rearrange("p (t b) -> p b t", b=NB)
                    dve.tensor_tensor(x1[:, :].rearrange("p (b t) -> p b t", b=NB)[:, :, bass.ts(blk, TB)], v(gff), v(x0), ALU.add)


def silu_stage(nc, src, work, dst):
    with stage(nc, "e_done", "d_done", "r_done") as (block, s):
        @block.scalar
        def _(act):
            act.activation(work[:, :], src[:, :], ACT.Exp, scale=-1.0).then_inc(s["e_done"], 1)

        @block.vector
        def _(dve):
            dve.wait_ge(s["e_done"], 1)
            dve.tensor_scalar(work[:, :], work[:, :], 1.0, None, ALU.add).then_inc(s["d_done"], 1)
            dve.wait_ge(s["d_done"], 1)
            dve.reciprocal(work[:, :], work[:, :]).then_inc(s["r_done"], 1)
            dve.wait_ge(s["r_done"], 1)
            dve.tensor_tensor(dst[:, :], src[:, :], work[:, :], ALU.mult)


def chunk_columns(chunk):
    return bass.ds(chunk * (Q * NB), Q * NB)


def chunk_z(zs, zc, chunk):
    return lambda pool: pool.tensor_copy(zc[:, :, :, :].rearrange("p m t b -> p m (t b)"), zs[:, :, chunk_columns(chunk)])


def chunk_zd(zs, d_b, zdc, chunk):
    return lambda dve: dve.tensor_tensor(zdc[:, :, :, :], zs[:, :, chunk_columns(chunk)].rearrange("p m (t b) -> p m t b", b=NB),
                                         d_b[:, :, None, :].to_broadcast([P, 2, Q, NB]), ALU.mult)


def chunk_pre(pin, pinc, chunk):
    return lambda act: act.activation(pinc[:, :, :, :].rearrange("p m t b -> p m (t b)"), pin[:, :, chunk_columns(chunk)], ACT.Copy)


def scan_chunk(nc, mem, m, yb, chunk):
    load_chunk_z = chunk_z(m["zs"], m["zc"], chunk + 1)
    load_chunk_pre = chunk_pre(m["pin"], m["pinc"], chunk + 1)
    load_chunk_zd = chunk_zd(m["zs"], m["d_b"], m["zdc"], chunk + 1)
    ps, ones = mem["ps"], mem["ones"]
    Ss, Gs, V, Wh, Pc, G = m["Ss"], m["Gs"], m["V"], m["Wh"], m["Pc"], m["G"]
    pre, e48, r48, rs, pinc, zc, yc = m["pre"], m["e48"], m["r48"], m["rs"], m["pinc"], m["zc"], m["yc"]
    C_T, B_T, X_T, D_T = 0, 1, slice(2, 4), slice(4, 6)
    CB_T = slice(0, 2)
    w_bank, x_bank, u_bank, dot_bank, ms_bank, d_bank = ps[0], ps[1], ps[2], ps[3], ps[4], ps[5]

    with stage(nc, "sq_each", "sq_done", "g_split", "wcb_mm", "wd_mm", "wx_mm", "ms_mm", "lnms", "rs_done", "cb_sum", "cb_mul",
               "cb_pre", "cb_exp", "cb_one", "cb_rec", "c_ready", "c_rest", "c_split", "d_sum", "d_mul", "d_pre", "d_exp",
               "d_one", "d_rec", "d_act", "x_sum", "x_mul", "x_pre", "x_exp", "x_one", "x_rec", "x_act", "cb_prod", "dots_mm",
               "u_mm", "w_done", "wabs", "wexp", "dt_parts", "dt_done", "dta", "da_done", "dtz", "dtzx", "dx",
               "zz_done", "past_in", "hist", "prod", "g_terms", "g_done", "g_high", "g_rest", "yn_done") as (block, s):

        @block.tensor
        def _(pe):
            def mean_square(n):
                pe.wait_ge(s["sq_done"], n)
                pe.matmul(ms_bank[:, 0:NB], ones[:, :], m["Gq1"][:, :], start=True, stop=True).then_inc(s["ms_mm"], 1)

            def recurrent(bank, tiles, sem):
                for n, j in enumerate(tiles):
                    for part in range(3):
                        for h in range(2):
                            last = pe.matmul(bank[:, n * 24:(n + 1) * 24], m["w_rs"][:, h, part, j * P:(j + 1) * P],
                                             Gs[:, h, :, :].rearrange("p c b -> p (c b)"),
                                             start=(part == 0 and h == 0), stop=(part == 2 and h == 1))
                last.then_inc(sem, 1)

            def state(batches):
                for b in batches:
                    for h in range(2):
                        for part in range(3):
                            last = pe.matmul(u_bank[:, (h * NB + b) * 3:(h * NB + b) * 3 + 3], Ss[:, part, b, h, :],
                                             m["Cs"][:, :, b], start=(part == 0), stop=(part == 2))
                return last

            for t in range(Q):
                if t >= 1:
                    mean_square(t)
                    pe.wait_ge(s["g_split"], t)
                recurrent(w_bank, (0, 1), s["wcb_mm"])
                recurrent(d_bank, (4, 5), s["wd_mm"])
                recurrent(x_bank, (2, 3), s["wx_mm"])
                pe.wait_ge(s["c_split"], t + 1)
                state(range(2))
                pe.wait_ge(s["cb_prod"], t + 1)
                pe.matmul(dot_bank[:, 0:(t + 1) * NB], ones[:, :], m["CB"][:, 0:t + 1, :].rearrange("p s b -> p (s b)"),
                          start=True, stop=True).then_inc(s["dots_mm"], 1)
                state(range(2, NB)).then_inc(s["u_mm"], 1)
            mean_square(Q)

        @block.scalar
        def _(act):
            def rstd(n):
                act.wait_ge(s["g_done"], n)
                act.activation(m["Gq"][:, :, :], G[:, :, :], ACT.Square).then_inc(s["sq_each"], 1)
                act.wait_ge(s["ms_mm"], n)
                act.activation(rs[:, :], ms_bank[:, 0:NB], ACT.Ln, bias=mem["eps"][:, 0:1], scale=1.0 / (2 * P)).then_inc(s["lnms"], 1)
                act.wait_ge(s["lnms"], n)
                act.activation(rs[:, :], rs[:, :], ACT.Exp, scale=-0.5).then_inc(s["rs_done"], 1)

            wa = m["wa"]
            for t in range(Q):
                if t >= 1:
                    rstd(t)
                act.wait_ge(s["cb_pre"], t + 1)
                act.activation(e48[:, CB_T, :], pre[:, CB_T, :], ACT.Exp, scale=-1.0).then_inc(s["cb_exp"], 1)
                act.wait_ge(s["d_pre"], t + 1)
                act.activation(e48[:, D_T, :], pre[:, D_T, :], ACT.Exp, scale=-1.0).then_inc(s["d_exp"], 1)
                act.wait_ge(s["w_done"], t + 1)
                act.activation(wa[:, :, :], m["w"][:, :, :], ACT.Abs).then_inc(s["wabs"], 1)
                act.activation(m["wm"][:, :, :], m["w"][:, :, :], ACT.Relu).then_inc(s["dt_parts"], 1)
                act.wait_ge(s["wabs"], t + 1)
                act.activation(wa[:, :, :], wa[:, :, :], ACT.Exp, scale=-1.0).then_inc(s["wexp"], 1)
                act.wait_ge(s["x_pre"], t + 1)
                act.activation(e48[:, X_T, :], pre[:, X_T, :], ACT.Exp, scale=-1.0).then_inc(s["x_exp"], 1)
                act.wait_ge(s["wexp"], t + 1)
                act.activation(wa[:, :, :], wa[:, :, :], ACT.Ln, bias=1.0).then_inc(s["dt_parts"], 1)
                act.wait_ge(s["dta"], t + 1)
                act.activation(m["dA"][:, :, :], m["dta"][:, :, :], ACT.Exp).then_inc(s["da_done"], 1)
            rstd(Q)

        @block.gpsimd
        def _(pool):
            dt, dA, dtz, dtzx, zz = (m[k] for k in ("dt", "dA", "dtz", "dtzx", "zz"))
            for t in range(Q):
                if t >= 1:
                    pool.wait_ge(s["past_in"], 2 * t)
                pool.tensor_copy(zz[:, 0, :, :], zc[:, :, t, :])
                if t >= 1:
                    pool.wait_ge(s["hist"], t)
                    pool.tensor_tensor(zz[:, 1, :, :], zc[:, :, t, :], Pc[:, :, :], ALU.mult).then_inc(s["zz_done"], 1)
                else:
                    pool.tensor_copy(zz[:, 1, :, :], zc[:, :, t, :]).then_inc(s["zz_done"], 1)
                pool.wait_ge(s["dt_done"], t + 1)
                pool.tensor_tensor(dtz[:, :, :], dt[:, :, :], zc[:, :, t, :], ALU.mult).then_inc(s["dtz"], 1)
                pool.wait_ge(s["dtz"], t + 1)
                pool.wait_ge(s["x_act"], t + 1)
                pool.tensor_tensor(dtzx[:, :, :], V[:, X_T, t, :], dtz[:, :, :], ALU.mult).then_inc(s["dtzx"], 1)
                pool.tensor_tensor(m["gt"][:, :, :, 5], V[:, X_T, t, :], m["zdc"][:, :, t, :], ALU.mult).then_inc(s["g_terms"], 1)
                pool.tensor_tensor(Wh[:, :, t, :], dt[:, :, :], V[:, X_T, t, :], ALU.mult).then_inc(s["dx"], 1)
                pool.wait_ge(s["da_done"], t + 1)
                if t >= 1:
                    pool.tensor_tensor(Pc[:, :, :], Pc[:, :, :], dA[:, :, :], ALU.mult)
                    pool.wait_ge(s["prod"], t)
                    pool.tensor_tensor(Wh[:, :, 0:t, :], Wh[:, :, 0:t, :], dA[:, :, :][:, :, None, :].to_broadcast([P, 2, t, NB]),
                                       ALU.mult).then_inc(s["hist"], 1)
                else:
                    pool.tensor_copy(Pc[:, :, :], dA[:, :, :]).then_inc(s["hist"], 1)

        @block.vector
        def _(dve):
            Cs, Cr, CB = m["Cs"], m["Cr"], m["CB"]
            gt, Gr = m["gt"], m["Gr"]
            W2 = [P, 2, NB]
            rsb = rs[:, None, :].to_broadcast(W2)

            def summed(bank, out):
                return dve.tensor_reduce(out, bank[:, 0:48].rearrange("p (m c b) -> p m b c", m=2, c=3), AX.X, ALU.add)

            for t in range(Q):
                dve.wait_ge(s["wcb_mm"], t + 1)
                summed(w_bank, pre[:, CB_T, :]).then_inc(s["cb_sum"], 1)
                if t >= 1:
                    dve.wait_ge(s["rs_done"], t)
                dve.wait_ge(s["cb_sum"], t + 1)
                dve.tensor_tensor(pre[:, CB_T, :], pre[:, CB_T, :], rsb, ALU.mult).then_inc(s["cb_mul"], 1)
                dve.wait_ge(s["wd_mm"], t + 1)
                summed(d_bank, pre[:, D_T, :]).then_inc(s["d_sum"], 1)
                dve.wait_ge(s["cb_mul"], t + 1)
                dve.tensor_tensor(pre[:, CB_T, :], pre[:, CB_T, :], pinc[:, CB_T, t, :], ALU.add).then_inc(s["cb_pre"], 1)
                dve.wait_ge(s["d_sum"], t + 1)
                dve.tensor_tensor(pre[:, D_T, :], pre[:, D_T, :], rsb, ALU.mult).then_inc(s["d_mul"], 1)
                if t >= 1:
                    dve.tensor_tensor(yc[:, :, t - 1, :], G[:, :, :], rsb, ALU.mult).then_inc(s["yn_done"], 1)
                dve.wait_ge(s["d_mul"], t + 1)
                dve.tensor_tensor(pre[:, D_T, :], pre[:, D_T, :], pinc[:, D_T, t, :], ALU.add).then_inc(s["d_pre"], 1)
                dve.wait_ge(s["cb_exp"], t + 1)
                dve.tensor_scalar(r48[:, CB_T, :], e48[:, CB_T, :], 1.0, None, ALU.add).then_inc(s["cb_one"], 1)
                dve.wait_ge(s["wx_mm"], t + 1)
                summed(x_bank, pre[:, X_T, :]).then_inc(s["x_sum"], 1)
                dve.wait_ge(s["cb_one"], t + 1)
                dve.reciprocal(r48[:, CB_T, :], r48[:, CB_T, :]).then_inc(s["cb_rec"], 1)
                dve.wait_ge(s["d_exp"], t + 1)
                dve.tensor_scalar(r48[:, D_T, :], e48[:, D_T, :], 1.0, None, ALU.add).then_inc(s["d_one"], 1)
                dve.wait_ge(s["cb_rec"], t + 1)
                dve.tensor_tensor(Cs[:, 0, :], pre[:, C_T, :], r48[:, C_T, :], ALU.mult).then_inc(s["c_ready"], 1)
                dve.tensor_tensor(V[:, CB_T, t, :], pre[:, CB_T, :], r48[:, CB_T, :], ALU.mult).then_inc(s["c_ready"], 1)
                dve.wait_ge(s["d_one"], t + 1)
                dve.reciprocal(r48[:, D_T, :], r48[:, D_T, :]).then_inc(s["d_rec"], 1)
                dve.wait_ge(s["c_ready"], 2 * t + 2)
                dve.tensor_tensor(Cs[:, 1, :], V[:, C_T, t, :], Cs[:, 0, :], ALU.subtract).then_inc(s["c_rest"], 1)
                dve.tensor_tensor(Cr[:, 0, :], V[:, C_T, t, :], Cs[:, 0, :], ALU.subtract).then_inc(s["c_rest"], 1)
                dve.wait_ge(s["d_rec"], t + 1)
                dve.tensor_tensor(V[:, D_T, t, :], pre[:, D_T, :], r48[:, D_T, :], ALU.mult).then_inc(s["d_act"], 1)
                dve.wait_ge(s["c_rest"], 2 * t + 2)
                dve.tensor_tensor(Cs[:, 2, :], Cr[:, 0, :], Cs[:, 1, :], ALU.subtract).then_inc(s["c_split"], 1)
                dve.wait_ge(s["d_act"], t + 1)
                dve.tensor_tensor(m["w"][:, :, :], V[:, D_T, t, :], m["dtb"][:, :, :], ALU.add).then_inc(s["w_done"], 1)
                dve.tensor_tensor(CB[:, 0:t + 1, :], V[:, B_T, 0:t + 1, :], V[:, C_T, t, :][:, None, :].to_broadcast([P, t + 1, NB]),
                                  ALU.mult).then_inc(s["cb_prod"], 1)
                dve.wait_ge(s["zz_done"], t + 1)
                dve.wait_ge(s["x_sum"], t + 1)
                dve.tensor_tensor(pre[:, X_T, :], pre[:, X_T, :], rsb, ALU.mult).then_inc(s["x_mul"], 1)
                dve.wait_ge(s["x_mul"], t + 1)
                dve.tensor_tensor(pre[:, X_T, :], pre[:, X_T, :], pinc[:, X_T, t, :], ALU.add).then_inc(s["x_pre"], 1)
                dve.wait_ge(s["x_exp"], t + 1)
                dve.tensor_scalar(r48[:, X_T, :], e48[:, X_T, :], 1.0, None, ALU.add).then_inc(s["x_one"], 1)
                dve.wait_ge(s["dt_parts"], 2 * t + 2)
                dve.tensor_tensor(m["dt"][:, :, :], m["wm"][:, :, :], m["wa"][:, :, :], ALU.add).then_inc(s["dt_done"], 1)
                dve.wait_ge(s["x_one"], t + 1)
                dve.reciprocal(r48[:, X_T, :], r48[:, X_T, :]).then_inc(s["x_rec"], 1)
                dve.wait_ge(s["dt_done"], t + 1)
                dve.tensor_tensor(m["dta"][:, :, :], m["dt"][:, :, :], m["a_b"][:, :, :], ALU.mult).then_inc(s["dta"], 1)
                dve.wait_ge(s["x_rec"], t + 1)
                dve.tensor_tensor(V[:, X_T, t, :], pre[:, X_T, :], r48[:, X_T, :], ALU.mult).then_inc(s["x_act"], 1)
                dve.wait_ge(s["dots_mm"], t + 1)
                if t >= 1:
                    dve.tensor_tensor(m["prod"][:, :, 0:t, :], Wh[:, :, 0:t, :],
                                      dot_bank[:, 0:t * NB].rearrange("p (s b) -> p s b", b=NB)[:, None, :, :].to_broadcast([P, 2, t, NB]),
                                      ALU.mult).then_inc(s["prod"], 1)
                dve.wait_ge(s["da_done"], t + 1)
                dve.tensor_tensor(m["zzd"][:, :, :, :], m["zz"][:, :, :, :], m["dA"][:, None, :, :].to_broadcast([P, 2, 2, NB]), ALU.mult).then_inc(s["past_in"], 1)
                if t >= 1:
                    dve.wait_ge(s["prod"], t)
                    dve.tensor_reduce(m["R"][:, :, :], m["prod"][:, :, 0:t, :].rearrange("p h s b -> p h b s"), AX.X, ALU.add).then_inc(s["past_in"], 1)
                else:
                    dve.memset(m["R"][:, :, :], 0.0).then_inc(s["past_in"], 1)
                dve.wait_ge(s["dtzx"], t + 1)
                dve.tensor_tensor(gt[:, :, :, 4], m["dtzx"][:, :, :], dot_bank[:, t * NB:(t + 1) * NB][:, None, :].to_broadcast(W2),
                                  ALU.mult).then_inc(s["g_terms"], 1)
                dve.wait_ge(s["past_in"], 2 * t + 2)
                dve.tensor_tensor(gt[:, :, :, 3], m["R"][:, :, :], m["zzd"][:, 0, :, :], ALU.mult).then_inc(s["g_terms"], 1)
                dve.wait_ge(s["u_mm"], t + 1)
                dve.tensor_tensor(gt[:, :, :, 0:3], u_bank[:, 0:48].rearrange("p (h b c) -> p h b c", h=2, b=NB),
                                  m["zzd"][:, 1, :, :][:, :, :, None].to_broadcast([P, 2, NB, 3]), ALU.mult).then_inc(s["g_terms"], 1)
                dve.wait_ge(s["g_terms"], 4 * t + 4)
                dve.tensor_reduce(G[:, :, :], gt[:, :, :, :], AX.X, ALU.add).then_inc(s["g_done"], 1)
                dve.wait_ge(s["g_done"], t + 1)
                dve.tensor_copy(Gs[:, :, 0, :], G[:, :, :]).then_inc(s["g_high"], 1)
                dve.wait_ge(s["sq_each"], t + 1)
                dve.tensor_tensor(m["Gq1"][:, :], m["Gq"][:, 0, :], m["Gq"][:, 1, :], ALU.add).then_inc(s["sq_done"], 1)
                dve.wait_ge(s["g_high"], t + 1)
                dve.tensor_tensor(Gs[:, :, 1, :], G[:, :, :], Gs[:, :, 0, :], ALU.subtract).then_inc(s["g_rest"], 1)
                dve.tensor_tensor(Gr[:, 0, :, :], G[:, :, :], Gs[:, :, 0, :], ALU.subtract).then_inc(s["g_rest"], 1)
                dve.wait_ge(s["g_rest"], 2 * t + 2)
                dve.tensor_tensor(Gs[:, :, 2, :], Gr[:, 0, :, :], Gs[:, :, 1, :], ALU.subtract).then_inc(s["g_split"], 1)
            dve.wait_ge(s["rs_done"], Q)
            dve.tensor_tensor(yc[:, :, Q - 1, :], G[:, :, :], rsb, ALU.mult).then_inc(s["yn_done"], 1)

    S, Sr, bT, wT, Psel, pd = m["S"], m["Sr"], m["bT"], m["wT"], m["Psel"], m["pd"]
    PAIRS = NB // 2
    VE_LAST = (2, 3)
    with stage(nc, "sel_done", "t_mm", "bT_done", "w0_done", "w1_done", "p_mm", "pd_done", "s_mul", "o_mm", "s_add", "sp1",
               "sp2", "sp3") as (block, s):
        @block.tensor
        def _(pe):
            pe.transpose(ps[0][:, 0:P], V[:, B_T, :, :].rearrange("p s b -> p (s b)"), mem["ident"][:, :])
            for h in range(2):
                last = pe.transpose(ps[1 + h][:, 0:P], Wh[:, h, :, :].rearrange("p s b -> p (s b)"), mem["ident"][:, :])
            last.then_inc(s["t_mm"], 1)
            pe.wait_ge(s["sel_done"], 1)
            pe.matmul(ps[3][:, 0:4 * NB], ones[:, :], Psel[:, :, :].rearrange("p h b -> p (h b)"), start=True, stop=True).then_inc(s["p_mm"], 1)
            pe.wait_ge(s["bT_done"], 1)
            for k in range(PAIRS):
                pe.wait_ge(s["w0_done"], 2 * k + 2)
                pe.wait_ge(s["w1_done"], k + 1)
                pe.matmul(ps[4 + k][:, :], bT[:, :], wT[:, 2 * k:2 * k + 2, :, :].rearrange("p b h f -> p (b h f)"), start=True, stop=True).then_inc(s["o_mm"], 1)

        @block.gpsimd
        def _(pool):
            load_chunk_z(pool)
            for k in range(PAIRS):
                sl = slice(2 * k, 2 * k + 2)
                if k == 0:
                    pool.wait_ge(s["pd_done"], 1)
                pool.tensor_tensor(S[:, sl, :, :].rearrange("p b h (k j) -> p b (h k) j", k=2),
                                   S[:, sl, :, :].rearrange("p b h (k j) -> p b (h k) j", k=2),
                                   pd[:, sl, :, None].to_broadcast([P, 2, 4, 64]), ALU.mult).then_inc(s["s_mul"], 1)
            for k in range(PAIRS):
                if k in VE_LAST:
                    continue
                sl = slice(2 * k, 2 * k + 2)
                pool.wait_ge(s["sp3"], k + 1)
                pool.tensor_tensor(Ss[:, 2, sl, :, :], Sr[:, sl, :, :], Ss[:, 1, sl, :, :], ALU.subtract)
            pool.tensor_copy(yb[:, :, bass.ds(chunk * (Q * NB), Q * NB)], m["yc"][:, :, :, :].rearrange("p m t b -> p m (t b)"))

        @block.scalar
        def _(act):
            load_chunk_pre(act)
            act.wait_ge(s["t_mm"], 1)
            act.activation(bT[:, :], ps[0][:, 0:P], ACT.Copy).then_inc(s["bT_done"], 1)
            for b in range(NB):
                act.activation(wT[:, b, 0, :], ps[1][:, 0:P], ACT.Copy, scale=m["bmask"][:, b:b + 1]).then_inc(s["w0_done"], 1)

            def third_input(k):
                sl = slice(2 * k, 2 * k + 2)
                act.wait_ge(s["sp2"], k + 1)
                act.activation(Ss[:, 1, sl, :, :], Sr[:, sl, :, :], ACT.Copy).then_inc(s["sp3"], 1)

            for k in range(PAIRS):
                sl = slice(2 * k, 2 * k + 2)
                act.wait_ge(s["s_add"], k + 1)
                act.activation(Ss[:, 0, sl, :, :], S[:, sl, :, :], ACT.Copy).then_inc(s["sp1"], 1)
                if k:
                    third_input(k - 1)
            third_input(PAIRS - 1)

        @block.vector
        def _(dve):
            for hh in range(2):
                last = dve.tensor_scalar(Psel[:, hh::2, :], Pc[:, :, :], m["hsel"][:, hh:hh + 1], None, ALU.mult)
            last.then_inc(s["sel_done"], 1)
            load_chunk_zd(dve)
            dve.wait_ge(s["p_mm"], 1)
            dve.tensor_copy(pd[:, :, :], ps[3][:, 0:4 * NB].rearrange("p (h b) -> p b h", h=4)).then_inc(s["pd_done"], 1)
            for k in range(PAIRS):
                dve.tensor_tensor(wT[:, 2 * k:2 * k + 2, 1, :], ps[2][:, None, 0:P].to_broadcast([P, 2, P]),
                                  m["bmask"][:, 2 * k:2 * k + 2][:, :, None].to_broadcast([P, 2, P]), ALU.mult).then_inc(s["w1_done"], 1)

            def rest(k):
                sl = slice(2 * k, 2 * k + 2)
                dve.wait_ge(s["sp1"], k + 1)
                dve.tensor_tensor(Sr[:, sl, :, :], S[:, sl, :, :], Ss[:, 0, sl, :, :], ALU.subtract).then_inc(s["sp2"], 1)

            for k in range(PAIRS):
                sl = slice(2 * k, 2 * k + 2)
                dve.wait_ge(s["s_mul"], k + 1)
                dve.wait_ge(s["o_mm"], k + 1)
                dve.tensor_tensor(S[:, sl, :, :], S[:, sl, :, :], ps[4 + k][:, :].rearrange("p (b h f) -> p b h f", b=2, h=2), ALU.add).then_inc(s["s_add"], 1)
                if k:
                    rest(k - 1)
            rest(PAIRS - 1)
            for k in VE_LAST:
                sl = slice(2 * k, 2 * k + 2)
                dve.wait_ge(s["sp3"], k + 1)
                dve.tensor_tensor(Ss[:, 2, sl, :, :], Sr[:, sl, :, :], Ss[:, 1, sl, :, :], ALU.subtract)


def attention_memory(sb, group):
    return dict(sc=sb("sc", [P, 3, NT]), pr=sb("pr", [P, 3, NT]), PT=sb("PT", [P, 2, 4, NT]),
                nmax=sb("nmax", [P, 4 * group]), rsum=sb("rsum", [P, 4 * group]), rinv=sb("rinv", [P, 4 * group]))


def heads_stage(nc, mem, w, group, causal, qm, kT, vm, bias, scale_of, prepare, out_acc, first=None):
    ps = mem["ps"]
    sc, pr, PT, nmax, rsum, rinv = (w[k] for k in ("sc", "pr", "PT", "nmax", "rsum", "rinv"))
    n_tiles = 4 * group

    def width(i):
        return (i + 1) * P if causal else NT

    with stage(nc, "q_ready", "v_ready", "s_mm", "sc_done", "mx_done", "exp_done", "rc_done", "norm_done", "t_mm", "tc_done",
               "pv_done") as (block, s):
        @block.tensor
        def _(pe):
            def scores(n):
                h, i = divmod(n, 4)
                if i == 0:
                    pe.wait_ge(s["q_ready"], h + 1)
                if n >= 3:
                    pe.wait_ge(s["sc_done"], n - 2)
                pe.matmul(ps[n % 3][:, 0:width(i)], qm(h)[:, i * P:(i + 1) * P], kT[:, 0:width(i)],
                          start=True, stop=True).then_inc(s["s_mm"], 1)

            def transposes(n):
                i = n % 4
                pe.wait_ge(s["norm_done"], n + 1)
                if n >= 2:
                    pe.wait_ge(s["tc_done"], n - 1)
                for j in range(width(i) // P):
                    last = pe.transpose(ps[3 + n % 2][:, j * P:(j + 1) * P], pr[:, n % 3, j * P:(j + 1) * P], mem["ident"][:, :])
                last.then_inc(s["t_mm"], 1)

            def values(h):
                if h == 0:
                    pe.wait_ge(s["v_ready"], group)
                pe.wait_ge(s["tc_done"], 4 * h + 4)
                for j in range(4):
                    c = j * P if causal else 0
                    last = pe.matmul(ps[5][:, c:NT], vm(h)[:, j, :], PT[:, h % 2, j, c:NT], start=(h == 0 and j == 0),
                                     stop=(h == group - 1 and j == 3), skip_group_check=True)
                last.then_inc(s["pv_done"], 1)

            scores(0)
            scores(1)
            for n in range(n_tiles):
                if n + 2 < n_tiles:
                    scores(n + 2)
                transposes(n)
                if n % 4 == 1 and n >= 4:
                    values(n // 4 - 1)
            values(group - 1)

        @block.scalar
        def _(act):
            def copy_out(n):
                h, i = divmod(n, 4)
                act.wait_ge(s["t_mm"], n + 1)
                if h >= 2 and i == 0:
                    act.wait_ge(s["pv_done"], h - 1)
                k = width(i)
                act.activation(PT[:, h % 2, 0:k // P, i * P:(i + 1) * P], ps[3 + n % 2][:, 0:k].rearrange("p (j t) -> p j t", t=P),
                               ACT.Copy).then_inc(s["tc_done"], 1)

            for n in range(n_tiles + 1):
                if n < n_tiles:
                    k = width(n % 4)
                    act.wait_ge(s["mx_done"], n + 1)
                    if n >= 3:
                        act.wait_ge(s["t_mm"], n - 2)
                    act.activation(pr[:, n % 3, 0:k], sc[:, n % 3, 0:k], ACT.Exp, bias=nmax[:, n:n + 1],
                                   accum_out=rsum[:, n:n + 1]).then_inc(s["exp_done"], 1)
                if n >= 1:
                    copy_out(n - 1)

        @block.gpsimd
        def _(pool):
            prepare[1](pool, s["v_ready"])

        @block.vector
        def _(dve):
            prepare[0](dve, s["q_ready"])

            def normalise(n):
                k = width(n % 4)
                dve.wait_ge(s["exp_done"], n + 1)
                dve.reciprocal(rinv[:, n:n + 1], rsum[:, n:n + 1]).then_inc(s["rc_done"], 1)
                dve.wait_ge(s["rc_done"], n + 1)
                dve.tensor_scalar(pr[:, n % 3, 0:k], pr[:, n % 3, 0:k], rinv[:, n:n + 1], None, ALU.mult).then_inc(s["norm_done"], 1)

            for n in range(n_tiles + 1):
                if n < n_tiles:
                    h, i = divmod(n, 4)
                    k = width(i)
                    dve.wait_ge(s["s_mm"], n + 1)
                    if n >= 3:
                        dve.wait_ge(s["exp_done"], n - 2)
                    dve.scalar_tensor_tensor(sc[:, n % 3, 0:k], bias(h, i), scale_of(h, i), ps[n % 3][:, 0:k], ALU.mult,
                                             ALU.add).then_inc(s["sc_done"], 1)
                    dve.wait_ge(s["sc_done"], n + 1)
                    dve.tensor_reduce(nmax[:, n:n + 1], sc[:, n % 3, 0:k], AX.X, ALU.max, negate=True).then_inc(s["mx_done"], 1)
                if n >= 1:
                    normalise(n - 1)
            dve.wait_ge(s["pv_done"], group)
            if first is None:
                dve.tensor_tensor(out_acc, out_acc, ps[5][:, :], ALU.add)
            else:
                dve.tensor_copy(out_acc, ps[5][:, :])


def residual_stage(nc, mem, x, sat, f, e, gap=None):
    n = TOK // CH
    with stage(nc, "e_done", "d_done", "r_done", "g_done", "m_done", "x_done") as (block, s):
        @block.scalar
        def _(act):
            for k in range(n):
                if k >= 2:
                    act.wait_ge(s["x_done"], k - 1)
                act.activation(e[:, k % 2, :], f[:, k * CH:(k + 1) * CH], ACT.Exp, scale=-1.0).then_inc(s["e_done"], 1)

        @block.gpsimd
        def _(pool):
            for k in range(n):
                c = slice(k * CH, (k + 1) * CH)
                pool.tensor_tensor(sat[:, c], sat[:, c], f[:, c], ALU.mult).then_inc(s["m_done"], 1)

        @block.vector
        def _(dve):
            for k in range(n):
                c = slice(k * CH, (k + 1) * CH)
                dve.wait_ge(s["e_done"], k + 1)
                dve.tensor_scalar(e[:, k % 2, :], e[:, k % 2, :], 1.0, None, ALU.add).then_inc(s["d_done"], 1)
                dve.wait_ge(s["d_done"], k + 1)
                dve.reciprocal(e[:, k % 2, :], e[:, k % 2, :]).then_inc(s["r_done"], 1)
                dve.wait_ge(s["r_done"], k + 1)
                dve.wait_ge(s["m_done"], k + 1)
                dve.tensor_tensor(e[:, k % 2, :], e[:, k % 2, :], sat[:, c], ALU.mult).then_inc(s["g_done"], 1)
                dve.wait_ge(s["g_done"], k + 1)
                dve.tensor_tensor(x[:, c], x[:, c], e[:, k % 2, :], ALU.add).then_inc(s["x_done"], 1)


CHUNKS = [slice(k * CH, (k + 1) * CH) for k in range(TOK // CH)]


def layer1(nc, mem, A, x):
    ps = mem["ps"]
    with ExitStack() as ctx:
        def sb(name, shape, dt=F32):
            return ctx.enter_context(nc.sbuf_tensor("l1_" + name, shape, dt))

        xn, sat = sb("xn", [P, TOK]), sb("sat", [P, TOK])
        wq, wk, wv = sb("wq", [P, P]), sb("wk", [P, P]), sb("wv", [P, P])
        cmask = sb("cmask", [P, NT])
        cn_w1, cn_w2, cn_w3, cn_w4 = sb("cn_w1", [P, P]), sb("cn_w2", [P, 64]), sb("cn_w3", [64, 32]), sb("cn_w4", [32, P])
        gc_w1, gc_w2, gc_w3 = sb("gc_w1", [P, 64]), sb("gc_w2", [64, 32]), sb("gc_w3", [32, P])
        cvec = sb("cvec", [P, 8])
        half = sb("half", [P, 2])
        twist = sb("twist", [P, P])
        with stage(nc, "loaded", "halved") as (block, s):
            loads = [(wq[:, :], A["l1_wq"]), (wk[:, :], A["l1_wk"]), (wv[:, :], A["l1_wv"]), (cmask[:, :], A["cmask"]),
                     (cn_w1[:, :], A["cn_w1"]), (cn_w2[:, :], A["cn_w2"]), (cn_w3[:, :], A["cn_w3"]), (cn_w4[:, :], A["cn_w4"]),
                     (gc_w1[:, :], A["gc_w1"]), (gc_w2[:, :], A["gc_w2"]), (gc_w3[:, :], A["gc_w3"]), (cvec[:, :], A["cvec"]),
                     (twist[:, :], A["twist"])]

            @block.sync
            def _(sp):
                for dst, src in loads:
                    sp.dma_start(dst, src).then_inc(s["loaded"], 16)
                sp.wait_ge(s["loaded"], 16 * len(loads))

            @block.vector
            def _(dve):
                dve.wait_ge(s["loaded"], 16 * len(loads))
                dve.tensor_scalar(half[:, :], cvec[:, 3:7:3], 0.5, None, ALU.mult)
        layernorm_stage(nc, mem, x, xn, CHUNKS)

        with ExitStack() as attn:
            def asb(name, shape, dt=F32):
                return attn.enter_context(nc.sbuf_tensor("l1_" + name, shape, dt))

            xb, qT, kT, vb = asb("xb", [P, NT]), asb("qT", [P, NT]), asb("kT", [P, NT]), asb("vb", [P, 4, P])
            w = attention_memory(asb, 1)
            with nc.Fori(0, NB) as b:
                qkv_stage(nc, mem, xn, b, xb, wq, wk, wv, qT, kT, vb, P ** -0.5)
                heads_stage(nc, mem, w, 1, True, lambda h: qT, kT, lambda h: vb,
                            lambda h, i: cmask[:, NT - (i + 1) * P:NT], lambda h, i: 1.0,
                            (lambda dve, sem: dve.sem_inc(sem, 1), lambda pool, sem: pool.sem_inc(sem, 1)),
                            sat[:, bass.ts(b, NT)], first=True)

        with ExitStack() as ffn:
            def fsb(name, shape, dt=F32):
                return ffn.enter_context(nc.sbuf_tensor("l1_" + name, shape, dt))

            hid = fsb("hid", [P, NB, CH])
            cpl = fsb("cpl", [P, 2, CH])
            gm, g1, g2, gt = fsb("gm", [P, NB]), fsb("g1", [64, NB]), fsb("g2", [32, NB]), fsb("gt", [P, NB])
            arc = fsb("arc", [P, 2])
            base = fsb("base", [P, NB])
            nc.scalar.preload_act_table_set("gelu_and_others")
            with stage(nc, "mean_done", "g_mm", "g_act", "ar_done", "b1_done") as (block, s):
                @block.tensor
                def _(pe):
                    pe.wait_ge(s["mean_done"], 1)
                    pe.matmul(ps[0][0:64, 0:NB], gc_w1[:, :], gm[:, :], start=True, stop=True).then_inc(s["g_mm"], 1)
                    pe.wait_ge(s["g_act"], 1)
                    pe.matmul(ps[1][0:32, 0:NB], gc_w2[:, :], g1[:, :], start=True, stop=True).then_inc(s["g_mm"], 1)
                    pe.wait_ge(s["g_act"], 2)
                    pe.matmul(ps[2][:, 0:NB], gc_w3[:, :], g2[:, :], start=True, stop=True).then_inc(s["g_mm"], 1)

                @block.scalar
                def _(act):
                    act.wait_ge(s["g_mm"], 1)
                    act.activation(g1[:, :], ps[0][0:64, 0:NB], ACT.Gelu, scale=1.0 / NT, bias=cvec[0:64, 4:5]).then_inc(s["g_act"], 1)
                    act.wait_ge(s["g_mm"], 2)
                    act.activation(g2[:, :], ps[1][0:32, 0:NB], ACT.Gelu, bias=cvec[0:32, 5:6]).then_inc(s["g_act"], 1)
                    act.wait_ge(s["g_mm"], 3)
                    act.activation(gt[:, :], ps[2][:, 0:NB], ACT.Tanh, scale=0.5, bias=half[:, 1:2]).then_inc(s["g_act"], 1)

                @block.vector
                def _(dve):
                    dve.tensor_reduce(gm[:, :], xn[:, :].rearrange("p (b t) -> p b t", b=NB), AX.X, ALU.add).then_inc(s["mean_done"], 1)
                    dve.tensor_scalar(arc[:, 0:1], cvec[:, 7:8], 0.3, None, ALU.mult)
                    dve.tensor_scalar(arc[:, 1:2], cvec[:, 7:8], 0.7, None, ALU.mult).then_inc(s["ar_done"], 1)
                    dve.wait_ge(s["g_act"], 3)
                    dve.wait_ge(s["ar_done"], 1)
                    dve.tensor_scalar(base[:, :], gt[:, :], arc[:, 1:2], 0.1, ALU.mult, ALU.add)
            with nc.Fori(0, 3) as cycle:
                with stage(nc, "mm", "acted", "read", "cpl_done", "tw_done") as (block, s):
                    ws = [cn_w1[:, :], cn_w2[:, :], cn_w3[:, :], cn_w4[:, :]]
                    rows = [P, 64, 32, P]

                    @block.tensor
                    def _(pe):
                        for l in range(4):
                            for k in range(NB):
                                if l:
                                    pe.wait_ge(s["acted"], (l - 1) * NB + k + 1)
                                src = xn[:, CHUNKS[k]] if l == 0 else hid[0:rows[l - 1], k, :]
                                pe.matmul(ps[k][0:rows[l], :], ws[l], src, start=True, stop=True).then_inc(s["mm"], 1)
                        for k in range(NB):
                            pe.wait_ge(s["acted"], 3 * NB + k + 1)
                            pe.matmul(ps[k][:, :], twist[:, :], xn[:, CHUNKS[k]], start=True, stop=True).then_inc(s["mm"], 1)

                    @block.scalar
                    def _(act):
                        for l in range(4):
                            for k in range(NB):
                                act.wait_ge(s["mm"], l * NB + k + 1)
                                r = rows[l]
                                if l < 3:
                                    act.activation(hid[0:r, k, :], ps[k][0:r, :], ACT.Gelu, bias=cvec[0:r, l:l + 1]).then_inc(s["acted"], 1)
                                else:
                                    act.activation(hid[:, k, :], ps[k][:, :], ACT.Tanh, scale=0.5, bias=half[:, 0:1]).then_inc(s["acted"], 1)

                    @block.vector
                    def _(dve):
                        for k in range(NB):
                            dve.wait_ge(s["acted"], 3 * NB + k + 1)
                            dve.tensor_scalar(hid[:, k, :], hid[:, k, :], arc[:, 0:1], base[:, k:k + 1], ALU.mult, ALU.add).then_inc(s["cpl_done"], 1)
                            dve.wait_ge(s["cpl_done"], k + 1)
                            dve.wait_ge(s["mm"], 4 * NB + k + 1)
                            if k >= 2:
                                dve.wait_ge(s["read"], k - 1)
                            dve.tensor_tensor(cpl[:, k % 2, :], hid[:, k, :], ps[k][:, :], ALU.mult).then_inc(s["tw_done"], 1)
                            dve.wait_ge(s["tw_done"], k + 1)
                            dve.tensor_tensor(xn[:, CHUNKS[k]], xn[:, CHUNKS[k]], cpl[:, k % 2, :], ALU.add).then_inc(s["read"], 1)
            nc.scalar.preload_act_table_set("natural_log_exp_and_others")
            residual_stage(nc, mem, x, sat, xn, cpl)


def qkv_stage(nc, mem, xn, b, xb, wq, wk, wv, qT, kT, vb, q_scale, q_bias=None, k_bias=None):
    ps = mem["ps"]
    with stage(nc, "x_done", "q_mm", "k_mm", "v_mm") as (block, s):
        @block.tensor
        def _(pe):
            pe.wait_ge(s["x_done"], 1)
            pe.matmul(ps[0][:, :], wq[:, :], xb[:, :], start=True, stop=True).then_inc(s["q_mm"], 1)
            pe.matmul(ps[1][:, :], wk[:, :], xb[:, :], start=True, stop=True).then_inc(s["k_mm"], 1)
            for j in range(4):
                last = pe.matmul(ps[2][:, j * P:(j + 1) * P], xb[:, j * P:(j + 1) * P], wv[:, :], start=True, stop=True)
            last.then_inc(s["v_mm"], 1)

        @block.scalar
        def _(act):
            act.wait_ge(s["q_mm"], 1)
            if q_bias is None:
                act.activation(qT[:, :], ps[0][:, :], ACT.Copy, scale=q_scale)
            else:
                act.activation(qT[:, :], ps[0][:, :], ACT.Identity, bias=q_bias)
            act.wait_ge(s["v_mm"], 1)
            act.activation(vb[:, :, :], ps[2][:, :].rearrange("p (j e) -> p j e", e=P), ACT.Copy)

        @block.vector
        def _(dve):
            dve.tensor_copy(xb[:, :], xn[:, bass.ts(b, NT)]).then_inc(s["x_done"], 1)
            dve.wait_ge(s["k_mm"], 1)
            if k_bias is None:
                dve.tensor_copy(kT[:, :], ps[1][:, :])
            else:
                dve.tensor_scalar(kT[:, :], ps[1][:, :], k_bias, None, ALU.add)


def layout_l1(i, A):
    A["l1_wq"], A["l1_wk"], A["l1_wv"] = i["L1_attn_Wq"], i["L1_attn_Wk"], i["L1_attn_Wv"]
    t, c = np.arange(P)[:, None], np.arange(NT)[None, :]
    A["cmask"] = np.where(c - 3 * P <= t, 0.0, -1e30).astype(np.float32)
    for n in ("cn_w1", "cn_w2", "cn_w3", "gc_w1", "gc_w2"):
        A[n] = i["L1_ffn_" + n]
    A["cn_w4"] = np.broadcast_to(i["L1_ffn_cn_w4"], (32, P))
    A["gc_w3"] = np.broadcast_to(i["L1_ffn_gc_w3"], (32, P))
    cv = np.zeros((P, 8), np.float32)
    for j, n in enumerate(("cn_b1", "cn_b2", "cn_b3", "cn_b4", "gc_b1", "gc_b2", "gc_b3", "adaptive_range")):
        v = i["L1_ffn_" + n]
        if v.shape == (1,):
            cv[:, j] = v[0]
        else:
            cv[0:v.shape[0], j] = v
    A["cvec"] = cv
    tw = np.zeros((P, P), np.float32)
    for r in range(32):
        tw[64 + r, r] = 1.0
        tw[96 + r, 32 + r] = -1.0
        tw[r, 64 + r] = -1.0
        tw[32 + r, 96 + r] = 1.0
    A["twist"] = tw


NH = 16
HD = P // NH
HG = 8


def group_prepare(w, group_index, qT, vb, hq, hv):
    def queries(dve, sem):
        for h in range(HG):
            dve.tensor_scalar(w["qm"][:, h, :], qT[:, :], hq[:, bass.ds(group_index * HG + h, 1)], None, ALU.mult).then_inc(sem, 1)

    def values(pool, sem):
        for h in range(HG):
            pool.tensor_tensor(w["vm"][:, h, :, :], vb[:, :, :],
                               hv[:, bass.ds(group_index * HG + h, 1), :].to_broadcast([P, 4, P]), ALU.mult).then_inc(sem, 1)

    return queries, values


def layer2(nc, mem, A, x):
    ps = mem["ps"]
    NE, TOPK, NPAIR = 16, 8, 8
    with ExitStack() as ctx:
        def sb(name, shape, dt=F32):
            return ctx.enter_context(nc.sbuf_tensor("l2_" + name, shape, dt))

        xn, sat = sb("xn", [P, TOK]), sb("sat", [P, TOK])
        layernorm_stage(nc, mem, x, xn, CHUNKS)

        with ExitStack() as attn:
            def asb(name, shape, dt=F32):
                return attn.enter_context(nc.sbuf_tensor("l2_" + name, shape, dt))

            wq, wk, wv = asb("wq", [P, P]), asb("wk", [P, P]), asb("wv", [P, P])
            rel, slope = asb("rel", [P, NT]), asb("slope", [P, NH])
            hq, hv = asb("hq", [P, NH]), asb("hv", [P, NH, P])
            xb, qT, kT, vb = asb("xb", [P, NT]), asb("qT", [P, NT]), asb("kT", [P, NT]), asb("vb", [P, 4, P])
            acc, slopes = asb("acc", [P, NT]), asb("slopes", [P, HG])
            w = attention_memory(asb, HG)
            w["qm"], w["vm"] = asb("qm", [P, HG, NT]), asb("vm", [P, HG, 4, P])
            with stage(nc, "loaded") as (block, s):
                loads = [(wq[:, :], A["l2_wq"]), (wk[:, :], A["l2_wk"]), (wv[:, :], A["l2_wv"]), (rel[:, :], A["rel"]),
                         (slope[:, :], A["slope"]), (hq[:, :], A["head_q"]), (hv[:, :, :], A["head_v"])]

                @block.sync
                def _(sp):
                    for dst, src in loads:
                        sp.dma_start(dst, src).then_inc(s["loaded"], 16)
                    sp.wait_ge(s["loaded"], 16 * len(loads))

            with nc.Fori(0, NB) as b:
                qkv_stage(nc, mem, xn, b, xb, wq, wk, wv, qT, kT, vb, P ** -0.5)
                zero_stage(nc, acc)
                with nc.Fori(0, NH // HG) as g:
                    copy_stage(nc, slopes[:, :], slope[:, bass.ts(g, HG)])
                    heads_stage(nc, mem, w, HG, True, lambda h: w["qm"][:, h, :], kT, lambda h: w["vm"][:, h, :, :],
                                lambda h, i: rel[:, NT - (i + 1) * P:NT], lambda h, i: slopes[:, h:h + 1],
                                group_prepare(w, g, qT, vb, hq, hv), acc[:, :])
                copy_stage(nc, sat[:, bass.ts(b, NT)], acc[:, :])

        with ExitStack() as ffn:
            def fsb(name, shape, dt=F32):
                return ffn.enter_context(nc.sbuf_tensor("l2_" + name, shape, dt))

            NTILE = TOK // P
            gate_w = fsb("gate_w", [P, NE])
            wg, wu, wd = fsb("wg", [P, NPAIR + 1, P]), fsb("wu", [P, NPAIR + 1, P]), fsb("wd", [P, NPAIR + 1, P])
            sel = fsb("sel", [NE, NPAIR, P])
            sq = fsb("sq", [P, 2, CH])
            gsq, gnorm, gi = fsb("gsq", [P, NE]), fsb("gnorm", [P, NE]), fsb("gi", [P, NE])
            xnorm, xinv = fsb("xnorm", [P, NTILE]), fsb("xinv", [P, NTILE])
            lg, lr = fsb("lg", [P, NTILE, NE]), fsb("lr", [P, NTILE, NE])
            top = fsb("top", [P, NTILE, TOPK])
            th = fsb("th", [P, NTILE, NE])
            csum, cinv = fsb("csum", [P, NTILE]), fsb("cinv", [P, NTILE])
            cT = fsb("cT", [NE, TOK])
            sl, us, cbuf = fsb("sl", [P, 3, CH]), fsb("us", [P, 2, CH]), fsb("cbuf", [P, 2, CH])

            with stage(nc, "loaded", "squared", "g_sq", "ss_mm", "g_mm", "ss_max", "root", "n_max", "inv", "gw_done", "lg_mm",
                       "lg_done", "top_done", "rep", "mask", "tanh_done", "sig", "wts", "sum_done", "comb", "c_mm", "c_done") as (block, s):
                loads = [(gate_w[:, :], A["l2_gate_w"]), (wg[:, :, :], A["l2_wg"]), (wu[:, :, :], A["l2_wu"]),
                         (wd[:, :, :], A["l2_wd"]), (sel[:, :, :], A["sel_pair"])]

                @block.sync
                def _(sp):
                    for dst, src in loads:
                        sp.dma_start(dst, src).then_inc(s["loaded"], 16)

                @block.tensor
                def _(pe):
                    pe.wait_ge(s["g_sq"], 1)
                    pe.matmul(ps[1][:, 0:NE], mem["ones"][:, :], gsq[:, :], start=True, stop=True).then_inc(s["g_mm"], 1)
                    for t in range(NTILE):
                        pe.wait_ge(s["squared"], t // 4 + 1)
                        pe.matmul(ps[0][:, t:t + 1], sq[:, (t // 4) % 2, (t % 4) * P:(t % 4 + 1) * P], mem["ones"][:, 0:1],
                                  start=True, stop=True).then_inc(s["ss_mm"], 1)
                    pe.wait_ge(s["gw_done"], 1)
                    for t in range(NTILE):
                        last = pe.matmul(ps[2][:, t * NE:(t + 1) * NE], xn[:, t * P:(t + 1) * P], gi[:, :], start=True, stop=True)
                    last.then_inc(s["lg_mm"], 1)
                    pe.wait_ge(s["comb"], 1)
                    for k in range(NB):
                        if k >= 2:
                            pe.wait_ge(s["c_done"], k - 1)
                        for t in range(4):
                            last = pe.transpose(ps[3 + k % 2][0:NE, t * P:(t + 1) * P], th[:, 4 * k + t, :], mem["ident"][:, :])
                        last.then_inc(s["c_mm"], 1)

                @block.scalar
                def _(act):
                    for k in range(NB):
                        if k >= 2:
                            act.wait_ge(s["ss_mm"], 4 * (k - 1))
                        act.activation(sq[:, k % 2, :], xn[:, CHUNKS[k]], ACT.Square).then_inc(s["squared"], 1)
                    act.wait_ge(s["ss_max"], 2)
                    act.activation(xnorm[:, :], xnorm[:, :], ACT.Sqrt).then_inc(s["root"], 1)
                    act.activation(gnorm[:, :], gnorm[:, :], ACT.Sqrt).then_inc(s["root"], 1)
                    act.wait_ge(s["lg_done"], 1)
                    act.activation(th[:, :, :], lg[:, :, :], ACT.Tanh, scale=0.5).then_inc(s["tanh_done"], 1)
                    for k in range(NB):
                        act.wait_ge(s["c_mm"], k + 1)
                        act.activation(cT[:, CHUNKS[k]], ps[3 + k % 2][0:NE, :], ACT.Copy).then_inc(s["c_done"], 1)

                @block.vector
                def _(dve):
                    dve.wait_ge(s["loaded"], 16 * len(loads))
                    dve.tensor_tensor(gsq[:, :], gate_w[:, :], gate_w[:, :], ALU.mult).then_inc(s["g_sq"], 1)
                    dve.wait_ge(s["g_mm"], 1)
                    dve.tensor_scalar(gnorm[:, :], ps[1][:, 0:NE], 1e-34, None, ALU.max).then_inc(s["ss_max"], 1)
                    dve.wait_ge(s["ss_mm"], NTILE)
                    dve.tensor_scalar(xnorm[:, :], ps[0][:, 0:NTILE], 1e-34, None, ALU.max).then_inc(s["ss_max"], 1)
                    dve.wait_ge(s["root"], 2)
                    dve.tensor_scalar(xnorm[:, :], xnorm[:, :], 1e-12, None, ALU.max).then_inc(s["n_max"], 1)
                    dve.tensor_scalar(gnorm[:, :], gnorm[:, :], 1e-12, None, ALU.max).then_inc(s["n_max"], 1)
                    dve.wait_ge(s["n_max"], 2)
                    dve.reciprocal(xinv[:, :], xnorm[:, :]).then_inc(s["inv"], 1)
                    dve.reciprocal(gsq[:, :], gnorm[:, :]).then_inc(s["inv"], 1)
                    dve.wait_ge(s["inv"], 2)
                    dve.tensor_tensor(gi[:, :], gate_w[:, :], gsq[:, :], ALU.mult).then_inc(s["gw_done"], 1)
                    dve.wait_ge(s["lg_mm"], 1)
                    dve.tensor_tensor(lg[:, :, :], ps[2][:, :].rearrange("p (t e) -> p t e", e=NE),
                                      xinv[:, :, None].to_broadcast([P, NTILE, NE]), ALU.mult).then_inc(s["lg_done"], 1)
                    dve.wait_ge(s["lg_done"], 1)
                    for t in range(NTILE):
                        dve.max(top[:, t, :], lg[:, t, :]).then_inc(s["top_done"], 1)
                    for t in range(NTILE):
                        dve.wait_ge(s["top_done"], t + 1)
                        dve.match_replace(lr[:, t, :], top[:, t, :], lg[:, t, :], -1e30).then_inc(s["rep"], 1)
                    dve.wait_ge(s["rep"], NTILE)
                    dve.tensor_scalar(lr[:, :, :], lr[:, :, :], -1e29, None, ALU.is_lt).then_inc(s["mask"], 1)
                    dve.wait_ge(s["tanh_done"], 1)
                    dve.tensor_scalar(th[:, :, :], th[:, :, :], 0.5, 0.5, ALU.mult, ALU.add).then_inc(s["sig"], 1)
                    dve.wait_ge(s["sig"], 1)
                    dve.wait_ge(s["mask"], 1)
                    dve.tensor_tensor(th[:, :, :], th[:, :, :], lr[:, :, :], ALU.mult).then_inc(s["wts"], 1)
                    dve.wait_ge(s["wts"], 1)
                    dve.tensor_reduce(csum[:, :], th[:, :, :], AX.X, ALU.add).then_inc(s["sum_done"], 1)
                    dve.wait_ge(s["sum_done"], 1)
                    dve.reciprocal(cinv[:, :], csum[:, :]).then_inc(s["sum_done"], 1)
                    dve.wait_ge(s["sum_done"], 2)
                    dve.tensor_tensor(th[:, :, :], th[:, :, :], cinv[:, :, None].to_broadcast([P, NTILE, NE]), ALU.mult).then_inc(s["comb"], 1)

            nc.scalar.preload_act_table_set("silu_and_others")
            with nc.Fori(0, NB) as k:
                with stage(nc, "g_mm", "u_mm", "c_mm", "silu_done", "c_done", "m1", "m2", "d_mm") as (block, s):
                    @block.tensor
                    def _(pe):
                        def up(e):
                            r = P if e < NPAIR else 64
                            if e >= 2:
                                pe.wait_ge(s["silu_done"], e - 1)
                            pe.matmul(ps[e % 2][0:r, :], wg[:, e, 0:r], xn[:, bass.ts(k, CH)], start=True, stop=True).then_inc(s["g_mm"], 1)
                            if e >= 2:
                                pe.wait_ge(s["m1"], e - 1)
                            pe.matmul(ps[2 + e % 2][0:r, :], wu[:, e, 0:r], xn[:, bass.ts(k, CH)], start=True, stop=True).then_inc(s["u_mm"], 1)
                            if e < NPAIR:
                                if e >= 2:
                                    pe.wait_ge(s["c_done"], e - 1)
                                pe.matmul(ps[4 + e % 2][:, :], sel[:, e, :], cT[:, bass.ts(k, CH)], start=True, stop=True).then_inc(s["c_mm"], 1)

                        up(0)
                        for e in range(NPAIR + 1):
                            if e < NPAIR:
                                up(e + 1)
                            r = P if e < NPAIR else 64
                            pe.wait_ge(s["m2"], e + 1)
                            pe.matmul(ps[6][:, :], wd[0:r, e, :], us[0:r, e % 2, :], start=(e == 0), stop=(e == NPAIR)).then_inc(s["d_mm"], 1)

                    @block.scalar
                    def _(act):
                        for e in range(NPAIR + 1):
                            r = P if e < NPAIR else 64
                            act.wait_ge(s["g_mm"], e + 1)
                            if e >= 3:
                                act.wait_ge(s["m2"], e - 2)
                            act.activation(sl[0:r, e % 3, :], ps[e % 2][0:r, :], ACT.Silu).then_inc(s["silu_done"], 1)
                            if e < NPAIR:
                                act.wait_ge(s["c_mm"], e + 1)
                                if e >= 2:
                                    act.wait_ge(s["m2"], e - 1)
                                act.activation(cbuf[:, e % 2, :], ps[4 + e % 2][:, :], ACT.Copy).then_inc(s["c_done"], 1)

                    @block.vector
                    def _(dve):
                        for e in range(NPAIR + 1):
                            r = P if e < NPAIR else 64
                            dve.wait_ge(s["silu_done"], e + 1)
                            dve.wait_ge(s["u_mm"], e + 1)
                            if e >= 2:
                                dve.wait_ge(s["d_mm"], e - 1)
                            if e < NPAIR:
                                dve.tensor_tensor(sl[0:r, e % 3, :], sl[0:r, e % 3, :], ps[2 + e % 2][0:r, :], ALU.mult).then_inc(s["m1"], 1)
                                dve.wait_ge(s["m1"], e + 1)
                                dve.wait_ge(s["c_done"], e + 1)
                                dve.tensor_tensor(us[:, e % 2, :], sl[:, e % 3, :], cbuf[:, e % 2, :], ALU.mult).then_inc(s["m2"], 1)
                            else:
                                dve.tensor_tensor(us[0:r, e % 2, :], sl[0:r, e % 3, :], ps[2 + e % 2][0:r, :], ALU.mult).then_inc(s["m2"], 1)
                        dve.wait_ge(s["d_mm"], NPAIR + 1)
                        dve.tensor_copy(xn[:, bass.ts(k, CH)], ps[6][:, :])

            nc.scalar.preload_act_table_set("natural_log_exp_and_others")
            residual_stage(nc, mem, x, sat, xn, cbuf)


def zero_stage(nc, a):
    with stage(nc, "zeroed") as (block, s):
        @block.gpsimd
        def _(pool):
            pool.memset(a[:, :], 0.0).then_inc(s["zeroed"], 1)


def copy_stage(nc, dst, src):
    with stage(nc, "copied") as (block, s):
        @block.vector
        def _(dve):
            dve.tensor_copy(dst, src).then_inc(s["copied"], 1)


def layout_l2(i, A):
    wkqv = i["L2_attn_W_kqv"]
    A["l2_wk"], A["l2_wq"], A["l2_wv"] = wkqv[0:P].T, wkqv[P:2 * P].T, wkqv[2 * P:3 * P].T
    t, c = np.arange(P)[:, None], np.arange(NT)[None, :]
    r = (c - 3 * P - t).astype(np.float32)
    A["rel"] = np.where(r <= 0, r, -1e30).astype(np.float32)
    sl = np.array([1.0 / (2.0 ** 8) ** ((n + 1) / NH) for n in range(NH)], np.float32)
    A["slope"] = np.broadcast_to(sl, (P, NH))
    own = (np.arange(P)[:, None] // HD == np.arange(NH)).astype(np.float32)
    A["head_q"] = own
    A["head_v"] = np.broadcast_to(own.T, (P, NH, P))
    A["l2_gate_w"] = i["L2_ffn_gate_w"].T
    for n, full, shared in (("l2_wg", "w_gate", "sw_gate"), ("l2_wu", "w_up", "sw_up")):
        a = np.zeros((P, 9, P), np.float32)
        a[:, 0:8, :] = i["L2_ffn_" + full].transpose(1, 0, 2).reshape(P, 8, P)
        a[:, 8, 0:64] = i["L2_ffn_" + shared]
        A[n] = a
    a = np.zeros((P, 9, P), np.float32)
    a[:, 0:8, :] = i["L2_ffn_w_down"].reshape(8, P, P).transpose(1, 0, 2)
    a[0:64, 8, :] = i["L2_ffn_sw_down"]
    A["l2_wd"] = a
    A["sel_pair"] = (np.arange(16)[:, None, None] == 2 * np.arange(8)[None, :, None] + np.arange(P)[None, None, :] // 64).astype(np.float32)


def butterfly_stages(dve, s, W, buf, work, weights, rows, transposed, bf0, m0):
    src, dst = W, buf
    for n, st in enumerate(range(8, -1, -1) if transposed else range(9)):
        d = 1 << st

        def half(t, r, k):
            return t[:, r, :].rearrange("p (n h s) -> p n h s", h=2, s=d)[:, :, k, :]

        def pair_weight(o, i):
            return weights[:, st, o, i, :].rearrange("p (n s) -> p n s", s=d)

        dve.wait_ge(s["bf"], bf0 + n * rows)
        for r in range(rows):
            for o in range(2):
                a, b = ((0, o), (1, o)) if transposed else ((o, 0), (o, 1))
                dve.tensor_tensor(half(dst, r, o), half(src, r, 0), pair_weight(*a), ALU.mult)
                dve.tensor_tensor(half(work, r, o), half(src, r, 1), pair_weight(*b), ALU.mult).then_inc(s["bf_m"], 1)
        dve.wait_ge(s["bf_m"], m0 + 2 * rows * (n + 1))
        for r in range(rows):
            dve.tensor_tensor(dst[:, r, :], dst[:, r, :], work[:, r, :], ALU.add).then_inc(s["bf"], 1)
        src, dst = dst, src
    return src


def layer3(nc, mem, A, x):
    ps = mem["ps"]
    NBU = 40
    LR = 1024
    with ExitStack() as ctx:
        def sb(name, shape, dt=F32):
            return ctx.enter_context(nc.sbuf_tensor("l3_" + name, shape, dt))

        xn, sat = sb("xn", [P, TOK]), sb("sat", [P, TOK])
        layernorm_stage(nc, mem, x, xn, CHUNKS)
        bias_dram = nc.dram_tensor("l3_bias_rows", (NH, LR), F32, kind="Internal").ap()

        with ExitStack() as attn:
            def asb(name, shape, dt=F32):
                return attn.enter_context(nc.sbuf_tensor("l3_" + name, shape, dt))

            wq, wk, wv, wo = asb("wq", [P, P]), asb("wk", [P, P]), asb("wv", [P, P]), asb("wo", [P, P])
            bvec = asb("bvec", [P, 4])
            gw = asb("gw", [P, 8, NH])
            gb = asb("gb", [P, 8])
            gconst = asb("gconst", [P, NH])
            hq, hv = asb("hq", [P, NH]), asb("hv", [P, NH, P])
            xb, qT, kT, vb = asb("xb", [P, NT]), asb("qT", [P, NT]), asb("kT", [P, NT]), asb("vb", [P, 4, P])
            acc = asb("acc", [P, NT])
            flip = asb("flip", [P, P])
            gp, gs = asb("gp", [P, 4, 8, NH]), asb("gs", [P, 4, 2, NH])
            gate, gates = asb("gate", [P, 4, NH]), asb("gates", [P, 4, HG])
            PBW = 7 * P
            pb = asb("pb", [P, HG, PBW])
            w = attention_memory(asb, HG)
            w["qm"], w["vm"] = asb("qm", [P, HG, NT]), asb("vm", [P, HG, 4, P])
            with ExitStack() as setup:
                rel_embed = setup.enter_context(nc.sbuf_tensor("l3_rel_embed", [NBU, NH], F32))
                onehot = setup.enter_context(nc.sbuf_tensor("l3_onehot", [NBU, LR], F32))
                rows = setup.enter_context(nc.sbuf_tensor("l3_rows", [NH, LR], F32))
                with stage(nc, "loaded", "row_mm", "row_done", "stored") as (block, s):
                    loads = [(rel_embed[:, :], A["rel_embed"]), (onehot[:, :], A["bucket_onehot"]),
                             (wq[:, :], A["l3_wq"]), (wk[:, :], A["l3_wk"]), (wv[:, :], A["l3_wv"]), (wo[:, :], A["l3_wo"]),
                             (bvec[:, :], A["l3_bvec"]), (gw[:, :, :], A["l3_gw"]), (gb[:, :], A["l3_gb"]),
                             (gconst[:, :], A["l3_gconst"]), (hq[:, :], A["head_q3"]), (hv[:, :, :], A["head_v"]), (flip[:, :], A["flip"])]

                    @block.sync
                    def _(sp):
                        for dst, src in loads:
                            sp.dma_start(dst, src).then_inc(s["loaded"], 16)
                        sp.wait_ge(s["row_done"], 2)
                        sp.dma_start(bias_dram, rows[:, :]).then_inc(s["stored"], 16)
                        sp.wait_ge(s["stored"], 16)

                    @block.tensor
                    def _(pe):
                        pe.wait_ge(s["loaded"], 16 * len(loads))
                        for c in range(2):
                            pe.matmul(ps[c][0:NH, :], rel_embed[:, :], onehot[:, c * 512:(c + 1) * 512], start=True, stop=True).then_inc(s["row_mm"], 1)

                    @block.vector
                    def _(dve):
                        for c in range(2):
                            dve.wait_ge(s["row_mm"], c + 1)
                            dve.tensor_copy(rows[:, c * 512:(c + 1) * 512], ps[c][0:NH, :]).then_inc(s["row_done"], 1)

            zero_stage(nc, sat)
            with nc.Fori(0, NH // HG) as g:
                with stage(nc, "loaded", "flip_mm", "flip_done") as (block, s):
                    hankel = [w["PT"][:, :, :, :].rearrange("p a j t -> p (a j t)"), w["vm"][:, :, :, :].rearrange("p h j t -> p (h j t)")]
                    cols = [slice(0, 512), slice(512, PBW)]

                    def rows_of(h):
                        return hankel[h // 4][:, (h % 4) * PBW:(h % 4 + 1) * PBW]

                    @block.sync
                    def _(sp):
                        for h in range(HG):
                            row = bias_dram[bass.ds(g * HG + h, 1), :]
                            sp.dma_start(rows_of(h), bass.AP(row.tensor, row.offset, [[1, P], [1, PBW]])).then_inc(s["loaded"], 16)

                    @block.tensor
                    def _(pe):
                        pe.wait_ge(s["loaded"], 16 * HG)
                        for h in range(HG):
                            for c in range(2):
                                n = 2 * h + c
                                if n >= 2:
                                    pe.wait_ge(s["flip_done"], n - 1)
                                pe.matmul(ps[c][:, 0:cols[c].stop - cols[c].start], flip[:, :], rows_of(h)[:, cols[c]],
                                          start=True, stop=True).then_inc(s["flip_mm"], 1)

                    @block.vector
                    def _(dve):
                        for h in range(HG):
                            for c in range(2):
                                dve.wait_ge(s["flip_mm"], 2 * h + c + 1)
                                dve.tensor_copy(pb[:, h, cols[c]], ps[c][:, 0:cols[c].stop - cols[c].start]).then_inc(s["flip_done"], 1)
                with nc.Fori(0, NB) as b:
                    qkv_stage(nc, mem, xn, b, xb, wq, wk, wv, qT, kT, vb, None, bvec[:, 0:1], bvec[:, 1:2])
                    with stage(nc, "p_mm", "g1", "g2", "g3", "e_done", "g4", "g5", "g6", "g7") as (block, s):
                        @block.tensor
                        def _(pe):
                            for i in range(4):
                                last = pe.matmul(ps[0][:, i * P:(i + 1) * P], xb[:, i * P:(i + 1) * P],
                                                 gw[:, :, :].rearrange("p e h -> p (e h)"), start=True, stop=True)
                            last.then_inc(s["p_mm"], 1)

                        @block.scalar
                        def _(act):
                            act.wait_ge(s["g2"], 1)
                            act.activation(gs[:, :, :, :], gs[:, :, :, :], ACT.Exp, scale=-1.0).then_inc(s["e_done"], 1)

                        @block.vector
                        def _(dve):
                            dve.wait_ge(s["p_mm"], 1)
                            for i in range(4):
                                dve.tensor_tensor(gp[:, i, :, :], ps[0][:, i * P:(i + 1) * P].rearrange("p (e h) -> p e h", e=8),
                                                  gb[:, :, None].to_broadcast([P, 8, NH]), ALU.add).then_inc(s["g1"], 1)
                            dve.wait_ge(s["g1"], 4)
                            dve.tensor_reduce(gs[:, :, :, :], gp[:, :, :, :].rearrange("p i (k e) h -> p (i k) h e", k=2), AX.X, ALU.add).then_inc(s["g2"], 1)
                            dve.wait_ge(s["e_done"], 1)
                            dve.tensor_scalar(gs[:, :, :, :], gs[:, :, :, :], 1.0, None, ALU.add).then_inc(s["g3"], 1)
                            dve.wait_ge(s["g3"], 1)
                            dve.reciprocal(gs[:, :, :, :], gs[:, :, :, :]).then_inc(s["g4"], 1)
                            dve.wait_ge(s["g4"], 1)
                            dve.tensor_tensor(gate[:, :, :], gs[:, :, 1, :], gconst[:, None, :].to_broadcast([P, 4, NH]), ALU.mult).then_inc(s["g5"], 1)
                            dve.wait_ge(s["g5"], 1)
                            dve.scalar_tensor_tensor(gate[:, :, :], gate[:, :, :], -1.0, gs[:, :, 0, :], ALU.add, ALU.mult).then_inc(s["g6"], 1)
                            dve.wait_ge(s["g6"], 1)
                            dve.tensor_scalar(gate[:, :, :], gate[:, :, :], 2.0, None, ALU.add).then_inc(s["g7"], 1)
                            dve.wait_ge(s["g7"], 1)
                            dve.tensor_copy(gates[:, :, :], gate[:, :, bass.ts(g, HG)])
                    heads_stage(nc, mem, w, HG, False, lambda h: w["qm"][:, h, :], kT, lambda h: w["vm"][:, h, :, :],
                                lambda h, i: pb[:, h, (3 - i) * P:(3 - i) * P + NT], lambda h, i: gates[:, i, h:h + 1],
                                group_prepare(w, g, qT, vb, hq, hv), acc[:, :], first=True)
                    store_rows_stage(nc, sat, acc, b, g)
            with stage(nc, "b_done", "o_mm", "o_done") as (block, s):
                @block.tensor
                def _(pe):
                    for k in range(NB):
                        pe.wait_ge(s["b_done"], k + 1)
                        pe.matmul(ps[k][:, :], wo[:, :], sat[:, CHUNKS[k]], start=True, stop=True).then_inc(s["o_mm"], 1)

                @block.scalar
                def _(act):
                    for k in range(NB):
                        act.wait_ge(s["o_mm"], k + 1)
                        act.activation(sat[:, CHUNKS[k]], ps[k][:, :], ACT.Identity, bias=bvec[:, 3:4]).then_inc(s["o_done"], 1)

                @block.vector
                def _(dve):
                    for k in range(NB):
                        dve.tensor_scalar(sat[:, CHUNKS[k]], sat[:, CHUNKS[k]], bvec[:, 2:3], None, ALU.add).then_inc(s["b_done"], 1)

        with ExitStack() as ffn:
            def fsb(name, shape, dt=F32):
                return ffn.enter_context(nc.sbuf_tensor("l3_" + name, shape, dt))

            H = 512
            FT = H // P
            up = fsb("up", [P, 2, H])
            down = fsb("down", [P, 1, H])
            buf, work = fsb("buf", [P, 2, H]), fsb("work", [P, 2, H])
            uw, dw = fsb("uw", [P, 9, 2, 2, 256]), fsb("dw", [P, 9, 2, 2, 256])
            ubias = fsb("ubias", [P, FT])
            obias = fsb("obias", [P, 2])
            hbias = fsb("hbias", [P, FT])
            w_up, w_down = fsb("w_up", [P, H]), fsb("w_down", [P, FT, P])
            hid = fsb("hid", [P, 2, FT, CH])
            e = fsb("e", [P, 2, CH])
            with stage(nc, "loaded", "bf", "bf_m", "t_mm", "hb_done", "ob_done") as (block, s):
                loads = [(up[:, :, :], A["l3_up"]), (down[:, :, :], A["l3_down"]), (ubias[:, :], A["l3_ubias"]), (obias[:, :], A["l3_obias"])]

                @block.sync
                def _(sp):
                    for dst, src in loads:
                        sp.dma_start(dst, src).then_inc(s["loaded"], 16)
                    sp.dma_start(uw[:, :, :, :, :], A["l3_uw"].partition_broadcast(P)).then_inc(s["loaded"], 16)
                    sp.dma_start(dw[:, :, :, :, :], A["l3_dw"].partition_broadcast(P)).then_inc(s["loaded"], 16)

                @block.vector
                def _(dve):
                    dve.wait_ge(s["loaded"], 16 * (len(loads) + 2))
                    dve.sem_inc(s["bf"], 1)
                    end = butterfly_stages(dve, s, up, buf, work, uw, 2, False, 1, 0)
                    n = 1 + 9 * 2
                    dve.wait_ge(s["bf"], n)
                    dve.tensor_copy(w_up[:, :], end[:, 0, :]).then_inc(s["bf"], 1)
                    for f in range(FT):
                        dve.tensor_tensor(work[:, 0, f * P:(f + 1) * P], end[:, 1, f * P:(f + 1) * P], mem["ident"][:, :], ALU.mult).then_inc(s["bf"], 1)
                    dve.wait_ge(s["bf"], n + 5)
                    dve.tensor_reduce(hbias[:, :], work[:, 0, :].rearrange("p (f c) -> p f c", f=FT), AX.X, ALU.add).then_inc(s["hb_done"], 1)
                    dve.wait_ge(s["hb_done"], 1)
                    dve.tensor_tensor(hbias[:, :], hbias[:, :], ubias[:, :], ALU.add)
                    butterfly_stages(dve, s, down, buf, work, dw, 1, True, n + 5, 36)
                    dve.tensor_scalar(obias[:, 0:1], obias[:, 0:1], obias[:, 1:2], None, ALU.add).then_inc(s["ob_done"], 1)
                    dve.wait_ge(s["t_mm"], 1)
                    dve.tensor_copy(w_down[:, :, :], ps[0][:, :].rearrange("p (f d) -> p f d", f=FT))

                @block.tensor
                def _(pe):
                    pe.wait_ge(s["bf"], 1 + 9 * 2 + 5 + 9)
                    for f in range(FT):
                        last = pe.transpose(ps[0][:, f * P:(f + 1) * P], buf[:, 0, f * P:(f + 1) * P], mem["ident"][:, :])
                    last.then_inc(s["t_mm"], 1)

            nc.scalar.preload_act_table_set("gelu_and_others")
            with stage(nc, "up_mm", "gelu_done", "down_mm", "out_done") as (block, s):
                @block.tensor
                def _(pe):
                    def ups(k):
                        for f in range(FT):
                            if k:
                                pe.wait_ge(s["gelu_done"], (k - 1) * FT + f + 1)
                            pe.matmul(ps[f][:, :], w_up[:, f * P:(f + 1) * P], xn[:, CHUNKS[k]], start=True, stop=True).then_inc(s["up_mm"], 1)

                    ups(0)
                    for k in range(NB):
                        if k + 1 < NB:
                            ups(k + 1)
                        if k >= 2:
                            pe.wait_ge(s["out_done"], k - 1)
                        for f in range(FT):
                            pe.wait_ge(s["gelu_done"], k * FT + f + 1)
                            last = pe.matmul(ps[4 + k % 2][:, :], w_down[:, f, :], hid[:, k % 2, f, :], start=(f == 0), stop=(f == FT - 1))
                        last.then_inc(s["down_mm"], 1)

                @block.scalar
                def _(act):
                    for k in range(NB):
                        for f in range(FT):
                            act.wait_ge(s["up_mm"], k * FT + f + 1)
                            if k >= 2:
                                act.wait_ge(s["down_mm"], k - 1)
                            act.activation(hid[:, k % 2, f, :], ps[f][:, :], ACT.Gelu, bias=hbias[:, f:f + 1]).then_inc(s["gelu_done"], 1)

                @block.vector
                def _(dve):
                    for k in range(NB):
                        dve.wait_ge(s["down_mm"], k + 1)
                        if k + 1 < NB:
                            dve.wait_ge(s["up_mm"], (k + 2) * FT)
                        dve.tensor_scalar(xn[:, CHUNKS[k]], ps[4 + k % 2][:, :], obias[:, 0:1], None, ALU.add).then_inc(s["out_done"], 1)
            nc.scalar.preload_act_table_set("natural_log_exp_and_others")
            residual_stage(nc, mem, x, sat, xn, e)


def store_rows_stage(nc, sat, acc, b, g):
    with stage(nc, "added") as (block, s):
        @block.vector
        def _(dve):
            dve.tensor_tensor(sat[:, bass.ts(b, NT)], sat[:, bass.ts(b, NT)], acc[:, :], ALU.add).then_inc(s["added"], 1)


def layout_l3(i, A):
    for n, k in (("l3_wq", "q_w"), ("l3_wk", "k_w"), ("l3_wv", "v_w"), ("l3_wo", "out_w")):
        A[n] = i["L3_attn_" + k].T
    A["l3_bvec"] = np.stack([i["L3_attn_" + k] for k in ("q_b", "k_b", "v_b", "out_b")], axis=1)
    own = (np.arange(P)[:, None] // HD == np.arange(NH)).astype(np.float32)
    A["head_q3"] = (own * np.float32(HD ** -0.5)).astype(np.float32)
    gw = np.zeros((NH, HD, 8, NH), np.float32)
    for h in range(NH):
        gw[h, :, :, h] = i["L3_attn_gru_w"].T
    A["l3_gw"] = gw.reshape(P, 8, NH)
    A["l3_gb"] = np.broadcast_to(i["L3_attn_gru_b"], (P, 8))
    A["l3_gconst"] = np.broadcast_to(i["L3_attn_gru_const"].reshape(NH), (P, NH))
    A["flip"] = np.eye(P, dtype=np.float32)[::-1]
    A["rel_embed"] = i["L3_attn_rel_embed"]
    rel = np.arange(-511, 512)
    n = np.abs(rel)
    large = np.log(np.maximum(n, 1).astype(np.float32) / np.float32(10)) / np.float32(np.log(100 / 10)) * np.float32(10)
    large = np.minimum((10 + large).astype(np.int32), 19)
    bucket = (rel > 0) * 20 + np.where(n < 10, n, large)
    oh = np.zeros((40, 1024), np.float32)
    oh[bucket, np.arange(1023)] = 1.0
    A["bucket_onehot"] = oh
    A["l3_up"] = np.stack([i["L3_ffn_W_exp"], np.broadcast_to(i["L3_ffn_b_exp"], (P, 512))], axis=1)
    A["l3_down"] = i["L3_ffn_W_con"].T.reshape(P, 1, 512)
    A["l3_uw"] = i["L3_ffn_up_weights"].transpose(0, 2, 3, 1)
    A["l3_dw"] = i["L3_ffn_down_weights"].transpose(0, 2, 3, 1)
    A["l3_ubias"] = columns(i["L3_ffn_up_bias"], 4)
    A["l3_obias"] = np.stack([i["L3_ffn_b_con"], i["L3_ffn_down_bias"]], axis=1)


def layout_rest(i, A):
    layout_l1(i, A)
    layout_l2(i, A)
    layout_l3(i, A)


def shared_memory(nc, ctx, A):
    def sb(name, shape, dt=F32):
        return ctx.enter_context(nc.sbuf_tensor(name, shape, dt))

    mem = dict(
        ps=[ctx.enter_context(nc.psum_tensor(f"bank{i}", [P, 512], F32)) for i in range(8)],
        ident=sb("ident", [P, P]), ones=sb("ones", [P, P]), ones_mean=sb("ones_mean", [P, P]), eps=sb("eps", [P, 1]),
        ln_xc=sb("ln_xc", [P, 2, CH]), ln_sq=sb("ln_sq", [P, 2, CH]), ln_rs=sb("ln_rs", [P, 2, CH]))
    with stage(nc, "loaded") as (block, s):
        @block.sync
        def _(sp):
            sp.dma_start(mem["ident"][:, :], A["ident"]).then_inc(s["loaded"], 16)
            sp.wait_ge(s["loaded"], 16)

        @block.gpsimd
        def _(pool):
            pool.memset(mem["ones"][:, :], 1.0)
            pool.memset(mem["ones_mean"][:, :], 1.0 / P)
            pool.memset(mem["eps"][:, :], LN_EPS)
    return mem


def program(nc, A, out, layers=4):
    with ExitStack() as ctx:
        x1 = ctx.enter_context(nc.sbuf_tensor("x1", [P, TOK], F32))
        mem = shared_memory(nc, ctx, A)
        nc.scalar.preload_act_table_set("natural_log_exp_and_others")
        layer0(nc, mem, A, x1)
        if layers >= 2:
            layer1(nc, mem, A, x1)
        if layers >= 3:
            layer2(nc, mem, A, x1)
        if layers >= 4:
            layer3(nc, mem, A, x1)
        with stage(nc, "stored") as (block, s):
            @block.sync
            def _(sp):
                sp.dma_start(out, x1[:, :]).then_inc(s["stored"], 16)
                sp.wait_ge(s["stored"], 16)


def columns(v, n):
    return v.reshape(n, P).T


def layout(i):
    c = np.ascontiguousarray
    A = {}
    A["ident"] = np.eye(P, dtype=np.float32)
    A["x0"] = i["L0_attn_u"].transpose(2, 1, 0).reshape(P, TOK)
    order = [3, 2, 0, 1]
    w = np.concatenate([i["L0_attn_W_in"][:256], i["L0_attn_W_in"][256:768].reshape(4, P, P)[order].reshape(512, P),
                        np.repeat(i["L0_attn_W_in"][768:], 64, axis=0)], axis=0)
    A["w_in"] = w.reshape(8, P, P).transpose(2, 0, 1)
    w = np.concatenate([i["L0_attn_W_rxbc"].reshape(4, P, 256)[order].reshape(512, 256), np.repeat(i["L0_attn_W_rdt"], 64, axis=0)], axis=0)
    A["w_r"] = w.reshape(6 * P, 2, P).transpose(2, 1, 0)
    A["w_out"] = i["L0_attn_W_out"].reshape(P, 2, P).transpose(2, 1, 0)
    A["conv_w"] = i["L0_attn_conv_w"].reshape(4, P, 4)[order].transpose(1, 0, 2)
    A["conv_b"] = i["L0_attn_conv_b"].reshape(4, P)[order].T
    A["vec"] = np.concatenate([columns(np.repeat(i["L0_attn_" + n], 64), 2) for n in ("dt_bias", "A_log", "D_param")]
                              + [columns(i["L0_attn_norm_w"], 2)], axis=1)
    A["cent"] = i["L0_ffn_centroids"].T
    A["ln_g"] = i["L0_ffn_ln_g"].T
    A["ln_b"] = i["L0_ffn_ln_b"].T
    A["b1"] = i["L0_ffn_b1"].reshape(8, 4, P).transpose(2, 0, 1)
    A["b2"] = i["L0_ffn_b2"].T
    A["w1"] = i["L0_ffn_w1"].transpose(2, 0, 1)
    A["w2"] = i["L0_ffn_w2"].reshape(8, P, 4, P).transpose(3, 0, 2, 1)
    A["rank"] = np.broadcast_to((8.0 - np.arange(8)).astype(np.float32), (P, 4, 8))
    A["sel_e"] = np.broadcast_to(np.eye(8, dtype=np.float32)[:, :, None], (8, 8, P))
    A["bmask"] = (np.arange(P)[:, None] % 8 == np.arange(8)).astype(np.float32)
    A["hsel"] = (np.arange(P)[:, None] == 64 * np.arange(2)).astype(np.float32)
    layout_rest(i, A)
    return {n: c(a) for n, a in A.items()}


def kernel(**inputs):
    import concourse.bacc as bacc
    from concourse.bass_utils import run_bass_kernel_spmd

    arrays = layout({n: np.asarray(a) for n, a in inputs.items()})
    nc = bacc.Bacc("TRN2", target_bir_lowering=False, num_devices=1)
    A = {n: nc.dram_tensor(f"in_{n}", a.shape, mybir.dt.from_np(a.dtype), kind="ExternalInput").ap() for n, a in arrays.items()}
    out = nc.dram_tensor("out_x", (P, TOK), F32, kind="ExternalOutput").ap()
    program(nc, A, out)
    r = run_bass_kernel_spmd(nc, [{f"in_{n}": a for n, a in arrays.items()}], core_ids=[0])
    return r.results[0]["out_x"].reshape(P, NB, NT).transpose(1, 2, 0)
```

```python
from contextlib import ExitStack, contextmanager

import numpy as np
import concourse.bass as bass
from concourse import mybir

F32 = mybir.dt.float32
BF16 = mybir.dt.bfloat16
ACT = mybir.ActivationFunctionType
ALU = mybir.AluOpType
AX = mybir.AxisListType

P = 128
NB = 8
NT = 512
TOK = NB * NT
TB = 64
NBLK = NT // TB
CH = TB * NB
Q = 16
NCH = TB // Q
LN_EPS = 1e-5


@contextmanager
def stage(nc, *names):
    with ExitStack() as ctx:
        own = {n: ctx.enter_context(nc.semaphore(n)) for n in names}
        with nc.Block() as block:
            yield block, own
        numbers = sorted(s.num for s in own.values())
        first = 0
        for i in range(len(numbers)):
            if i + 1 == len(numbers) or numbers[i + 1] != numbers[i] + 1:
                nc.gpsimd.sem_clear(range(numbers[first], numbers[i] + 1))
                first = i + 1
        nc.all_engine_barrier()


def layernorm_stage(nc, mem, src, dst, chunks):
    xc, sq, rs, ps = mem["ln_xc"], mem["ln_sq"], mem["ln_rs"], mem["ps"]
    ones = mem["ones_mean"]
    n = len(chunks)
    with stage(nc, "mean_ready", "centred", "squared", "var_ready", "ln_done", "rstd_ready", "normed") as (block, s):
        @block.tensor
        def _(pe):
            def mean(k):
                if k >= 2:
                    pe.wait_ge(s["centred"], k - 1)
                pe.matmul(ps[k % 2][:, 0:CH], ones[:, :], src[:, chunks[k]], start=True, stop=True).then_inc(s["mean_ready"], 1)

            mean(0)
            for k in range(n):
                if k + 1 < n:
                    mean(k + 1)
                pe.wait_ge(s["squared"], k + 1)
                if k >= 2:
                    pe.wait_ge(s["ln_done"], k - 1)
                pe.matmul(ps[2 + k % 2][:, 0:CH], ones[:, :], sq[:, k % 2, :], start=True, stop=True).then_inc(s["var_ready"], 1)

        @block.scalar
        def _(act):
            for k in range(n):
                act.wait_ge(s["centred"], k + 1)
                if k >= 2:
                    act.wait_ge(s["var_ready"], k - 1)
                act.activation(sq[:, k % 2, :], xc[:, k % 2, :], ACT.Square).then_inc(s["squared"], 1)
                act.wait_ge(s["var_ready"], k + 1)
                if k >= 2:
                    act.wait_ge(s["normed"], k - 1)
                act.activation(rs[:, k % 2, :], ps[2 + k % 2][:, 0:CH], ACT.Ln, bias=mem["eps"][:, 0:1]).then_inc(s["ln_done"], 1)
                act.wait_ge(s["ln_done"], k + 1)
                act.activation(rs[:, k % 2, :], rs[:, k % 2, :], ACT.Exp, scale=-0.5).then_inc(s["rstd_ready"], 1)

        @block.vector
        def _(dve):
            for k in range(n + 1):
                if k < n:
                    dve.wait_ge(s["mean_ready"], k + 1)
                    if k >= 2:
                        dve.wait_ge(s["squared"], k - 1)
                        dve.wait_ge(s["normed"], k - 1)
                    dve.tensor_tensor(xc[:, k % 2, :], src[:, chunks[k]], ps[k % 2][:, 0:CH], ALU.subtract).then_inc(s["centred"], 1)
                if k >= 1:
                    j = k - 1
                    dve.wait_ge(s["rstd_ready"], j + 1)
                    dve.wait_ge(s["centred"], j + 1)
                    dve.tensor_tensor(dst[:, chunks[j]], xc[:, j % 2, :], rs[:, j % 2, :], ALU.mult).then_inc(s["normed"], 1)


def layer0(nc, mem, A, x1):
    NE = 8
    FT = 4
    with ExitStack() as ctx:
        def sb(name, shape, dt=F32):
            return ctx.enter_context(nc.sbuf_tensor(name, shape, dt))

        ps = mem["ps"]
        w_in = sb("w_in", [P, 8, P])
        w_r = sb("w_r", [P, 2, 6 * P])
        w_rs = sb("w_rs", [P, 2, 3, 6 * P], BF16)
        w_out = sb("w_out", [P, 2, P])
        conv_w = sb("conv_w", [P, 4, 4])
        conv_b = sb("conv_b", [P, 4])
        vec = sb("vec", [P, 8])
        a_col = sb("a_col", [P, 2])
        dtb = sb("dtb", [P, 2, NB])
        d_b = sb("d_b", [P, 2, NB])
        a_b = sb("a_b", [P, 2, NB])
        zero16 = sb("zero16", [P, 2 * NB])
        cent = sb("cent", [P, NE])
        ln_g = sb("ln_g", [P, NE])
        ln_b = sb("ln_b", [P, NE])
        b1 = sb("b1", [P, NE, FT])
        b2 = sb("b2", [P, NE])
        w1 = sb("w1", [P, NE, FT * P])
        w2 = sb("w2", [P, NE, FT, P])
        rank = sb("rank", [P, 4, NE])
        bmask = sb("bmask", [P, NB])
        hsel = sb("hsel", [P, 2])

        x0 = sb("x0", [P, CH])
        xn = sb("xn", [P, CH])
        xh = sb("xh", [P, CH])
        zs = sb("zs", [P, 2, CH + Q * NB])
        raw = sb("raw", [P, 4, 3 * NB + CH])
        pin = sb("pin", [P, 6, CH + Q * NB])
        gff = sb("gff", [P, CH])
        yb = sb("yb", [P, 2, CH])

        aff = sb("aff", [P, 4, NE])
        affx = sb("affx", [P, 4])
        ea = sb("ea", [P, 4, NE])
        key = sb("key", [P, 4, NE])
        coef = sb("coef", [P, 4, NE])
        coefT = sb("coefT", [NE, CH])
        w1c, w2c = sb("w1c", [P, 2, FT * P]), sb("w2c", [P, 2, FT, P])
        b1c, b2c, cbc = sb("b1c", [P, 2, FT]), sb("b2c", [P, 2]), sb("cbc", [P, 2, CH])
        hb = sb("hb", [P, FT, CH])
        w_res = hb[:, 0:3, :].rearrange("p f c -> p (f c)").rearrange("p (h c) -> p h c", h=2)
        tmp = sb("tmp", [P, CH])
        sg = sb("sg", [P, CH])

        S = sb("S", [P, NB, 2, P])
        Ss = sb("Ss", [P, 3, NB, 2, P], BF16)
        Sr = sb("Sr", [P, NB, 2, P])
        V = sb("V", [P, 6, Q, NB])
        Wh = sb("Wh", [P, 2, Q, NB])
        Pc = sb("Pc", [P, 2, NB])
        G = sb("G", [P, 2, NB])
        Gs = sb("Gs", [P, 2, 3, NB], BF16)
        Gr = sb("Gr", [P, 2, 2, NB])
        Gq = sb("Gq", [P, 2, NB])
        Gq1 = sb("Gq1", [P, NB])
        rs = sb("rs", [P, NB])
        pre = sb("pre", [P, 6, NB])
        e48 = sb("e48", [P, 6, NB])
        r48 = sb("r48", [P, 6, NB])
        Cs = sb("Cs", [P, 3, NB], BF16)
        Cr = sb("Cr", [P, 2, NB])
        CB = sb("CB", [P, Q, NB])
        prod = sb("prod", [P, 2, Q + 1, NB])
        small = {k: sb(k, [P, 2, NB]) for k in ("w", "wa", "wm", "dt", "dA", "dta", "dtz", "dtzx", "R")}
        zz, zzd = sb("zz", [P, 2, 2, NB]), sb("zzd", [P, 2, 2, NB])
        gt = sb("gt", [P, 2, NB, 6])
        pinc = sb("pinc", [P, 6, Q, NB])
        zc = sb("zc", [P, 2, Q, NB])
        zdc = sb("zdc", [P, 2, Q, NB])
        yc = sb("yc", [P, 2, Q, NB])
        bT = sb("bT", [P, P])
        wT = sb("wT", [P, NB, 2, P])
        Psel = sb("Psel", [P, 4, NB])
        pd = sb("pd", [P, NB, 4])

        with stage(nc, "loaded", "w_scaled", "split", "bias_mm", "prep", "expd") as (block, s):
            loads = [(w_in[:, :, :], A["w_in"]), (w_r[:, :, :], A["w_r"]), (w_out[:, :, :], A["w_out"]),
                     (conv_w[:, :, :], A["conv_w"]), (conv_b[:, :], A["conv_b"]), (vec[:, :], A["vec"]),
                     (cent[:, :], A["cent"]), (ln_g[:, :], A["ln_g"]), (ln_b[:, :], A["ln_b"]),
                     (b1[:, :, :], A["b1"]), (b2[:, :], A["b2"]), (w1[:, :, :], A["w1"]), (w2[:, :, :, :], A["w2"]),
                     (rank[:, :, :], A["rank"]), (bmask[:, :], A["bmask"]),
                     (hsel[:, :], A["hsel"])]
            n_loads = 16 * len(loads)

            @block.sync
            def _(sp):
                for dst, src in loads:
                    sp.dma_start(dst, src).then_inc(s["loaded"], 16)

            @block.gpsimd
            def _(pool):
                pool.memset(raw[:, :, 0:3 * NB], 0.0)
                pool.memset(zs[:, :, CH:], 0.0)
                pool.memset(pin[:, :, CH:], 0.0)
                pool.memset(S[:, :, :, :], 0.0)
                pool.memset(Ss[:, :, :, :, :], 0.0)
                pool.memset(Gs[:, :, :, :], 0.0)
                pool.memset(zero16[:, :], 0.0)
                pool.memset(rs[:, :], 0.0).then_inc(s["prep"], 1)

            @block.scalar
            def _(act):
                act.wait_ge(s["loaded"], n_loads)
                act.activation(a_col[:, :], vec[:, 2:4], ACT.Exp).then_inc(s["expd"], 1)

            @block.vector
            def _(dve):
                dve.wait_ge(s["loaded"], n_loads)
                dve.wait_ge(s["prep"], 1)
                dve.wait_ge(s["expd"], 1)
                for h in range(2):
                    z8 = zero16[:, 0:NB]
                    dve.tensor_scalar(dtb[:, h, :], z8, vec[:, h:h + 1], None, ALU.add)
                    dve.tensor_scalar(a_b[:, h, :], z8, a_col[:, h:h + 1], -1.0, ALU.add, ALU.mult)
                    dve.tensor_scalar(d_b[:, h, :], z8, vec[:, 4 + h:5 + h], None, ALU.add)
                    dve.tensor_scalar(w_r[:, h, :], w_r[:, h, :], vec[:, 6 + h:7 + h], None, ALU.mult)
                    dve.tensor_scalar(w_out[:, h, :], w_out[:, h, :], vec[:, 6 + h:7 + h], None, ALU.mult).then_inc(s["w_scaled"], 1)
                dve.wait_ge(s["w_scaled"], 2)
                dve.tensor_copy(w_rs[:, :, 0, :], w_r[:, :, :]).then_inc(s["split"], 1)
                dve.wait_ge(s["split"], 1)
                dve.tensor_tensor(w_res, w_r[:, :, :], w_rs[:, :, 0, :], ALU.subtract).then_inc(s["split"], 1)
                dve.wait_ge(s["split"], 2)
                dve.tensor_copy(w_rs[:, :, 1, :], w_res).then_inc(s["split"], 1)
                dve.wait_ge(s["split"], 3)
                dve.tensor_tensor(w_rs[:, :, 2, :], w_res, w_rs[:, :, 1, :], ALU.subtract).then_inc(s["split"], 1)
                dve.wait_ge(s["bias_mm"], 1)
                dve.tensor_tensor(b1[:, :, :], b1[:, :, :], ps[0][:, 0:NE * FT].rearrange("p (e f) -> p e f", e=NE), ALU.add)
                for e in range(NE):
                    dve.tensor_scalar(w1[:, e, :], w1[:, e, :], ln_g[:, e:e + 1], None, ALU.mult)

            @block.tensor
            def _(pe):
                pe.wait_ge(s["loaded"], n_loads)
                for e in range(NE):
                    for f in range(FT):
                        last = pe.matmul(ps[0][:, e * FT + f:e * FT + f + 1], w1[:, e, f * P:(f + 1) * P], ln_b[:, e:e + 1],
                                         start=True, stop=True)
                last.then_inc(s["bias_mm"], 1)

        coef_dram = nc.dram_tensor("moe_coef", (NE, CH), F32, kind="Internal").ap()
        with nc.Fori(0, NBLK) as blk:
            with stage(nc, "x_loaded") as (block, s):
                @block.sync
                def _(sp):
                    sp.dma_start(x0[:, :], A["x0"][:, bass.ts(blk, CH)]).then_inc(s["x_loaded"], 16)
                    sp.wait_ge(s["x_loaded"], 16)
            layernorm_stage(nc, mem, x0, xn, [slice(0, CH)])

            with stage(nc, "projected", "moved", "ez", "z1", "z2", "conv") as (block, s):
                ORDER = (2, 3, 4, 5, 0, 1, 6, 7)

                def projected(engine, m):
                    engine.wait_ge(s["projected"], ORDER.index(m) + 1)

                @block.tensor
                def _(pe):
                    for m in ORDER:
                        pe.matmul(ps[m][:, 0:CH], w_in[:, m, :], xn[:, :], start=True, stop=True).then_inc(s["projected"], 1)

                @block.scalar
                def _(act):
                    for m in range(2, 6):
                        projected(act, m)
                        act.activation(raw[:, m - 2, 3 * NB:], ps[m][:, 0:CH], ACT.Copy).then_inc(s["moved"], 1)
                    for m in range(2):
                        projected(act, m)
                        act.activation(zs[:, m, 0:CH], ps[m][:, 0:CH], ACT.Exp, scale=-1.0).then_inc(s["ez"], 1)
                    for m in range(6, 8):
                        projected(act, m)
                        act.activation(pin[:, m - 2, 0:CH], ps[m][:, 0:CH], ACT.Copy)

                @block.gpsimd
                def _(pool):
                    for m in range(2):
                        pool.wait_ge(s["ez"], m + 1)
                        pool.tensor_scalar(zs[:, m, 0:CH], zs[:, m, 0:CH], 1.0, None, ALU.add).then_inc(s["z1"], 1)

                @block.vector
                def _(dve):
                    for pair in ((0, 1), (2, 3)):
                        for m in pair:
                            dve.wait_ge(s["moved"], m + 1)
                            dve.tensor_scalar(pin[:, m, 0:CH], raw[:, m, 0:CH], conv_w[:, m, 0:1], conv_b[:, m:m + 1],
                                              ALU.mult, ALU.add).then_inc(s["conv"], 1)
                        for k in range(1, 4):
                            for m in pair:
                                dve.wait_ge(s["conv"], 8 * (pair[0] // 2) + 2 * k - 1 + m % 2)
                                dve.scalar_tensor_tensor(pin[:, m, 0:CH], raw[:, m, k * NB:k * NB + CH], conv_w[:, m, k:k + 1],
                                                         pin[:, m, 0:CH], ALU.mult, ALU.add).then_inc(s["conv"], 1)
                    for m in range(2):
                        dve.wait_ge(s["z1"], m + 1)
                        dve.reciprocal(zs[:, m, 0:CH], zs[:, m, 0:CH]).then_inc(s["z2"], 1)
                    dve.tensor_copy(raw[:, :, 0:3 * NB], raw[:, :, CH:CH + 3 * NB])
                    for m in range(2):
                        dve.wait_ge(s["z2"], m + 1)
                        dve.tensor_tensor(zs[:, m, 0:CH], ps[m][:, 0:CH], zs[:, m, 0:CH], ALU.mult)

            with stage(nc, "aff_mm", "ea_done", "a1", "a2", "mx", "eq", "k2", "oh", "coef_done", "ct_mm", "ct_done", "stored",
                       "mean_mm", "centred", "squared", "var_mm", "ln_done", "rstd_done") as (block, s):
                xc, sq, rstd = mem["ln_xc"][:, 0, :], mem["ln_sq"][:, 0, :], mem["ln_rs"][:, 0, :]

                @block.tensor
                def _(pe):
                    for t in range(4):
                        last = pe.matmul(ps[0][:, t * NE:(t + 1) * NE], xn[:, t * P:(t + 1) * P], cent[:, :], start=True, stop=True)
                    last.then_inc(s["aff_mm"], 1)
                    pe.matmul(ps[1][:, 0:CH], mem["ones_mean"][:, :], xn[:, :], start=True, stop=True).then_inc(s["mean_mm"], 1)
                    pe.wait_ge(s["squared"], 1)
                    pe.matmul(ps[2][:, 0:CH], mem["ones_mean"][:, :], sq, start=True, stop=True).then_inc(s["var_mm"], 1)
                    pe.wait_ge(s["coef_done"], 1)
                    for t in range(4):
                        last = pe.transpose(ps[7][0:NE, t * P:(t + 1) * P], coef[:, t, :], mem["ident"][:, :])
                    last.then_inc(s["ct_mm"], 1)

                @block.scalar
                def _(act):
                    act.wait_ge(s["a1"], 1)
                    act.activation(ea[:, :, :], aff[:, :, :], ACT.Exp, scale=-1.0).then_inc(s["ea_done"], 1)
                    act.wait_ge(s["centred"], 1)
                    act.activation(sq, xc, ACT.Square).then_inc(s["squared"], 1)
                    act.wait_ge(s["var_mm"], 1)
                    act.activation(rstd, ps[2][:, 0:CH], ACT.Ln, bias=mem["eps"][:, 0:1]).then_inc(s["ln_done"], 1)
                    act.wait_ge(s["ln_done"], 1)
                    act.activation(rstd, rstd, ACT.Exp, scale=-0.5).then_inc(s["rstd_done"], 1)

                @block.sync
                def _(sp):
                    sp.wait_ge(s["ct_done"], 1)
                    sp.dma_start(coef_dram, coefT[:, :]).then_inc(s["stored"], 16)
                    sp.wait_ge(s["stored"], 16)

                @block.gpsimd
                def _(pool):
                    pool.tensor_copy(gff[:, :], xn[:, :])

                @block.vector
                def _(dve):
                    dve.wait_ge(s["aff_mm"], 1)
                    dve.tensor_copy(aff[:, :, :], ps[0][:, 0:4 * NE].rearrange("p (t e) -> p t e", t=4)).then_inc(s["a1"], 1)
                    dve.wait_ge(s["mean_mm"], 1)
                    dve.tensor_tensor(xc, xn[:, :], ps[1][:, 0:CH], ALU.subtract).then_inc(s["centred"], 1)
                    dve.wait_ge(s["ea_done"], 1)
                    dve.tensor_scalar(ea[:, :, :], ea[:, :, :], 1.0, None, ALU.add).then_inc(s["a2"], 1)
                    dve.wait_ge(s["a1"], 1)
                    dve.tensor_reduce(affx[:, :], aff[:, :, :], AX.X, ALU.max).then_inc(s["mx"], 1)
                    dve.wait_ge(s["mx"], 1)
                    dve.tensor_tensor(key[:, :, :], aff[:, :, :], affx[:, :, None].to_broadcast([P, 4, NE]), ALU.is_equal).then_inc(s["eq"], 1)
                    dve.wait_ge(s["a2"], 1)
                    dve.reciprocal(ea[:, :, :], ea[:, :, :]).then_inc(s["a2"], 1)
                    dve.wait_ge(s["eq"], 1)
                    dve.tensor_tensor(key[:, :, :], key[:, :, :], rank[:, :, :], ALU.mult).then_inc(s["k2"], 1)
                    dve.wait_ge(s["k2"], 1)
                    dve.tensor_reduce(affx[:, :], key[:, :, :], AX.X, ALU.max).then_inc(s["k2"], 1)
                    dve.wait_ge(s["k2"], 2)
                    dve.tensor_tensor(key[:, :, :], key[:, :, :], affx[:, :, None].to_broadcast([P, 4, NE]), ALU.is_equal).then_inc(s["oh"], 1)
                    dve.wait_ge(s["oh"], 1)
                    dve.wait_ge(s["a2"], 2)
                    dve.tensor_tensor(coef[:, :, :], key[:, :, :], ea[:, :, :], ALU.mult).then_inc(s["coef_done"], 1)
                    dve.wait_ge(s["ct_mm"], 1)
                    dve.tensor_copy(coefT[:, :], ps[7][0:NE, 0:CH]).then_inc(s["ct_done"], 1)
                    dve.wait_ge(s["centred"], 1)
                    dve.wait_ge(s["rstd_done"], 1)
                    dve.tensor_tensor(xh[:, :], xc, rstd, ALU.mult)

            with stage(nc) as (block, s):
                @block.gpsimd
                def _(pool):
                    chunk_z(zs, zc, 0)(pool)

                @block.scalar
                def _(act):
                    chunk_pre(pin, pinc, 0)(act)

                @block.vector
                def _(dve):
                    chunk_zd(zs, d_b, zdc, 0)(dve)

            with nc.Fori(0, NCH) as chunk:
                scan_chunk(nc, mem, dict(w_rs=w_rs, S=S, Ss=Ss, Sr=Sr, V=V, Wh=Wh, Pc=Pc, G=G, Gs=Gs, Gr=Gr, Gq=Gq,
                                         rs=rs, pre=pre, e48=e48, r48=r48, Cs=Cs, Cr=Cr, CB=CB, prod=prod, gt=gt,
                                         bT=bT, wT=wT, Psel=Psel, zs=zs, pin=pin, pd=pd, pinc=pinc, zc=zc, zdc=zdc, yc=yc, a_b=a_b, zz=zz, zzd=zzd, Gq1=Gq1,
                                         dtb=dtb, d_b=d_b, bmask=bmask, hsel=hsel, **small),
                           dict(w1=w1, w2=w2, b1=b1, b2=b2, w1c=w1c, w2c=w2c, b1c=b1c, b2c=b2c, cbc=cbc, hb=hb, tmp=tmp, xh=xh, gff=gff,
                                coef_dram=coef_dram), yb, chunk)

            with stage(nc, "out_mm", "e_done", "d_done", "r_done", "scaled", "gated") as (block, s):
                @block.tensor
                def _(pe):
                    for h in range(2):
                        last = pe.matmul(ps[0][:, 0:CH], w_out[:, h, :], yb[:, h, :], start=(h == 0), stop=(h == 1))
                    last.then_inc(s["out_mm"], 1)

                @block.scalar
                def _(act):
                    act.activation(sg[:, :], gff[:, :], ACT.Exp, scale=-1.0).then_inc(s["e_done"], 1)

                @block.vector
                def _(dve):
                    dve.wait_ge(s["e_done"], 1)
                    dve.tensor_scalar(sg[:, :], sg[:, :], 1.0, None, ALU.add).then_inc(s["d_done"], 1)
                    dve.wait_ge(s["out_mm"], 1)
                    dve.tensor_tensor(gff[:, :], ps[0][:, 0:CH], gff[:, :], ALU.mult).then_inc(s["scaled"], 1)
                    dve.wait_ge(s["d_done"], 1)
                    dve.reciprocal(sg[:, :], sg[:, :]).then_inc(s["r_done"], 1)
                    dve.wait_ge(s["scaled"], 1)
                    dve.wait_ge(s["r_done"], 1)
                    dve.tensor_tensor(gff[:, :], gff[:, :], sg[:, :], ALU.mult).then_inc(s["gated"], 1)
                    dve.wait_ge(s["gated"], 1)
                    v = lambda a: a[:, :].rearrange("p (t b) -> p b t", b=NB)
                    dve.tensor_tensor(x1[:, :].rearrange("p (b t) -> p b t", b=NB)[:, :, bass.ts(blk, TB)], v(gff), v(x0), ALU.add)


def chunk_columns(chunk):
    return bass.ds(chunk * (Q * NB), Q * NB)


def chunk_z(zs, zc, chunk):
    return lambda pool: pool.tensor_copy(zc[:, :, :, :].rearrange("p m t b -> p m (t b)"), zs[:, :, chunk_columns(chunk)])


def chunk_zd(zs, d_b, zdc, chunk):
    return lambda dve: dve.tensor_tensor(zdc[:, :, :, :], zs[:, :, chunk_columns(chunk)].rearrange("p m (t b) -> p m t b", b=NB),
                                         d_b[:, :, None, :].to_broadcast([P, 2, Q, NB]), ALU.mult)


def chunk_pre(pin, pinc, chunk):
    return lambda act: act.activation(pinc[:, :, :, :].rearrange("p m t b -> p m (t b)"), pin[:, :, chunk_columns(chunk)], ACT.Copy)


def scan_chunk(nc, mem, m, x, yb, chunk):
    load_chunk_z = chunk_z(m["zs"], m["zc"], chunk + 1)
    load_chunk_pre = chunk_pre(m["pin"], m["pinc"], chunk + 1)
    load_chunk_zd = chunk_zd(m["zs"], m["d_b"], m["zdc"], chunk + 1)
    ps, ones = mem["ps"], mem["ones"]
    Ss, Gs, V, Wh, Pc, G = m["Ss"], m["Gs"], m["V"], m["Wh"], m["Pc"], m["G"]
    pre, e48, r48, rs, pinc, zc, yc = m["pre"], m["e48"], m["r48"], m["rs"], m["pinc"], m["zc"], m["yc"]
    C_T, B_T, X_T, D_T = 0, 1, slice(2, 4), slice(4, 6)
    CB_T = slice(0, 2)
    w_bank, x_bank, u_bank, dot_bank, ms_bank, d_bank = ps[0], ps[1], ps[2], ps[3], ps[4], ps[5]

    with stage(nc, "sq_each", "sq_done", "g_split", "wcb_mm", "wd_mm", "wx_mm", "ms_mm", "lnms", "rs_done", "cb_sum", "cb_mul",
               "cb_pre", "cb_exp", "cb_one", "cb_rec", "c_ready", "c_rest", "c_split", "d_sum", "d_mul", "d_pre", "d_exp",
               "d_one", "d_rec", "d_act", "x_sum", "x_mul", "x_pre", "x_exp", "x_one", "x_rec", "x_act", "cb_prod", "dots_mm",
               "u_mm", "w_done", "wabs", "wexp", "dt_parts", "dt_done", "dta", "da_done", "dtz", "dtzx", "dx",
               "zz_done", "past_in", "hist", "prod", "g_terms", "g_done", "g_high", "g_rest", "yn_done",
               "x_loaded", "up_mm", "h_done", "down_mm", "moved", "weighted", "summed") as (block, s):
        FT = 4
        UP_STEPS = (range(1, 5), range(8, 12))
        DOWN_STEPS = (range(5, 8), range(12, 16))
        MOVE_STEPS = (8, 15)
        up_bank, down_bank = ps[6], ps[7]
        x_loads = [(x["w1c"][:, :, :], x["w1"][:, bass.ds(chunk * 2, 2), :]), (x["w2c"][:, :, :, :], x["w2"][:, bass.ds(chunk * 2, 2), :, :]),
                   (x["b1c"][:, :, :], x["b1"][:, bass.ds(chunk * 2, 2), :]), (x["b2c"][:, :], x["b2"][:, bass.ds(chunk * 2, 2)])]
        rows = x["coef_dram"][bass.ds(chunk * 2, 2), :]
        x_loads.append((x["cbc"][:, :, :], bass.AP(rows.tensor, rows.offset, [[0, P], [CH, 2], [1, CH]])))
        n_x_loads = 16 * len(x_loads)

        def is_up(t):
            for e in range(2):
                if t in UP_STEPS[e]:
                    return e, t - UP_STEPS[e][0]
            return None

        @block.sync
        def _(sp):
            for dst, src in x_loads:
                sp.dma_start(dst, src).then_inc(s["x_loaded"], 16)

        @block.tensor
        def _(pe):
            def mean_square(n):
                pe.wait_ge(s["sq_done"], n)
                pe.matmul(ms_bank[:, 0:NB], ones[:, :], m["Gq1"][:, :], start=True, stop=True).then_inc(s["ms_mm"], 1)

            def recurrent(bank, tiles, sem):
                for n, j in enumerate(tiles):
                    for part in range(3):
                        for h in range(2):
                            last = pe.matmul(bank[:, n * 24:(n + 1) * 24], m["w_rs"][:, h, part, j * P:(j + 1) * P],
                                             Gs[:, h, :, :].rearrange("p c b -> p (c b)"),
                                             start=(part == 0 and h == 0), stop=(part == 2 and h == 1))
                last.then_inc(sem, 1)

            def state(batches):
                for b in batches:
                    for h in range(2):
                        for part in range(3):
                            last = pe.matmul(u_bank[:, (h * NB + b) * 3:(h * NB + b) * 3 + 3], Ss[:, part, b, h, :],
                                             m["Cs"][:, :, b], start=(part == 0), stop=(part == 2))
                return last

            def down(e, f):
                pe.wait_ge(s["h_done"], FT * e + f + 1)
                if e == 1 and f == 0:
                    pe.wait_ge(s["moved"], 1)
                pe.matmul(down_bank[:, 0:CH], x["w2c"][:, e, f, :], x["hb"][:, f, :], start=(f == 0), stop=(f == FT - 1)).then_inc(s["down_mm"], 1)

            def mixture(t):
                if t == UP_STEPS[0][0]:
                    pe.wait_ge(s["x_loaded"], n_x_loads)
                if is_up(t):
                    e, f = is_up(t)
                    if FT * e + f:
                        pe.wait_ge(s["h_done"], FT * e + f)
                    pe.matmul(up_bank[:, 0:CH], x["w1c"][:, e, f * P:(f + 1) * P], x["xh"][:, :], start=True, stop=True).then_inc(s["up_mm"], 1)
                for e in range(2):
                    if t in DOWN_STEPS[e]:
                        down(e, t - DOWN_STEPS[e][0])

            for t in range(Q):
                if t >= 1:
                    mean_square(t)
                    pe.wait_ge(s["g_split"], t)
                recurrent(w_bank, (0, 1), s["wcb_mm"])
                recurrent(d_bank, (4, 5), s["wd_mm"])
                recurrent(x_bank, (2, 3), s["wx_mm"])
                mixture(t)
                pe.wait_ge(s["c_split"], t + 1)
                state(range(2))
                pe.wait_ge(s["cb_prod"], t + 1)
                pe.matmul(dot_bank[:, 0:(t + 1) * NB], ones[:, :], m["CB"][:, 0:t + 1, :].rearrange("p s b -> p (s b)"),
                          start=True, stop=True).then_inc(s["dots_mm"], 1)
                state(range(2, NB)).then_inc(s["u_mm"], 1)
                if t == DOWN_STEPS[0][-1]:
                    down(0, FT - 1)
            mean_square(Q)

        @block.scalar
        def _(act):
            def rstd(n):
                act.wait_ge(s["g_done"], n)
                act.activation(m["Gq"][:, :, :], G[:, :, :], ACT.Square).then_inc(s["sq_each"], 1)
                act.wait_ge(s["ms_mm"], n)
                act.activation(rs[:, :], ms_bank[:, 0:NB], ACT.Ln, bias=mem["eps"][:, 0:1], scale=1.0 / (2 * P)).then_inc(s["lnms"], 1)
                act.wait_ge(s["lnms"], n)
                act.activation(rs[:, :], rs[:, :], ACT.Exp, scale=-0.5).then_inc(s["rs_done"], 1)

            def move(e):
                act.wait_ge(s["down_mm"], FT * (e + 1))
                if e:
                    act.wait_ge(s["weighted"], e)
                act.activation(x["tmp"][:, :], down_bank[:, 0:CH], ACT.Identity, bias=x["b2c"][:, e:e + 1]).then_inc(s["moved"], 1)

            wa = m["wa"]
            for t in range(Q):
                if t >= 1:
                    rstd(t)
                act.wait_ge(s["cb_pre"], t + 1)
                act.activation(e48[:, CB_T, :], pre[:, CB_T, :], ACT.Exp, scale=-1.0).then_inc(s["cb_exp"], 1)
                act.wait_ge(s["d_pre"], t + 1)
                act.activation(e48[:, D_T, :], pre[:, D_T, :], ACT.Exp, scale=-1.0).then_inc(s["d_exp"], 1)
                if t == MOVE_STEPS[0]:
                    move(0)
                act.wait_ge(s["w_done"], t + 1)
                act.activation(wa[:, :, :], m["w"][:, :, :], ACT.Abs).then_inc(s["wabs"], 1)
                act.activation(m["wm"][:, :, :], m["w"][:, :, :], ACT.Relu).then_inc(s["dt_parts"], 1)
                act.wait_ge(s["wabs"], t + 1)
                act.activation(wa[:, :, :], wa[:, :, :], ACT.Exp, scale=-1.0).then_inc(s["wexp"], 1)
                act.wait_ge(s["x_pre"], t + 1)
                act.activation(e48[:, X_T, :], pre[:, X_T, :], ACT.Exp, scale=-1.0).then_inc(s["x_exp"], 1)
                act.wait_ge(s["wexp"], t + 1)
                act.activation(wa[:, :, :], wa[:, :, :], ACT.Ln, bias=1.0).then_inc(s["dt_parts"], 1)
                act.wait_ge(s["dta"], t + 1)
                act.activation(m["dA"][:, :, :], m["dta"][:, :, :], ACT.Exp).then_inc(s["da_done"], 1)
                if is_up(t):
                    e, f = is_up(t)
                    act.wait_ge(s["up_mm"], FT * e + f + 1)
                    if e:
                        act.wait_ge(s["down_mm"], FT)
                    act.activation(x["hb"][:, f, :], up_bank[:, 0:CH], ACT.Relu, bias=x["b1c"][:, e, f:f + 1]).then_inc(s["h_done"], 1)
                if t == MOVE_STEPS[1]:
                    move(1)
            rstd(Q)

        @block.gpsimd
        def _(pool):
            def add_expert(e):
                pool.wait_ge(s["moved"], e + 1)
                pool.tensor_tensor(x["cbc"][:, e, :], x["cbc"][:, e, :], x["tmp"][:, :], ALU.mult).then_inc(s["weighted"], 1)
                pool.wait_ge(s["weighted"], e + 1)
                pool.tensor_tensor(x["gff"][:, :], x["gff"][:, :], x["cbc"][:, e, :], ALU.add).then_inc(s["summed"], 1)

            dt, dA, dtz, dtzx, zz = (m[k] for k in ("dt", "dA", "dtz", "dtzx", "zz"))
            for t in range(Q):
                if t >= 1:
                    pool.wait_ge(s["past_in"], 2 * t)
                pool.tensor_copy(zz[:, 0, :, :], zc[:, :, t, :])
                if t >= 1:
                    pool.wait_ge(s["hist"], t)
                    pool.tensor_tensor(zz[:, 1, :, :], zc[:, :, t, :], Pc[:, :, :], ALU.mult).then_inc(s["zz_done"], 1)
                else:
                    pool.tensor_copy(zz[:, 1, :, :], zc[:, :, t, :]).then_inc(s["zz_done"], 1)
                if t == MOVE_STEPS[0] + 1:
                    add_expert(0)
                pool.wait_ge(s["dt_done"], t + 1)
                pool.tensor_tensor(dtz[:, :, :], dt[:, :, :], zc[:, :, t, :], ALU.mult).then_inc(s["dtz"], 1)
                pool.wait_ge(s["dtz"], t + 1)
                pool.wait_ge(s["x_act"], t + 1)
                pool.tensor_tensor(dtzx[:, :, :], V[:, X_T, t, :], dtz[:, :, :], ALU.mult).then_inc(s["dtzx"], 1)
                pool.tensor_tensor(m["gt"][:, :, :, 5], V[:, X_T, t, :], m["zdc"][:, :, t, :], ALU.mult).then_inc(s["g_terms"], 1)
                pool.tensor_tensor(Wh[:, :, t, :], dt[:, :, :], V[:, X_T, t, :], ALU.mult).then_inc(s["dx"], 1)
                pool.wait_ge(s["da_done"], t + 1)
                if t >= 1:
                    pool.tensor_tensor(Pc[:, :, :], Pc[:, :, :], dA[:, :, :], ALU.mult)
                    pool.wait_ge(s["prod"], t)
                    pool.tensor_tensor(Wh[:, :, 0:t, :], Wh[:, :, 0:t, :], dA[:, :, :][:, :, None, :].to_broadcast([P, 2, t, NB]),
                                       ALU.mult).then_inc(s["hist"], 1)
                else:
                    pool.tensor_copy(Pc[:, :, :], dA[:, :, :]).then_inc(s["hist"], 1)
            add_expert(1)

        @block.vector
        def _(dve):
            Cs, Cr, CB = m["Cs"], m["Cr"], m["CB"]
            gt, Gr = m["gt"], m["Gr"]
            W2 = [P, 2, NB]
            rsb = rs[:, None, :].to_broadcast(W2)

            def summed(bank, out):
                return dve.tensor_reduce(out, bank[:, 0:48].rearrange("p (m c b) -> p m b c", m=2, c=3), AX.X, ALU.add)

            for t in range(Q):
                dve.wait_ge(s["wcb_mm"], t + 1)
                summed(w_bank, pre[:, CB_T, :]).then_inc(s["cb_sum"], 1)
                dve.wait_ge(s["cb_sum"], t + 1)
                if t >= 1:
                    dve.wait_ge(s["rs_done"], t)
                dve.tensor_tensor(pre[:, CB_T, :], pre[:, CB_T, :], rsb, ALU.mult).then_inc(s["cb_mul"], 1)
                dve.wait_ge(s["wd_mm"], t + 1)
                summed(d_bank, pre[:, D_T, :]).then_inc(s["d_sum"], 1)
                dve.wait_ge(s["cb_mul"], t + 1)
                dve.tensor_tensor(pre[:, CB_T, :], pre[:, CB_T, :], pinc[:, CB_T, t, :], ALU.add).then_inc(s["cb_pre"], 1)
                dve.wait_ge(s["d_sum"], t + 1)
                dve.tensor_tensor(pre[:, D_T, :], pre[:, D_T, :], rsb, ALU.mult).then_inc(s["d_mul"], 1)
                if t >= 1:
                    dve.tensor_tensor(yc[:, :, t - 1, :], G[:, :, :], rsb, ALU.mult).then_inc(s["yn_done"], 1)
                dve.wait_ge(s["d_mul"], t + 1)
                dve.tensor_tensor(pre[:, D_T, :], pre[:, D_T, :], pinc[:, D_T, t, :], ALU.add).then_inc(s["d_pre"], 1)
                dve.wait_ge(s["cb_exp"], t + 1)
                dve.tensor_scalar(r48[:, CB_T, :], e48[:, CB_T, :], 1.0, None, ALU.add).then_inc(s["cb_one"], 1)
                dve.wait_ge(s["wx_mm"], t + 1)
                summed(x_bank, pre[:, X_T, :]).then_inc(s["x_sum"], 1)
                dve.wait_ge(s["cb_one"], t + 1)
                dve.reciprocal(r48[:, CB_T, :], r48[:, CB_T, :]).then_inc(s["cb_rec"], 1)
                dve.wait_ge(s["d_exp"], t + 1)
                dve.tensor_scalar(r48[:, D_T, :], e48[:, D_T, :], 1.0, None, ALU.add).then_inc(s["d_one"], 1)
                dve.wait_ge(s["cb_rec"], t + 1)
                dve.tensor_tensor(Cs[:, 0, :], pre[:, C_T, :], r48[:, C_T, :], ALU.mult).then_inc(s["c_ready"], 1)
                dve.tensor_tensor(V[:, CB_T, t, :], pre[:, CB_T, :], r48[:, CB_T, :], ALU.mult).then_inc(s["c_ready"], 1)
                dve.wait_ge(s["d_one"], t + 1)
                dve.reciprocal(r48[:, D_T, :], r48[:, D_T, :]).then_inc(s["d_rec"], 1)
                dve.wait_ge(s["c_ready"], 2 * t + 2)
                dve.tensor_tensor(Cs[:, 1, :], V[:, C_T, t, :], Cs[:, 0, :], ALU.subtract).then_inc(s["c_rest"], 1)
                dve.tensor_tensor(Cr[:, 0, :], V[:, C_T, t, :], Cs[:, 0, :], ALU.subtract).then_inc(s["c_rest"], 1)
                dve.wait_ge(s["d_rec"], t + 1)
                dve.tensor_tensor(V[:, D_T, t, :], pre[:, D_T, :], r48[:, D_T, :], ALU.mult).then_inc(s["d_act"], 1)
                dve.wait_ge(s["c_rest"], 2 * t + 2)
                dve.tensor_tensor(Cs[:, 2, :], Cr[:, 0, :], Cs[:, 1, :], ALU.subtract).then_inc(s["c_split"], 1)
                dve.wait_ge(s["d_act"], t + 1)
                dve.tensor_tensor(m["w"][:, :, :], V[:, D_T, t, :], m["dtb"][:, :, :], ALU.add).then_inc(s["w_done"], 1)
                dve.tensor_tensor(CB[:, 0:t + 1, :], V[:, B_T, 0:t + 1, :], V[:, C_T, t, :][:, None, :].to_broadcast([P, t + 1, NB]),
                                  ALU.mult).then_inc(s["cb_prod"], 1)
                dve.wait_ge(s["zz_done"], t + 1)
                dve.wait_ge(s["x_sum"], t + 1)
                dve.tensor_tensor(pre[:, X_T, :], pre[:, X_T, :], rsb, ALU.mult).then_inc(s["x_mul"], 1)
                dve.wait_ge(s["x_mul"], t + 1)
                dve.tensor_tensor(pre[:, X_T, :], pre[:, X_T, :], pinc[:, X_T, t, :], ALU.add).then_inc(s["x_pre"], 1)
                dve.wait_ge(s["x_exp"], t + 1)
                dve.tensor_scalar(r48[:, X_T, :], e48[:, X_T, :], 1.0, None, ALU.add).then_inc(s["x_one"], 1)
                dve.wait_ge(s["dt_parts"], 2 * t + 2)
                dve.tensor_tensor(m["dt"][:, :, :], m["wm"][:, :, :], m["wa"][:, :, :], ALU.add).then_inc(s["dt_done"], 1)
                dve.wait_ge(s["x_one"], t + 1)
                dve.reciprocal(r48[:, X_T, :], r48[:, X_T, :]).then_inc(s["x_rec"], 1)
                dve.wait_ge(s["dt_done"], t + 1)
                dve.tensor_tensor(m["dta"][:, :, :], m["dt"][:, :, :], m["a_b"][:, :, :], ALU.mult).then_inc(s["dta"], 1)
                dve.wait_ge(s["x_rec"], t + 1)
                dve.tensor_tensor(V[:, X_T, t, :], pre[:, X_T, :], r48[:, X_T, :], ALU.mult).then_inc(s["x_act"], 1)
                dve.wait_ge(s["dots_mm"], t + 1)
                if t >= 1:
                    dve.tensor_tensor(m["prod"][:, :, 0:t, :], Wh[:, :, 0:t, :],
                                      dot_bank[:, 0:t * NB].rearrange("p (s b) -> p s b", b=NB)[:, None, :, :].to_broadcast([P, 2, t, NB]),
                                      ALU.mult).then_inc(s["prod"], 1)
                dve.wait_ge(s["da_done"], t + 1)
                dve.tensor_tensor(m["zzd"][:, :, :, :], m["zz"][:, :, :, :], m["dA"][:, None, :, :].to_broadcast([P, 2, 2, NB]), ALU.mult).then_inc(s["past_in"], 1)
                if t >= 1:
                    dve.wait_ge(s["prod"], t)
                    dve.tensor_reduce(m["R"][:, :, :], m["prod"][:, :, 0:t, :].rearrange("p h s b -> p h b s"), AX.X, ALU.add).then_inc(s["past_in"], 1)
                else:
                    dve.memset(m["R"][:, :, :], 0.0).then_inc(s["past_in"], 1)
                dve.wait_ge(s["dtzx"], t + 1)
                dve.tensor_tensor(gt[:, :, :, 4], m["dtzx"][:, :, :], dot_bank[:, t * NB:(t + 1) * NB][:, None, :].to_broadcast(W2),
                                  ALU.mult).then_inc(s["g_terms"], 1)
                dve.wait_ge(s["past_in"], 2 * t + 2)
                dve.tensor_tensor(gt[:, :, :, 3], m["R"][:, :, :], m["zzd"][:, 0, :, :], ALU.mult).then_inc(s["g_terms"], 1)
                dve.wait_ge(s["u_mm"], t + 1)
                dve.tensor_tensor(gt[:, :, :, 0:3], u_bank[:, 0:48].rearrange("p (h b c) -> p h b c", h=2, b=NB),
                                  m["zzd"][:, 1, :, :][:, :, :, None].to_broadcast([P, 2, NB, 3]), ALU.mult).then_inc(s["g_terms"], 1)
                dve.wait_ge(s["g_terms"], 4 * t + 4)
                dve.tensor_reduce(G[:, :, :], gt[:, :, :, :], AX.X, ALU.add).then_inc(s["g_done"], 1)
                dve.wait_ge(s["g_done"], t + 1)
                dve.tensor_copy(Gs[:, :, 0, :], G[:, :, :]).then_inc(s["g_high"], 1)
                dve.wait_ge(s["sq_each"], t + 1)
                dve.tensor_tensor(m["Gq1"][:, :], m["Gq"][:, 0, :], m["Gq"][:, 1, :], ALU.add).then_inc(s["sq_done"], 1)
                dve.wait_ge(s["g_high"], t + 1)
                dve.tensor_tensor(Gs[:, :, 1, :], G[:, :, :], Gs[:, :, 0, :], ALU.subtract).then_inc(s["g_rest"], 1)
                dve.tensor_tensor(Gr[:, 0, :, :], G[:, :, :], Gs[:, :, 0, :], ALU.subtract).then_inc(s["g_rest"], 1)
                dve.wait_ge(s["g_rest"], 2 * t + 2)
                dve.tensor_tensor(Gs[:, :, 2, :], Gr[:, 0, :, :], Gs[:, :, 1, :], ALU.subtract).then_inc(s["g_split"], 1)
            dve.wait_ge(s["rs_done"], Q)
            dve.tensor_tensor(yc[:, :, Q - 1, :], G[:, :, :], rsb, ALU.mult).then_inc(s["yn_done"], 1)

    S, Sr, bT, wT, Psel, pd = m["S"], m["Sr"], m["bT"], m["wT"], m["Psel"], m["pd"]
    PAIRS = NB // 2
    VE_LAST = (3,)
    with stage(nc, "sel_done", "t_mm", "bT_done", "w0_done", "w1_done", "p_mm", "pd_done", "s_mul", "o_mm", "s_add", "sp1",
               "sp2", "sp3") as (block, s):
        @block.tensor
        def _(pe):
            pe.transpose(ps[0][:, 0:P], V[:, B_T, :, :].rearrange("p s b -> p (s b)"), mem["ident"][:, :])
            for h in range(2):
                last = pe.transpose(ps[1 + h][:, 0:P], Wh[:, h, :, :].rearrange("p s b -> p (s b)"), mem["ident"][:, :])
            last.then_inc(s["t_mm"], 1)
            pe.wait_ge(s["sel_done"], 1)
            pe.matmul(ps[3][:, 0:4 * NB], ones[:, :], Psel[:, :, :].rearrange("p h b -> p (h b)"), start=True, stop=True).then_inc(s["p_mm"], 1)
            pe.wait_ge(s["bT_done"], 1)
            for k in range(PAIRS):
                pe.wait_ge(s["w0_done"], 2 * k + 2)
                pe.wait_ge(s["w1_done"], k + 1)
                pe.matmul(ps[4 + k][:, :], bT[:, :], wT[:, 2 * k:2 * k + 2, :, :].rearrange("p b h f -> p (b h f)"), start=True, stop=True).then_inc(s["o_mm"], 1)

        @block.gpsimd
        def _(pool):
            load_chunk_z(pool)
            for k in range(PAIRS):
                sl = slice(2 * k, 2 * k + 2)
                if k == 0:
                    pool.wait_ge(s["pd_done"], 1)
                pool.tensor_tensor(S[:, sl, :, :].rearrange("p b h (k j) -> p b (h k) j", k=2),
                                   S[:, sl, :, :].rearrange("p b h (k j) -> p b (h k) j", k=2),
                                   pd[:, sl, :, None].to_broadcast([P, 2, 4, 64]), ALU.mult).then_inc(s["s_mul"], 1)
            pool.tensor_copy(yb[:, :, bass.ds(chunk * (Q * NB), Q * NB)], m["yc"][:, :, :, :].rearrange("p m t b -> p m (t b)"))
            for k in range(PAIRS):
                if k in VE_LAST:
                    continue
                sl = slice(2 * k, 2 * k + 2)
                pool.wait_ge(s["sp3"], k + 1)
                pool.tensor_tensor(Ss[:, 2, sl, :, :], Sr[:, sl, :, :], Ss[:, 1, sl, :, :], ALU.subtract)

        @block.scalar
        def _(act):
            load_chunk_pre(act)
            act.wait_ge(s["t_mm"], 1)
            act.activation(bT[:, :], ps[0][:, 0:P], ACT.Copy).then_inc(s["bT_done"], 1)
            for b in range(NB):
                act.activation(wT[:, b, 0, :], ps[1][:, 0:P], ACT.Copy, scale=m["bmask"][:, b:b + 1]).then_inc(s["w0_done"], 1)

            def third_input(k):
                sl = slice(2 * k, 2 * k + 2)
                act.wait_ge(s["sp2"], k + 1)
                act.activation(Ss[:, 1, sl, :, :], Sr[:, sl, :, :], ACT.Copy).then_inc(s["sp3"], 1)

            for k in range(PAIRS):
                sl = slice(2 * k, 2 * k + 2)
                act.wait_ge(s["s_add"], k + 1)
                act.activation(Ss[:, 0, sl, :, :], S[:, sl, :, :], ACT.Copy).then_inc(s["sp1"], 1)
                if k:
                    third_input(k - 1)
            third_input(PAIRS - 1)

        @block.vector
        def _(dve):
            for hh in range(2):
                last = dve.tensor_scalar(Psel[:, hh::2, :], Pc[:, :, :], m["hsel"][:, hh:hh + 1], None, ALU.mult)
            last.then_inc(s["sel_done"], 1)
            load_chunk_zd(dve)
            dve.wait_ge(s["p_mm"], 1)
            dve.tensor_copy(pd[:, :, :], ps[3][:, 0:4 * NB].rearrange("p (h b) -> p b h", h=4)).then_inc(s["pd_done"], 1)
            for k in range(PAIRS):
                dve.tensor_tensor(wT[:, 2 * k:2 * k + 2, 1, :], ps[2][:, None, 0:P].to_broadcast([P, 2, P]),
                                  m["bmask"][:, 2 * k:2 * k + 2][:, :, None].to_broadcast([P, 2, P]), ALU.mult).then_inc(s["w1_done"], 1)

            def rest(k):
                sl = slice(2 * k, 2 * k + 2)
                dve.wait_ge(s["sp1"], k + 1)
                dve.tensor_tensor(Sr[:, sl, :, :], S[:, sl, :, :], Ss[:, 0, sl, :, :], ALU.subtract).then_inc(s["sp2"], 1)

            for k in range(PAIRS):
                sl = slice(2 * k, 2 * k + 2)
                dve.wait_ge(s["s_mul"], k + 1)
                dve.wait_ge(s["o_mm"], k + 1)
                dve.tensor_tensor(S[:, sl, :, :], S[:, sl, :, :], ps[4 + k][:, :].rearrange("p (b h f) -> p b h f", b=2, h=2), ALU.add).then_inc(s["s_add"], 1)
                if k:
                    rest(k - 1)
            rest(PAIRS - 1)
            for k in VE_LAST:
                sl = slice(2 * k, 2 * k + 2)
                dve.wait_ge(s["sp3"], k + 1)
                dve.tensor_tensor(Ss[:, 2, sl, :, :], Sr[:, sl, :, :], Ss[:, 1, sl, :, :], ALU.subtract)


AHEAD = 3
TILES = NT // P


def attention_memory(sb, heads):
    return dict(sc=sb("sc", [P, AHEAD + 1, NT]), pr=sb("pr", [P, AHEAD + 1, NT]), PT=sb("PT", [P, 2, TILES, NT]),
                nmax=sb("nmax", [P, TILES * heads]), rsum=sb("rsum", [P, TILES * heads]), rinv=sb("rinv", [P, TILES * heads]))


def heads_stage(nc, mem, w, heads, causal, qT, hq, kT, vb, vm, bias, scale_of, out):
    ps = mem["ps"]
    sc, pr, PT, nmax, rsum, rinv = (w[k] for k in ("sc", "pr", "PT", "nmax", "rsum", "rinv"))
    n_tiles = TILES * heads
    NBUF = AHEAD + 1
    sc_bank, t_bank, out_bank = (0, 1, 2, 6), (3, 4, 7), 5

    def width(n):
        return (n % TILES + 1) * P if causal else NT

    def normalise(engine, n, done):
        k = width(n)
        engine.wait_ge(s["rc_done"], n + 1)
        engine.tensor_scalar(pr[:, n % NBUF, 0:k], pr[:, n % NBUF, 0:k], rinv[:, n:n + 1], None, ALU.mult).then_inc(done, 1)

    with stage(nc, "q_ready", "v_ready", "s_mm", "sc_done", "mx_done", "exp_done", "rc_done", "even_norm", "odd_norm", "t_mm", "tc_done",
               "pv_done") as (block, s):
        @block.tensor
        def _(pe):
            def scores(n):
                h, i = divmod(n, TILES)
                if i == 0 and hq is not None:
                    pe.wait_ge(s["q_ready"], h + 1)
                if n >= NBUF:
                    pe.wait_ge(s["sc_done"], n - NBUF + 1)
                q = qT if hq is None else w["qm"][:, h % 2, :]
                pe.matmul(ps[sc_bank[n % NBUF]][:, 0:width(n)], q[:, i * P:(i + 1) * P], kT[:, 0:width(n)],
                          start=True, stop=True).then_inc(s["s_mm"], 1)

            def transposes(n):
                pe.wait_ge(s["odd_norm" if n % 2 else "even_norm"], n // 2 + 1)
                if n >= 3:
                    pe.wait_ge(s["tc_done"], n - 2)
                for j in range(width(n) // P):
                    last = pe.transpose(ps[t_bank[n % 3]][:, j * P:(j + 1) * P], pr[:, n % NBUF, j * P:(j + 1) * P], mem["ident"][:, :])
                last.then_inc(s["t_mm"], 1)

            def values(h, j):
                if j == 0:
                    pe.wait_ge(s["tc_done"], TILES * h + TILES)
                    if vm is not None:
                        pe.wait_ge(s["v_ready"], h + 1)
                v = vb if vm is None else vm[:, h, :, :]
                c = j * P if causal else 0
                pe.matmul(ps[out_bank][:, c:NT], v[:, j, :], PT[:, h % 2, j, c:NT], start=(h == 0 and j == 0),
                          stop=(h == heads - 1 and j == TILES - 1), skip_group_check=True).then_inc(s["pv_done"], 1)

            for n in range(min(AHEAD, n_tiles)):
                scores(n)
            for n in range(n_tiles):
                if n + AHEAD < n_tiles:
                    scores(n + AHEAD)
                transposes(n)
                if n >= TILES:
                    values(n // TILES - 1, n % TILES)
            for j in range(TILES):
                values(heads - 1, j)

        @block.scalar
        def _(act):
            def copy_out(n):
                h, i = divmod(n, TILES)
                act.wait_ge(s["t_mm"], n + 1)
                if h >= 2 and i == 0:
                    act.wait_ge(s["pv_done"], TILES * (h - 1))
                k = width(n)
                act.activation(PT[:, h % 2, 0:k // P, i * P:(i + 1) * P], ps[t_bank[n % 3]][:, 0:k].rearrange("p (j t) -> p j t", t=P),
                               ACT.Copy).then_inc(s["tc_done"], 1)

            for n in range(n_tiles + 2):
                if n < n_tiles:
                    k = width(n)
                    act.wait_ge(s["mx_done"], n + 1)
                    if n >= NBUF:
                        act.wait_ge(s["t_mm"], n - NBUF + 1)
                    act.activation(pr[:, n % NBUF, 0:k], sc[:, n % NBUF, 0:k], ACT.Exp, bias=nmax[:, n:n + 1],
                                   accum_out=rsum[:, n:n + 1]).then_inc(s["exp_done"], 1)
                if n >= 2:
                    copy_out(n - 2)

        @block.gpsimd
        def _(pool):
            for n in range(0, n_tiles, 2):
                if n % TILES == 0 and vm is not None:
                    h = n // TILES
                    c = slice(h * (P // heads), (h + 1) * (P // heads))
                    pool.tensor_copy(vm[:, h, :, c], vb[:, :, c]).then_inc(s["v_ready"], 1)
                normalise(pool, n, s["even_norm"])

        @block.vector
        def _(dve):
            def queries(h):
                if h >= 2:
                    dve.wait_ge(s["s_mm"], TILES * (h - 1))
                dve.tensor_scalar(w["qm"][:, h % 2, :], qT[:, :], hq[:, h:h + 1], None, ALU.mult).then_inc(s["q_ready"], 1)

            def inverse(n):
                dve.wait_ge(s["exp_done"], n + 1)
                dve.reciprocal(rinv[:, n:n + 1], rsum[:, n:n + 1]).then_inc(s["rc_done"], 1)

            if hq is not None:
                queries(0)
            for n in range(n_tiles):
                h, i = divmod(n, TILES)
                k = width(n)
                if i == 0 and h + 1 < heads:
                    queries(h + 1)
                dve.wait_ge(s["s_mm"], n + 1)
                if n >= NBUF:
                    dve.wait_ge(s["exp_done"], n - NBUF + 1)
                dve.scalar_tensor_tensor(sc[:, n % NBUF, 0:k], bias(h, i), scale_of(h, i), ps[sc_bank[n % NBUF]][:, 0:k], ALU.mult,
                                         ALU.add).then_inc(s["sc_done"], 1)
                if n >= 1:
                    inverse(n - 1)
                dve.wait_ge(s["sc_done"], n + 1)
                dve.tensor_reduce(nmax[:, n:n + 1], sc[:, n % NBUF, 0:k], AX.X, ALU.max, negate=True).then_inc(s["mx_done"], 1)
                if n >= 2 and n % 2 == 0:
                    normalise(dve, n - 1, s["odd_norm"])
            inverse(n_tiles - 1)
            normalise(dve, n_tiles - 1, s["odd_norm"])
            dve.wait_ge(s["pv_done"], n_tiles)
            dve.tensor_copy(out, ps[out_bank][:, :])


def residual_stage(nc, mem, x, sat, f, e, gap=None):
    n = TOK // CH
    with stage(nc, "e_done", "d_done", "r_done", "g_done", "m_done", "x_done") as (block, s):
        @block.scalar
        def _(act):
            for k in range(n):
                if k >= 2:
                    act.wait_ge(s["x_done"], k - 1)
                act.activation(e[:, k % 2, :], f[:, k * CH:(k + 1) * CH], ACT.Exp, scale=-1.0).then_inc(s["e_done"], 1)

        @block.gpsimd
        def _(pool):
            for k in range(n):
                c = slice(k * CH, (k + 1) * CH)
                pool.tensor_tensor(sat[:, c], sat[:, c], f[:, c], ALU.mult).then_inc(s["m_done"], 1)

        @block.vector
        def _(dve):
            for k in range(n):
                c = slice(k * CH, (k + 1) * CH)
                dve.wait_ge(s["e_done"], k + 1)
                dve.tensor_scalar(e[:, k % 2, :], e[:, k % 2, :], 1.0, None, ALU.add).then_inc(s["d_done"], 1)
                dve.wait_ge(s["d_done"], k + 1)
                dve.reciprocal(e[:, k % 2, :], e[:, k % 2, :]).then_inc(s["r_done"], 1)
                dve.wait_ge(s["r_done"], k + 1)
                dve.wait_ge(s["m_done"], k + 1)
                dve.tensor_tensor(e[:, k % 2, :], e[:, k % 2, :], sat[:, c], ALU.mult).then_inc(s["g_done"], 1)
                dve.wait_ge(s["g_done"], k + 1)
                dve.tensor_tensor(x[:, c], x[:, c], e[:, k % 2, :], ALU.add).then_inc(s["x_done"], 1)


CHUNKS = [slice(k * CH, (k + 1) * CH) for k in range(TOK // CH)]


def layer1(nc, mem, A, x):
    ps = mem["ps"]
    with ExitStack() as ctx:
        def sb(name, shape, dt=F32):
            return ctx.enter_context(nc.sbuf_tensor("l1_" + name, shape, dt))

        xn, sat = sb("xn", [P, TOK]), sb("sat", [P, TOK])
        wq, wk, wv = sb("wq", [P, P]), sb("wk", [P, P]), sb("wv", [P, P])
        cmask = sb("cmask", [P, NT])
        cn_w1, cn_w2, cn_w3, cn_w4 = sb("cn_w1", [P, P]), sb("cn_w2", [P, 64]), sb("cn_w3", [64, 32]), sb("cn_w4", [32, P])
        gc_w1, gc_w2, gc_w3 = sb("gc_w1", [P, 64]), sb("gc_w2", [64, 32]), sb("gc_w3", [32, P])
        cvec = sb("cvec", [P, 8])
        half = sb("half", [P, 2])
        twist = sb("twist", [P, P])
        with stage(nc, "loaded") as (block, s):
            loads = [(wq[:, :], A["l1_wq"]), (wk[:, :], A["l1_wk"]), (wv[:, :], A["l1_wv"]), (cmask[:, :], A["cmask"]),
                     (cn_w1[:, :], A["cn_w1"]), (cn_w2[:, :], A["cn_w2"]), (cn_w3[:, :], A["cn_w3"]), (cn_w4[:, :], A["cn_w4"]),
                     (gc_w1[:, :], A["gc_w1"]), (gc_w2[:, :], A["gc_w2"]), (gc_w3[:, :], A["gc_w3"]), (cvec[:, :], A["cvec"]),
                     (twist[:, :], A["twist"])]

            @block.sync
            def _(sp):
                for dst, src in loads:
                    sp.dma_start(dst, src).then_inc(s["loaded"], 16)
                sp.wait_ge(s["loaded"], 16 * len(loads))

            @block.vector
            def _(dve):
                dve.wait_ge(s["loaded"], 16 * len(loads))
                dve.tensor_scalar(half[:, :], cvec[:, 3:7:3], 0.5, None, ALU.mult)
        layernorm_stage(nc, mem, x, xn, CHUNKS)

        with ExitStack() as attn:
            def asb(name, shape, dt=F32):
                return attn.enter_context(nc.sbuf_tensor("l1_" + name, shape, dt))

            xb, qT, kT, vb = asb("xb", [P, NT]), asb("qT", [P, NT]), asb("kT", [P, NT]), asb("vb", [P, 4, P])
            w = attention_memory(asb, 1)
            with nc.Fori(0, NB) as b:
                qkv_stage(nc, mem, xn, b, xb, wq, wk, wv, qT, kT, vb, P ** -0.5)
                heads_stage(nc, mem, w, 1, True, qT, None, kT, vb, None,
                            lambda h, i: cmask[:, NT - (i + 1) * P:NT], lambda h, i: 1.0, sat[:, bass.ts(b, NT)])

        with ExitStack() as ffn:
            def fsb(name, shape, dt=F32):
                return ffn.enter_context(nc.sbuf_tensor("l1_" + name, shape, dt))

            hid = fsb("hid", [P, NB, CH])
            cpl = fsb("cpl", [P, 2, CH])
            gm, g1, g2, gt = fsb("gm", [P, NB]), fsb("g1", [64, NB]), fsb("g2", [32, NB]), fsb("gt", [P, NB])
            arc = fsb("arc", [P, 2])
            base = fsb("base", [P, NB])
            nc.scalar.preload_act_table_set("gelu_and_others")
            with stage(nc, "mean_done", "g_mm", "g_act", "ar_done") as (block, s):
                @block.tensor
                def _(pe):
                    pe.wait_ge(s["mean_done"], 1)
                    pe.matmul(ps[0][0:64, 0:NB], gc_w1[:, :], gm[:, :], start=True, stop=True).then_inc(s["g_mm"], 1)
                    pe.wait_ge(s["g_act"], 1)
                    pe.matmul(ps[1][0:32, 0:NB], gc_w2[:, :], g1[:, :], start=True, stop=True).then_inc(s["g_mm"], 1)
                    pe.wait_ge(s["g_act"], 2)
                    pe.matmul(ps[2][:, 0:NB], gc_w3[:, :], g2[:, :], start=True, stop=True).then_inc(s["g_mm"], 1)

                @block.scalar
                def _(act):
                    act.wait_ge(s["g_mm"], 1)
                    act.activation(g1[:, :], ps[0][0:64, 0:NB], ACT.Gelu, scale=1.0 / NT, bias=cvec[0:64, 4:5]).then_inc(s["g_act"], 1)
                    act.wait_ge(s["g_mm"], 2)
                    act.activation(g2[:, :], ps[1][0:32, 0:NB], ACT.Gelu, bias=cvec[0:32, 5:6]).then_inc(s["g_act"], 1)
                    act.wait_ge(s["g_mm"], 3)
                    act.activation(gt[:, :], ps[2][:, 0:NB], ACT.Tanh, scale=0.5, bias=half[:, 1:2]).then_inc(s["g_act"], 1)

                @block.vector
                def _(dve):
                    dve.tensor_reduce(gm[:, :], xn[:, :].rearrange("p (b t) -> p b t", b=NB), AX.X, ALU.add).then_inc(s["mean_done"], 1)
                    dve.tensor_scalar(arc[:, 0:1], cvec[:, 7:8], 0.3, None, ALU.mult)
                    dve.tensor_scalar(arc[:, 1:2], cvec[:, 7:8], 0.7, None, ALU.mult).then_inc(s["ar_done"], 1)
                    dve.wait_ge(s["g_act"], 3)
                    dve.wait_ge(s["ar_done"], 1)
                    dve.tensor_scalar(base[:, :], gt[:, :], arc[:, 1:2], 0.1, ALU.mult, ALU.add)
            with nc.Fori(0, 3) as cycle:
                with stage(nc, "mm", "acted", "read", "cpl_done", "tw_done") as (block, s):
                    ws = [cn_w1[:, :], cn_w2[:, :], cn_w3[:, :], cn_w4[:, :]]
                    rows = [P, 64, 32, P]

                    @block.tensor
                    def _(pe):
                        for l in range(4):
                            for k in range(NB):
                                if l:
                                    pe.wait_ge(s["acted"], (l - 1) * NB + k + 1)
                                src = xn[:, CHUNKS[k]] if l == 0 else hid[0:rows[l - 1], k, :]
                                pe.matmul(ps[k][0:rows[l], :], ws[l], src, start=True, stop=True).then_inc(s["mm"], 1)
                        for k in range(NB):
                            pe.wait_ge(s["acted"], 3 * NB + k + 1)
                            pe.matmul(ps[k][:, :], twist[:, :], xn[:, CHUNKS[k]], start=True, stop=True).then_inc(s["mm"], 1)

                    @block.scalar
                    def _(act):
                        for l in range(4):
                            for k in range(NB):
                                act.wait_ge(s["mm"], l * NB + k + 1)
                                r = rows[l]
                                if l < 3:
                                    act.activation(hid[0:r, k, :], ps[k][0:r, :], ACT.Gelu, bias=cvec[0:r, l:l + 1]).then_inc(s["acted"], 1)
                                else:
                                    act.activation(hid[:, k, :], ps[k][:, :], ACT.Tanh, scale=0.5, bias=half[:, 0:1]).then_inc(s["acted"], 1)

                    @block.vector
                    def _(dve):
                        for k in range(NB):
                            dve.wait_ge(s["acted"], 3 * NB + k + 1)
                            dve.tensor_scalar(hid[:, k, :], hid[:, k, :], arc[:, 0:1], base[:, k:k + 1], ALU.mult, ALU.add).then_inc(s["cpl_done"], 1)
                            dve.wait_ge(s["cpl_done"], k + 1)
                            dve.wait_ge(s["mm"], 4 * NB + k + 1)
                            if k >= 2:
                                dve.wait_ge(s["read"], k - 1)
                            dve.tensor_tensor(cpl[:, k % 2, :], hid[:, k, :], ps[k][:, :], ALU.mult).then_inc(s["tw_done"], 1)
                            dve.wait_ge(s["tw_done"], k + 1)
                            dve.tensor_tensor(xn[:, CHUNKS[k]], xn[:, CHUNKS[k]], cpl[:, k % 2, :], ALU.add).then_inc(s["read"], 1)
            nc.scalar.preload_act_table_set("natural_log_exp_and_others")
            residual_stage(nc, mem, x, sat, xn, cpl)


def qkv_stage(nc, mem, xn, b, xb, wq, wk, wv, qT, kT, vb, q_scale, q_bias=None, k_bias=None):
    ps = mem["ps"]
    with stage(nc, "x_done", "q_mm", "k_mm", "v_mm") as (block, s):
        @block.tensor
        def _(pe):
            pe.wait_ge(s["x_done"], 1)
            pe.matmul(ps[0][:, :], wq[:, :], xb[:, :], start=True, stop=True).then_inc(s["q_mm"], 1)
            pe.matmul(ps[1][:, :], wk[:, :], xb[:, :], start=True, stop=True).then_inc(s["k_mm"], 1)
            for j in range(4):
                last = pe.matmul(ps[2][:, j * P:(j + 1) * P], xb[:, j * P:(j + 1) * P], wv[:, :], start=True, stop=True)
            last.then_inc(s["v_mm"], 1)

        @block.scalar
        def _(act):
            act.wait_ge(s["q_mm"], 1)
            if q_bias is None:
                act.activation(qT[:, :], ps[0][:, :], ACT.Copy, scale=q_scale)
            else:
                act.activation(qT[:, :], ps[0][:, :], ACT.Identity, bias=q_bias)
            act.wait_ge(s["v_mm"], 1)
            act.activation(vb[:, :, :], ps[2][:, :].rearrange("p (j e) -> p j e", e=P), ACT.Copy)

        @block.vector
        def _(dve):
            dve.tensor_copy(xb[:, :], xn[:, bass.ts(b, NT)]).then_inc(s["x_done"], 1)
            dve.wait_ge(s["k_mm"], 1)
            if k_bias is None:
                dve.tensor_copy(kT[:, :], ps[1][:, :])
            else:
                dve.tensor_scalar(kT[:, :], ps[1][:, :], k_bias, None, ALU.add)


def layout_l1(i, A):
    A["l1_wq"], A["l1_wk"], A["l1_wv"] = i["L1_attn_Wq"], i["L1_attn_Wk"], i["L1_attn_Wv"]
    t, c = np.arange(P)[:, None], np.arange(NT)[None, :]
    A["cmask"] = np.where(c - 3 * P <= t, 0.0, -1e30).astype(np.float32)
    for n in ("cn_w1", "cn_w2", "cn_w3", "gc_w1", "gc_w2"):
        A[n] = i["L1_ffn_" + n]
    A["cn_w4"] = np.broadcast_to(i["L1_ffn_cn_w4"], (32, P))
    A["gc_w3"] = np.broadcast_to(i["L1_ffn_gc_w3"], (32, P))
    cv = np.zeros((P, 8), np.float32)
    for j, n in enumerate(("cn_b1", "cn_b2", "cn_b3", "cn_b4", "gc_b1", "gc_b2", "gc_b3", "adaptive_range")):
        v = i["L1_ffn_" + n]
        if v.shape == (1,):
            cv[:, j] = v[0]
        else:
            cv[0:v.shape[0], j] = v
    A["cvec"] = cv
    tw = np.zeros((P, P), np.float32)
    for r in range(32):
        tw[64 + r, r] = 1.0
        tw[96 + r, 32 + r] = -1.0
        tw[r, 64 + r] = -1.0
        tw[32 + r, 96 + r] = 1.0
    A["twist"] = tw


NH = 16
HD = P // NH


def layer2(nc, mem, A, x):
    ps = mem["ps"]
    NE, TOPK, NPAIR = 16, 8, 8
    with ExitStack() as ctx:
        def sb(name, shape, dt=F32):
            return ctx.enter_context(nc.sbuf_tensor("l2_" + name, shape, dt))

        xn, sat = sb("xn", [P, TOK]), sb("sat", [P, TOK])
        layernorm_stage(nc, mem, x, xn, CHUNKS)

        with ExitStack() as attn:
            def asb(name, shape, dt=F32):
                return attn.enter_context(nc.sbuf_tensor("l2_" + name, shape, dt))

            wq, wk, wv = asb("wq", [P, P]), asb("wk", [P, P]), asb("wv", [P, P])
            rel, slope = asb("rel", [P, NT]), asb("slope", [P, NH])
            hq = asb("hq", [P, NH])
            xb, qT, kT, vb = asb("xb", [P, NT]), asb("qT", [P, NT]), asb("kT", [P, NT]), asb("vb", [P, 4, P])
            w = attention_memory(asb, NH)
            w["qm"], vm = asb("qm", [P, 2, NT]), asb("vm", [P, NH, 4, P])
            with stage(nc, "loaded") as (block, s):
                loads = [(wq[:, :], A["l2_wq"]), (wk[:, :], A["l2_wk"]), (wv[:, :], A["l2_wv"]), (rel[:, :], A["rel"]),
                         (slope[:, :], A["slope"]), (hq[:, :], A["head_q"])]

                @block.sync
                def _(sp):
                    for dst, src in loads:
                        sp.dma_start(dst, src).then_inc(s["loaded"], 16)
                    sp.wait_ge(s["loaded"], 16 * len(loads))

                @block.gpsimd
                def _(pool):
                    pool.memset(vm[:, :, :, :], 0.0)

            with nc.Fori(0, NB) as b:
                qkv_stage(nc, mem, xn, b, xb, wq, wk, wv, qT, kT, vb, P ** -0.5)
                heads_stage(nc, mem, w, NH, True, qT, hq, kT, vb, vm,
                            lambda h, i: rel[:, NT - (i + 1) * P:NT], lambda h, i: slope[:, h:h + 1], sat[:, bass.ts(b, NT)])

        with ExitStack() as ffn:
            def fsb(name, shape, dt=F32):
                return ffn.enter_context(nc.sbuf_tensor("l2_" + name, shape, dt))

            NTILE = TOK // P
            gate_w = fsb("gate_w", [P, NE])
            wg, wu, wd = fsb("wg", [P, NPAIR + 1, P]), fsb("wu", [P, NPAIR + 1, P]), fsb("wd", [P, NPAIR + 1, P])
            sel = fsb("sel", [NE, NPAIR, P])
            sq = fsb("sq", [P, 2, CH])
            gsq, gnorm, gi = fsb("gsq", [P, NE]), fsb("gnorm", [P, NE]), fsb("gi", [P, NE])
            xnorm, xinv = fsb("xnorm", [P, NTILE]), fsb("xinv", [P, NTILE])
            lg, lr = fsb("lg", [P, NTILE, NE]), fsb("lr", [P, NTILE, NE])
            top = fsb("top", [P, NTILE, TOPK])
            th = fsb("th", [P, NTILE, NE])
            csum, cinv = fsb("csum", [P, NTILE]), fsb("cinv", [P, NTILE])
            cT = fsb("cT", [NE, TOK])
            sl, us, cbuf = fsb("sl", [P, 3, CH]), fsb("us", [P, 2, CH]), fsb("cbuf", [P, 2, CH])

            with stage(nc, "loaded", "squared", "g_sq", "ss_mm", "g_mm", "ss_max", "root", "n_max", "inv", "gw_done", "lg_mm",
                       "lg_done", "top_done", "rep", "mask", "tanh_done", "sig", "wts", "sum_done", "comb", "c_mm", "c_done") as (block, s):
                loads = [(gate_w[:, :], A["l2_gate_w"]), (wg[:, :, :], A["l2_wg"]), (wu[:, :, :], A["l2_wu"]),
                         (wd[:, :, :], A["l2_wd"]), (sel[:, :, :], A["sel_pair"])]

                @block.sync
                def _(sp):
                    for dst, src in loads:
                        sp.dma_start(dst, src).then_inc(s["loaded"], 16)

                @block.tensor
                def _(pe):
                    pe.wait_ge(s["g_sq"], 1)
                    pe.matmul(ps[1][:, 0:NE], mem["ones"][:, :], gsq[:, :], start=True, stop=True).then_inc(s["g_mm"], 1)
                    for t in range(NTILE):
                        pe.wait_ge(s["squared"], t // 4 + 1)
                        pe.matmul(ps[0][:, t:t + 1], sq[:, (t // 4) % 2, (t % 4) * P:(t % 4 + 1) * P], mem["ones"][:, 0:1],
                                  start=True, stop=True).then_inc(s["ss_mm"], 1)
                    pe.wait_ge(s["gw_done"], 1)
                    for t in range(NTILE):
                        last = pe.matmul(ps[2][:, t * NE:(t + 1) * NE], xn[:, t * P:(t + 1) * P], gi[:, :], start=True, stop=True)
                    last.then_inc(s["lg_mm"], 1)
                    pe.wait_ge(s["comb"], 1)
                    for k in range(NB):
                        if k >= 2:
                            pe.wait_ge(s["c_done"], k - 1)
                        for t in range(4):
                            last = pe.transpose(ps[3 + k % 2][0:NE, t * P:(t + 1) * P], th[:, 4 * k + t, :], mem["ident"][:, :])
                        last.then_inc(s["c_mm"], 1)

                @block.scalar
                def _(act):
                    for k in range(NB):
                        if k >= 2:
                            act.wait_ge(s["ss_mm"], 4 * (k - 1))
                        act.activation(sq[:, k % 2, :], xn[:, CHUNKS[k]], ACT.Square).then_inc(s["squared"], 1)
                    act.wait_ge(s["ss_max"], 2)
                    act.activation(xnorm[:, :], xnorm[:, :], ACT.Sqrt).then_inc(s["root"], 1)
                    act.activation(gnorm[:, :], gnorm[:, :], ACT.Sqrt).then_inc(s["root"], 1)
                    act.wait_ge(s["lg_done"], 1)
                    act.activation(th[:, :, :], lg[:, :, :], ACT.Tanh, scale=0.5).then_inc(s["tanh_done"], 1)
                    for k in range(NB):
                        act.wait_ge(s["c_mm"], k + 1)
                        act.activation(cT[:, CHUNKS[k]], ps[3 + k % 2][0:NE, :], ACT.Copy).then_inc(s["c_done"], 1)

                @block.vector
                def _(dve):
                    dve.wait_ge(s["loaded"], 16 * len(loads))
                    dve.tensor_tensor(gsq[:, :], gate_w[:, :], gate_w[:, :], ALU.mult).then_inc(s["g_sq"], 1)
                    dve.wait_ge(s["g_mm"], 1)
                    dve.tensor_scalar(gnorm[:, :], ps[1][:, 0:NE], 1e-34, None, ALU.max).then_inc(s["ss_max"], 1)
                    dve.wait_ge(s["ss_mm"], NTILE)
                    dve.tensor_scalar(xnorm[:, :], ps[0][:, 0:NTILE], 1e-34, None, ALU.max).then_inc(s["ss_max"], 1)
                    dve.wait_ge(s["root"], 2)
                    dve.tensor_scalar(xnorm[:, :], xnorm[:, :], 1e-12, None, ALU.max).then_inc(s["n_max"], 1)
                    dve.tensor_scalar(gnorm[:, :], gnorm[:, :], 1e-12, None, ALU.max).then_inc(s["n_max"], 1)
                    dve.wait_ge(s["n_max"], 2)
                    dve.reciprocal(xinv[:, :], xnorm[:, :]).then_inc(s["inv"], 1)
                    dve.reciprocal(gsq[:, :], gnorm[:, :]).then_inc(s["inv"], 1)
                    dve.wait_ge(s["inv"], 2)
                    dve.tensor_tensor(gi[:, :], gate_w[:, :], gsq[:, :], ALU.mult).then_inc(s["gw_done"], 1)
                    dve.wait_ge(s["lg_mm"], 1)
                    dve.tensor_tensor(lg[:, :, :], ps[2][:, :].rearrange("p (t e) -> p t e", e=NE),
                                      xinv[:, :, None].to_broadcast([P, NTILE, NE]), ALU.mult).then_inc(s["lg_done"], 1)
                    dve.wait_ge(s["lg_done"], 1)
                    for t in range(NTILE):
                        dve.max(top[:, t, :], lg[:, t, :]).then_inc(s["top_done"], 1)
                    for t in range(NTILE):
                        dve.wait_ge(s["top_done"], t + 1)
                        dve.match_replace(lr[:, t, :], top[:, t, :], lg[:, t, :], -1e30).then_inc(s["rep"], 1)
                    dve.wait_ge(s["rep"], NTILE)
                    dve.tensor_scalar(lr[:, :, :], lr[:, :, :], -1e29, None, ALU.is_lt).then_inc(s["mask"], 1)
                    dve.wait_ge(s["tanh_done"], 1)
                    dve.tensor_scalar(th[:, :, :], th[:, :, :], 0.5, 0.5, ALU.mult, ALU.add).then_inc(s["sig"], 1)
                    dve.wait_ge(s["sig"], 1)
                    dve.wait_ge(s["mask"], 1)
                    dve.tensor_tensor(th[:, :, :], th[:, :, :], lr[:, :, :], ALU.mult).then_inc(s["wts"], 1)
                    dve.wait_ge(s["wts"], 1)
                    dve.tensor_reduce(csum[:, :], th[:, :, :], AX.X, ALU.add).then_inc(s["sum_done"], 1)
                    dve.wait_ge(s["sum_done"], 1)
                    dve.reciprocal(cinv[:, :], csum[:, :]).then_inc(s["sum_done"], 1)
                    dve.wait_ge(s["sum_done"], 2)
                    dve.tensor_tensor(th[:, :, :], th[:, :, :], cinv[:, :, None].to_broadcast([P, NTILE, NE]), ALU.mult).then_inc(s["comb"], 1)

            nc.scalar.preload_act_table_set("silu_and_others")
            with nc.Fori(0, NB) as k:
                with stage(nc, "g_mm", "u_mm", "c_mm", "silu_done", "c_done", "m1", "m2", "d_mm") as (block, s):
                    @block.tensor
                    def _(pe):
                        def up(e):
                            r = P if e < NPAIR else 64
                            if e >= 2:
                                pe.wait_ge(s["silu_done"], e - 1)
                            pe.matmul(ps[e % 2][0:r, :], wg[:, e, 0:r], xn[:, bass.ts(k, CH)], start=True, stop=True).then_inc(s["g_mm"], 1)
                            if e >= 2:
                                pe.wait_ge(s["m1"], e - 1)
                            pe.matmul(ps[2 + e % 2][0:r, :], wu[:, e, 0:r], xn[:, bass.ts(k, CH)], start=True, stop=True).then_inc(s["u_mm"], 1)
                            if e < NPAIR:
                                if e >= 2:
                                    pe.wait_ge(s["c_done"], e - 1)
                                pe.matmul(ps[4 + e % 2][:, :], sel[:, e, :], cT[:, bass.ts(k, CH)], start=True, stop=True).then_inc(s["c_mm"], 1)

                        up(0)
                        for e in range(NPAIR + 1):
                            if e < NPAIR:
                                up(e + 1)
                            r = P if e < NPAIR else 64
                            pe.wait_ge(s["m2"], e + 1)
                            pe.matmul(ps[6][:, :], wd[0:r, e, :], us[0:r, e % 2, :], start=(e == 0), stop=(e == NPAIR)).then_inc(s["d_mm"], 1)

                    @block.scalar
                    def _(act):
                        for e in range(NPAIR + 1):
                            r = P if e < NPAIR else 64
                            act.wait_ge(s["g_mm"], e + 1)
                            if e >= 3:
                                act.wait_ge(s["m2"], e - 2)
                            act.activation(sl[0:r, e % 3, :], ps[e % 2][0:r, :], ACT.Silu).then_inc(s["silu_done"], 1)
                            if e < NPAIR:
                                act.wait_ge(s["c_mm"], e + 1)
                                if e >= 2:
                                    act.wait_ge(s["m2"], e - 1)
                                act.activation(cbuf[:, e % 2, :], ps[4 + e % 2][:, :], ACT.Copy).then_inc(s["c_done"], 1)

                    @block.vector
                    def _(dve):
                        for e in range(NPAIR + 1):
                            r = P if e < NPAIR else 64
                            dve.wait_ge(s["silu_done"], e + 1)
                            dve.wait_ge(s["u_mm"], e + 1)
                            if e >= 2:
                                dve.wait_ge(s["d_mm"], e - 1)
                            if e < NPAIR:
                                dve.tensor_tensor(sl[0:r, e % 3, :], sl[0:r, e % 3, :], ps[2 + e % 2][0:r, :], ALU.mult).then_inc(s["m1"], 1)
                                dve.wait_ge(s["m1"], e + 1)
                                dve.wait_ge(s["c_done"], e + 1)
                                dve.tensor_tensor(us[:, e % 2, :], sl[:, e % 3, :], cbuf[:, e % 2, :], ALU.mult).then_inc(s["m2"], 1)
                            else:
                                dve.tensor_tensor(us[0:r, e % 2, :], sl[0:r, e % 3, :], ps[2 + e % 2][0:r, :], ALU.mult).then_inc(s["m2"], 1)
                        dve.wait_ge(s["d_mm"], NPAIR + 1)
                        dve.tensor_copy(xn[:, bass.ts(k, CH)], ps[6][:, :])

            nc.scalar.preload_act_table_set("natural_log_exp_and_others")
            residual_stage(nc, mem, x, sat, xn, cbuf)


def layout_l2(i, A):
    wkqv = i["L2_attn_W_kqv"]
    A["l2_wk"], A["l2_wq"], A["l2_wv"] = wkqv[0:P].T, wkqv[P:2 * P].T, wkqv[2 * P:3 * P].T
    t, c = np.arange(P)[:, None], np.arange(NT)[None, :]
    r = (c - 3 * P - t).astype(np.float32)
    A["rel"] = np.where(r <= 0, r, -1e30).astype(np.float32)
    sl = np.array([1.0 / (2.0 ** 8) ** ((n + 1) / NH) for n in range(NH)], np.float32)
    A["slope"] = np.broadcast_to(sl, (P, NH))
    own = (np.arange(P)[:, None] // HD == np.arange(NH)).astype(np.float32)
    A["head_q"] = own
    A["l2_gate_w"] = i["L2_ffn_gate_w"].T
    for n, full, shared in (("l2_wg", "w_gate", "sw_gate"), ("l2_wu", "w_up", "sw_up")):
        a = np.zeros((P, 9, P), np.float32)
        a[:, 0:8, :] = i["L2_ffn_" + full].transpose(1, 0, 2).reshape(P, 8, P)
        a[:, 8, 0:64] = i["L2_ffn_" + shared]
        A[n] = a
    a = np.zeros((P, 9, P), np.float32)
    a[:, 0:8, :] = i["L2_ffn_w_down"].reshape(8, P, P).transpose(1, 0, 2)
    a[0:64, 8, :] = i["L2_ffn_sw_down"]
    A["l2_wd"] = a
    A["sel_pair"] = (np.arange(16)[:, None, None] == 2 * np.arange(8)[None, :, None] + np.arange(P)[None, None, :] // 64).astype(np.float32)


def butterfly_stages(dve, s, W, buf, work, weights, rows, transposed, bf0, m0):
    src, dst = W, buf
    for n, st in enumerate(range(8, -1, -1) if transposed else range(9)):
        d = 1 << st

        def half(t, r, k):
            return t[:, r, :].rearrange("p (n h s) -> p n h s", h=2, s=d)[:, :, k, :]

        def pair_weight(o, i):
            return weights[:, st, o, i, :].rearrange("p (n s) -> p n s", s=d)

        dve.wait_ge(s["bf"], bf0 + n * rows)
        for r in range(rows):
            for o in range(2):
                a, b = ((0, o), (1, o)) if transposed else ((o, 0), (o, 1))
                dve.tensor_tensor(half(dst, r, o), half(src, r, 0), pair_weight(*a), ALU.mult)
                dve.tensor_tensor(half(work, r, o), half(src, r, 1), pair_weight(*b), ALU.mult).then_inc(s["bf_m"], 1)
        dve.wait_ge(s["bf_m"], m0 + 2 * rows * (n + 1))
        for r in range(rows):
            dve.tensor_tensor(dst[:, r, :], dst[:, r, :], work[:, r, :], ALU.add).then_inc(s["bf"], 1)
        src, dst = dst, src
    return src


def layer3(nc, mem, A, x):
    ps = mem["ps"]
    NBU = 40
    LR = 1024
    with ExitStack() as ctx:
        def sb(name, shape, dt=F32):
            return ctx.enter_context(nc.sbuf_tensor("l3_" + name, shape, dt))

        xn, sat = sb("xn", [P, TOK]), sb("sat", [P, TOK])
        layernorm_stage(nc, mem, x, xn, CHUNKS)
        bias_dram = nc.dram_tensor("l3_bias_rows", (NH, LR), F32, kind="Internal").ap()

        with ExitStack() as attn:
            def asb(name, shape, dt=F32):
                return attn.enter_context(nc.sbuf_tensor("l3_" + name, shape, dt))

            wq, wk, wv, wo = asb("wq", [P, P]), asb("wk", [P, P]), asb("wv", [P, P]), asb("wo", [P, P])
            bvec = asb("bvec", [P, 4])
            gw = asb("gw", [P, 8, NH])
            gb = asb("gb", [P, 8])
            gconst = asb("gconst", [P, NH])
            hq = asb("hq", [P, NH])
            xb, qT, kT, vb = asb("xb", [P, NT]), asb("qT", [P, NT]), asb("kT", [P, NT]), asb("vb", [P, 4, P])
            flip = asb("flip", [P, P])
            gp, gs = asb("gp", [P, 4, 8, NH]), asb("gs", [P, 4, 2, NH])
            gate = asb("gate", [P, 4, NH])
            PBW = 7 * P
            pb = asb("pb", [P, NH, PBW])
            w = attention_memory(asb, NH)
            w["qm"], vm = asb("qm", [P, 2, NT]), asb("vm", [P, NH, 4, P])
            HG = 8
            with ExitStack() as setup:
                rel_embed = setup.enter_context(nc.sbuf_tensor("l3_rel_embed", [NBU, NH], F32))
                onehot = setup.enter_context(nc.sbuf_tensor("l3_onehot", [NBU, LR], F32))
                rows = pb[0:NH, :, :].rearrange("p h c -> p (h c)")[:, 0:LR]
                with stage(nc, "loaded", "row_mm", "row_done", "stored") as (block, s):
                    loads = [(rel_embed[:, :], A["rel_embed"]), (onehot[:, :], A["bucket_onehot"]),
                             (wq[:, :], A["l3_wq"]), (wk[:, :], A["l3_wk"]), (wv[:, :], A["l3_wv"]), (wo[:, :], A["l3_wo"]),
                             (bvec[:, :], A["l3_bvec"]), (gw[:, :, :], A["l3_gw"]), (gb[:, :], A["l3_gb"]),
                             (gconst[:, :], A["l3_gconst"]), (hq[:, :], A["head_q3"]), (flip[:, :], A["flip"])]

                    @block.sync
                    def _(sp):
                        for dst, src in loads:
                            sp.dma_start(dst, src).then_inc(s["loaded"], 16)
                        sp.wait_ge(s["row_done"], 2)
                        sp.dma_start(bias_dram, rows).then_inc(s["stored"], 16)
                        sp.wait_ge(s["stored"], 16)

                    @block.tensor
                    def _(pe):
                        pe.wait_ge(s["loaded"], 16 * len(loads))
                        for c in range(2):
                            pe.matmul(ps[c][0:NH, :], rel_embed[:, :], onehot[:, c * 512:(c + 1) * 512], start=True, stop=True).then_inc(s["row_mm"], 1)

                    @block.vector
                    def _(dve):
                        for c in range(2):
                            dve.wait_ge(s["row_mm"], c + 1)
                            dve.tensor_copy(rows[:, c * 512:(c + 1) * 512], ps[c][0:NH, :]).then_inc(s["row_done"], 1)

            with nc.Fori(0, NH // HG) as g:
                with stage(nc, "loaded", "flip_mm", "flip_done") as (block, s):
                    hankel = vm[:, :, :, :].rearrange("p h j t -> p (h j t)")
                    cols = [slice(0, 512), slice(512, PBW)]

                    def rows_of(h):
                        return hankel[:, h * PBW:(h + 1) * PBW]

                    @block.sync
                    def _(sp):
                        for h in range(HG):
                            row = bias_dram[bass.ds(g * HG + h, 1), :]
                            sp.dma_start(rows_of(h), bass.AP(row.tensor, row.offset, [[1, P], [1, PBW]])).then_inc(s["loaded"], 16)

                    @block.tensor
                    def _(pe):
                        pe.wait_ge(s["loaded"], 16 * HG)
                        for h in range(HG):
                            for c in range(2):
                                n = 2 * h + c
                                if n >= 2:
                                    pe.wait_ge(s["flip_done"], n - 1)
                                pe.matmul(ps[c][:, 0:cols[c].stop - cols[c].start], flip[:, :], rows_of(h)[:, cols[c]],
                                          start=True, stop=True).then_inc(s["flip_mm"], 1)

                    @block.vector
                    def _(dve):
                        for h in range(HG):
                            for c in range(2):
                                dve.wait_ge(s["flip_mm"], 2 * h + c + 1)
                                dve.tensor_copy(pb[:, bass.ds(g * HG + h, 1), cols[c]].rearrange("p o c -> p (o c)"), ps[c][:, 0:cols[c].stop - cols[c].start]).then_inc(s["flip_done"], 1)
            with stage(nc) as (block, s):
                @block.gpsimd
                def _(pool):
                    pool.memset(vm[:, :, :, :], 0.0)
            with nc.Fori(0, NB) as b:
                qkv_stage(nc, mem, xn, b, xb, wq, wk, wv, qT, kT, vb, None, bvec[:, 0:1], bvec[:, 1:2])
                with stage(nc, "p_mm", "g1", "g2", "g3", "e_done", "g4", "g5", "g6", "g7") as (block, s):
                    @block.tensor
                    def _(pe):
                        for i in range(4):
                            last = pe.matmul(ps[0][:, i * P:(i + 1) * P], xb[:, i * P:(i + 1) * P],
                                             gw[:, :, :].rearrange("p e h -> p (e h)"), start=True, stop=True)
                        last.then_inc(s["p_mm"], 1)

                    @block.scalar
                    def _(act):
                        act.wait_ge(s["g2"], 1)
                        act.activation(gs[:, :, :, :], gs[:, :, :, :], ACT.Exp, scale=-1.0).then_inc(s["e_done"], 1)

                    @block.vector
                    def _(dve):
                        dve.wait_ge(s["p_mm"], 1)
                        for i in range(4):
                            dve.tensor_tensor(gp[:, i, :, :], ps[0][:, i * P:(i + 1) * P].rearrange("p (e h) -> p e h", e=8),
                                              gb[:, :, None].to_broadcast([P, 8, NH]), ALU.add).then_inc(s["g1"], 1)
                        dve.wait_ge(s["g1"], 4)
                        dve.tensor_reduce(gs[:, :, :, :], gp[:, :, :, :].rearrange("p i (k e) h -> p (i k) h e", k=2), AX.X, ALU.add).then_inc(s["g2"], 1)
                        dve.wait_ge(s["e_done"], 1)
                        dve.tensor_scalar(gs[:, :, :, :], gs[:, :, :, :], 1.0, None, ALU.add).then_inc(s["g3"], 1)
                        dve.wait_ge(s["g3"], 1)
                        dve.reciprocal(gs[:, :, :, :], gs[:, :, :, :]).then_inc(s["g4"], 1)
                        dve.wait_ge(s["g4"], 1)
                        dve.tensor_tensor(gate[:, :, :], gs[:, :, 1, :], gconst[:, None, :].to_broadcast([P, 4, NH]), ALU.mult).then_inc(s["g5"], 1)
                        dve.wait_ge(s["g5"], 1)
                        dve.scalar_tensor_tensor(gate[:, :, :], gate[:, :, :], -1.0, gs[:, :, 0, :], ALU.add, ALU.mult).then_inc(s["g6"], 1)
                        dve.wait_ge(s["g6"], 1)
                        dve.tensor_scalar(gate[:, :, :], gate[:, :, :], 2.0, None, ALU.add).then_inc(s["g7"], 1)
                heads_stage(nc, mem, w, NH, False, qT, hq, kT, vb, vm,
                            lambda h, i: pb[:, h, (3 - i) * P:(3 - i) * P + NT], lambda h, i: gate[:, i, h:h + 1], sat[:, bass.ts(b, NT)])
            with stage(nc, "b_done", "o_mm", "o_done") as (block, s):
                @block.tensor
                def _(pe):
                    for k in range(NB):
                        pe.wait_ge(s["b_done"], k + 1)
                        pe.matmul(ps[k][:, :], wo[:, :], sat[:, CHUNKS[k]], start=True, stop=True).then_inc(s["o_mm"], 1)

                @block.scalar
                def _(act):
                    for k in range(NB):
                        act.wait_ge(s["o_mm"], k + 1)
                        act.activation(sat[:, CHUNKS[k]], ps[k][:, :], ACT.Identity, bias=bvec[:, 3:4]).then_inc(s["o_done"], 1)

                @block.vector
                def _(dve):
                    for k in range(NB):
                        dve.tensor_scalar(sat[:, CHUNKS[k]], sat[:, CHUNKS[k]], bvec[:, 2:3], None, ALU.add).then_inc(s["b_done"], 1)

        with ExitStack() as ffn:
            def fsb(name, shape, dt=F32):
                return ffn.enter_context(nc.sbuf_tensor("l3_" + name, shape, dt))

            H = 512
            FT = H // P
            up = fsb("up", [P, 2, H])
            down = fsb("down", [P, 1, H])
            buf, work = fsb("buf", [P, 2, H]), fsb("work", [P, 2, H])
            uw, dw = fsb("uw", [P, 9, 2, 2, 256]), fsb("dw", [P, 9, 2, 2, 256])
            ubias = fsb("ubias", [P, FT])
            obias = fsb("obias", [P, 2])
            hbias = fsb("hbias", [P, FT])
            w_up, w_down = fsb("w_up", [P, H]), fsb("w_down", [P, FT, P])
            hid = fsb("hid", [P, 2, FT, CH])
            e = fsb("e", [P, 2, CH])
            with stage(nc, "loaded", "bf", "bf_m", "t_mm", "hb_done", "ob_done") as (block, s):
                loads = [(up[:, :, :], A["l3_up"]), (down[:, :, :], A["l3_down"]), (ubias[:, :], A["l3_ubias"]), (obias[:, :], A["l3_obias"])]

                @block.sync
                def _(sp):
                    for dst, src in loads:
                        sp.dma_start(dst, src).then_inc(s["loaded"], 16)
                    sp.dma_start(uw[:, :, :, :, :], A["l3_uw"].partition_broadcast(P)).then_inc(s["loaded"], 16)
                    sp.dma_start(dw[:, :, :, :, :], A["l3_dw"].partition_broadcast(P)).then_inc(s["loaded"], 16)

                @block.vector
                def _(dve):
                    dve.wait_ge(s["loaded"], 16 * (len(loads) + 2))
                    dve.sem_inc(s["bf"], 1)
                    end = butterfly_stages(dve, s, up, buf, work, uw, 2, False, 1, 0)
                    n = 1 + 9 * 2
                    dve.wait_ge(s["bf"], n)
                    dve.tensor_copy(w_up[:, :], end[:, 0, :]).then_inc(s["bf"], 1)
                    for f in range(FT):
                        dve.tensor_tensor(work[:, 0, f * P:(f + 1) * P], end[:, 1, f * P:(f + 1) * P], mem["ident"][:, :], ALU.mult).then_inc(s["bf"], 1)
                    dve.wait_ge(s["bf"], n + 5)
                    dve.tensor_reduce(hbias[:, :], work[:, 0, :].rearrange("p (f c) -> p f c", f=FT), AX.X, ALU.add).then_inc(s["hb_done"], 1)
                    dve.wait_ge(s["hb_done"], 1)
                    dve.tensor_tensor(hbias[:, :], hbias[:, :], ubias[:, :], ALU.add)
                    butterfly_stages(dve, s, down, buf, work, dw, 1, True, n + 5, 36)
                    dve.tensor_scalar(obias[:, 0:1], obias[:, 0:1], obias[:, 1:2], None, ALU.add).then_inc(s["ob_done"], 1)
                    dve.wait_ge(s["t_mm"], 1)
                    dve.tensor_copy(w_down[:, :, :], ps[0][:, :].rearrange("p (f d) -> p f d", f=FT))

                @block.tensor
                def _(pe):
                    pe.wait_ge(s["bf"], 1 + 9 * 2 + 5 + 9)
                    for f in range(FT):
                        last = pe.transpose(ps[0][:, f * P:(f + 1) * P], buf[:, 0, f * P:(f + 1) * P], mem["ident"][:, :])
                    last.then_inc(s["t_mm"], 1)

            nc.scalar.preload_act_table_set("gelu_and_others")
            with stage(nc, "up_mm", "gelu_done", "down_mm", "out_done") as (block, s):
                @block.tensor
                def _(pe):
                    def ups(k):
                        for f in range(FT):
                            if k:
                                pe.wait_ge(s["gelu_done"], (k - 1) * FT + f + 1)
                            pe.matmul(ps[f][:, :], w_up[:, f * P:(f + 1) * P], xn[:, CHUNKS[k]], start=True, stop=True).then_inc(s["up_mm"], 1)

                    ups(0)
                    for k in range(NB):
                        if k + 1 < NB:
                            ups(k + 1)
                        if k >= 2:
                            pe.wait_ge(s["out_done"], k - 1)
                        for f in range(FT):
                            pe.wait_ge(s["gelu_done"], k * FT + f + 1)
                            last = pe.matmul(ps[4 + k % 2][:, :], w_down[:, f, :], hid[:, k % 2, f, :], start=(f == 0), stop=(f == FT - 1))
                        last.then_inc(s["down_mm"], 1)

                @block.scalar
                def _(act):
                    for k in range(NB):
                        for f in range(FT):
                            act.wait_ge(s["up_mm"], k * FT + f + 1)
                            if k >= 2:
                                act.wait_ge(s["down_mm"], k - 1)
                            act.activation(hid[:, k % 2, f, :], ps[f][:, :], ACT.Gelu, bias=hbias[:, f:f + 1]).then_inc(s["gelu_done"], 1)

                @block.vector
                def _(dve):
                    for k in range(NB):
                        dve.wait_ge(s["down_mm"], k + 1)
                        if k + 1 < NB:
                            dve.wait_ge(s["up_mm"], (k + 2) * FT)
                        dve.tensor_scalar(xn[:, CHUNKS[k]], ps[4 + k % 2][:, :], obias[:, 0:1], None, ALU.add).then_inc(s["out_done"], 1)
            nc.scalar.preload_act_table_set("natural_log_exp_and_others")
            residual_stage(nc, mem, x, sat, xn, e)


def layout_l3(i, A):
    for n, k in (("l3_wq", "q_w"), ("l3_wk", "k_w"), ("l3_wv", "v_w"), ("l3_wo", "out_w")):
        A[n] = i["L3_attn_" + k].T
    A["l3_bvec"] = np.stack([i["L3_attn_" + k] for k in ("q_b", "k_b", "v_b", "out_b")], axis=1)
    own = (np.arange(P)[:, None] // HD == np.arange(NH)).astype(np.float32)
    A["head_q3"] = (own * np.float32(HD ** -0.5)).astype(np.float32)
    gw = np.zeros((NH, HD, 8, NH), np.float32)
    for h in range(NH):
        gw[h, :, :, h] = i["L3_attn_gru_w"].T
    A["l3_gw"] = gw.reshape(P, 8, NH)
    A["l3_gb"] = np.broadcast_to(i["L3_attn_gru_b"], (P, 8))
    A["l3_gconst"] = np.broadcast_to(i["L3_attn_gru_const"].reshape(NH), (P, NH))
    A["flip"] = np.eye(P, dtype=np.float32)[::-1]
    A["rel_embed"] = i["L3_attn_rel_embed"]
    rel = np.arange(-511, 512)
    n = np.abs(rel)
    large = np.log(np.maximum(n, 1).astype(np.float32) / np.float32(10)) / np.float32(np.log(100 / 10)) * np.float32(10)
    large = np.minimum((10 + large).astype(np.int32), 19)
    bucket = (rel > 0) * 20 + np.where(n < 10, n, large)
    oh = np.zeros((40, 1024), np.float32)
    oh[bucket, np.arange(1023)] = 1.0
    A["bucket_onehot"] = oh
    A["l3_up"] = np.stack([i["L3_ffn_W_exp"], np.broadcast_to(i["L3_ffn_b_exp"], (P, 512))], axis=1)
    A["l3_down"] = i["L3_ffn_W_con"].T.reshape(P, 1, 512)
    A["l3_uw"] = i["L3_ffn_up_weights"].transpose(0, 2, 3, 1)
    A["l3_dw"] = i["L3_ffn_down_weights"].transpose(0, 2, 3, 1)
    A["l3_ubias"] = columns(i["L3_ffn_up_bias"], 4)
    A["l3_obias"] = np.stack([i["L3_ffn_b_con"], i["L3_ffn_down_bias"]], axis=1)


def layout_rest(i, A):
    layout_l1(i, A)
    layout_l2(i, A)
    layout_l3(i, A)


def shared_memory(nc, ctx, A):
    def sb(name, shape, dt=F32):
        return ctx.enter_context(nc.sbuf_tensor(name, shape, dt))

    mem = dict(
        ps=[ctx.enter_context(nc.psum_tensor(f"bank{i}", [P, 512], F32)) for i in range(8)],
        ident=sb("ident", [P, P]), ones=sb("ones", [P, P]), ones_mean=sb("ones_mean", [P, P]), eps=sb("eps", [P, 1]),
        ln_xc=sb("ln_xc", [P, 2, CH]), ln_sq=sb("ln_sq", [P, 2, CH]), ln_rs=sb("ln_rs", [P, 2, CH]))
    with stage(nc, "loaded") as (block, s):
        @block.sync
        def _(sp):
            sp.dma_start(mem["ident"][:, :], A["ident"]).then_inc(s["loaded"], 16)
            sp.wait_ge(s["loaded"], 16)

        @block.gpsimd
        def _(pool):
            pool.memset(mem["ones"][:, :], 1.0)
            pool.memset(mem["ones_mean"][:, :], 1.0 / P)
            pool.memset(mem["eps"][:, :], LN_EPS)
    return mem


def program(nc, A, out, layers=4):
    with ExitStack() as ctx:
        x1 = ctx.enter_context(nc.sbuf_tensor("x1", [P, TOK], F32))
        mem = shared_memory(nc, ctx, A)
        nc.scalar.preload_act_table_set("natural_log_exp_and_others")
        layer0(nc, mem, A, x1)
        if layers >= 2:
            layer1(nc, mem, A, x1)
        if layers >= 3:
            layer2(nc, mem, A, x1)
        if layers >= 4:
            layer3(nc, mem, A, x1)
        with stage(nc, "stored") as (block, s):
            @block.sync
            def _(sp):
                sp.dma_start(out, x1[:, :]).then_inc(s["stored"], 16)
                sp.wait_ge(s["stored"], 16)


def columns(v, n):
    return v.reshape(n, P).T


def layout(i):
    c = np.ascontiguousarray
    A = {}
    A["ident"] = np.eye(P, dtype=np.float32)
    A["x0"] = i["L0_attn_u"].transpose(2, 1, 0).reshape(P, TOK)
    order = [3, 2, 0, 1]
    w = np.concatenate([i["L0_attn_W_in"][:256], i["L0_attn_W_in"][256:768].reshape(4, P, P)[order].reshape(512, P),
                        np.repeat(i["L0_attn_W_in"][768:], 64, axis=0)], axis=0)
    A["w_in"] = w.reshape(8, P, P).transpose(2, 0, 1)
    w = np.concatenate([i["L0_attn_W_rxbc"].reshape(4, P, 256)[order].reshape(512, 256), np.repeat(i["L0_attn_W_rdt"], 64, axis=0)], axis=0)
    A["w_r"] = w.reshape(6 * P, 2, P).transpose(2, 1, 0)
    A["w_out"] = i["L0_attn_W_out"].reshape(P, 2, P).transpose(2, 1, 0)
    A["conv_w"] = i["L0_attn_conv_w"].reshape(4, P, 4)[order].transpose(1, 0, 2)
    A["conv_b"] = i["L0_attn_conv_b"].reshape(4, P)[order].T
    A["vec"] = np.concatenate([columns(np.repeat(i["L0_attn_" + n], 64), 2) for n in ("dt_bias", "A_log", "D_param")]
                              + [columns(i["L0_attn_norm_w"], 2)], axis=1)
    A["cent"] = i["L0_ffn_centroids"].T
    A["ln_g"] = i["L0_ffn_ln_g"].T
    A["ln_b"] = i["L0_ffn_ln_b"].T
    A["b1"] = i["L0_ffn_b1"].reshape(8, 4, P).transpose(2, 0, 1)
    A["b2"] = i["L0_ffn_b2"].T
    A["w1"] = i["L0_ffn_w1"].transpose(2, 0, 1)
    A["w2"] = i["L0_ffn_w2"].reshape(8, P, 4, P).transpose(3, 0, 2, 1)
    A["rank"] = np.broadcast_to((8.0 - np.arange(8)).astype(np.float32), (P, 4, 8))
    A["bmask"] = (np.arange(P)[:, None] % 8 == np.arange(8)).astype(np.float32)
    A["hsel"] = (np.arange(P)[:, None] == 64 * np.arange(2)).astype(np.float32)
    layout_rest(i, A)
    return {n: c(a) for n, a in A.items()}


def kernel(**inputs):
    import concourse.bacc as bacc
    from concourse.bass_utils import run_bass_kernel_spmd

    arrays = layout({n: np.asarray(a) for n, a in inputs.items()})
    nc = bacc.Bacc("TRN2", target_bir_lowering=False, num_devices=1)
    A = {n: nc.dram_tensor(f"in_{n}", a.shape, mybir.dt.from_np(a.dtype), kind="ExternalInput").ap() for n, a in arrays.items()}
    out = nc.dram_tensor("out_x", (P, TOK), F32, kind="ExternalOutput").ap()
    program(nc, A, out)
    r = run_bass_kernel_spmd(nc, [{f"in_{n}": a for n, a in arrays.items()}], core_ids=[0])
    return r.results[0]["out_x"].reshape(P, NB, NT).transpose(1, 2, 0)
```
